# Optimizing a Trainium2 kernel written in Bass

```python
import numpy as np
import jax
import jax.numpy as jnp

def _softmax(x, axis=-1):
    return jax.nn.softmax(x, axis=axis)

def _gelu(x):
    return jax.nn.gelu(x, approximate=True)

def _silu(x):
    return jax.nn.silu(x)

def _sigmoid(x):
    return jax.nn.sigmoid(x)

def _layernorm(x, axis=-1, eps=1e-05):
    m = jnp.mean(x, axis=axis, keepdims=True)
    v = jnp.var(x, axis=axis, keepdims=True)
    return (x - m) / jnp.sqrt(v + eps)

def _scatter_add(tgt, idx, src, axis=0):
    return tgt.at[idx].add(src)

def _segment_sum(src, seg, n):
    return jax.ops.segment_sum(src, seg, n)
kernel_name = 'mk_pixart_resid_d4_seqx_r4_ea0fcf'

def setup_inputs(seed: int=0):
    np.random.seed(seed)
    _w = jnp.asarray

    def _rec_inputs():
        import jax
        import jax.numpy as jnp
        _rk = jax.random.key(seed)
        x = -0.0002928 + 1 * jax.random.normal(jax.random.fold_in(_rk, 1), (4, 512, 256), jnp.float32)
        _lenS = 512 - jax.random.randint(jax.random.fold_in(_rk, 7), (4,), 0, max(1, 512 // 4) + 1, jnp.int32)
        _lenS2 = 64 - jax.random.randint(jax.random.fold_in(_rk, 8), (4,), 0, max(1, 64 // 4) + 1, jnp.int32)
        _ctx_1024P = jax.random.normal(jax.random.fold_in(_rk, 11), (4, 16, 256), jnp.float32)
        _ctx_1024c = jax.random.dirichlet(jax.random.fold_in(_rk, 511), 0.3 * jnp.ones((16,), jnp.float32), (4, 64))
        _ctx_1024t = jnp.einsum('bsk,bkd->bsd', _ctx_1024c, _ctx_1024P)
        _ctx_1024t = _ctx_1024t * jax.lax.rsqrt(jnp.mean(jnp.square(_ctx_1024t)) + 1e-12) * 0.953939
        ctx_1024 = -1.39393e-06 + 0.999914 * (_ctx_1024t + 0.3 * jax.random.normal(jax.random.fold_in(_rk, 611), (4, 64, 256), jnp.float32))
        condB_tau = jax.random.uniform(jax.random.fold_in(_rk, 12), (4,), jnp.float32, 0.0, 1.23395)
        fside_BxS2_0 = -0.00205293 + 0.99739 * jax.random.normal(jax.random.fold_in(_rk, 13), (4, 64), jnp.float32)
        condB_pt = jax.random.uniform(jax.random.fold_in(_rk, 15), (4,), jnp.float32, 0.0, 226.919)
        return (x, ctx_1024, condB_tau, fside_BxS2_0, condB_pt, _lenS2)
    x, ctx_1024, condB_tau, fside_BxS2_0, condB_pt, _lenS2 = _rec_inputs()

    def _L0_xcond_setup():
        import jax, jax.numpy as jnp
        import numpy as np
        B, S, D, H = (2, 512, 256, 16)
        DK = D // H

        def _split_heads(x):
            b, s, _ = x.shape
            return x.reshape(b, s, H, DK).transpose(0, 2, 1, 3)
        key = jax.random.key(seed)
        ks = jax.random.split(key, 14)
        inp = {'query': jax.random.normal(ks[0], (B, S, D), jnp.float32), 'key': jax.random.normal(ks[1], (B, S, D), jnp.float32), 'value': jax.random.normal(ks[2], (B, S, D), jnp.float32), 'tau': jax.random.uniform(ks[3], (B, 1), jnp.float32, 0.5, 1.5), 'delta': jax.random.normal(ks[4], (B, S), jnp.float32)}
        sc = 1.0 / np.sqrt(D)
        for i, name in enumerate(['q', 'k', 'v', 'o']):
            inp[f'W{name}'] = jax.random.normal(ks[5 + 2 * i], (D, D), jnp.float32) * sc
            inp[f'b{name}'] = jax.random.normal(ks[6 + 2 * i], (D,), jnp.float32) * 0.01
        return inp
    _L0_xcond_all = _L0_xcond_setup()
    _L0_xcond_in = {k: v for k, v in _L0_xcond_all.items() if k in ('Wq', 'bq', 'Wk', 'bk', 'Wv', 'bv', 'Wo', 'bo')}
    del _L0_xcond_all

    def _L0_ffn_setup():
        import jax, jax.numpy as jnp
        import numpy as np
        TOP_K = 2
        key = jax.random.key(seed)
        k1, k2, k3, k4 = jax.random.split(key, 4)
        B, N, D, E, F = (4, 512, 256, 8, 1024)
        x = jax.random.normal(k1, (B, N, D), dtype=jnp.float32)
        gate_w = jax.random.normal(k2, (D, E), dtype=jnp.float32) * D ** (-0.5)
        w1 = jax.random.normal(k3, (E, D, F), dtype=jnp.float32) * D ** (-0.5)
        w2 = jax.random.normal(k4, (E, F, D), dtype=jnp.float32) * F ** (-0.5)
        return {'x': x, 'gate_w': gate_w, 'w1': w1, 'w2': w2}
    _L0_ffn_all = _L0_ffn_setup()
    _L0_ffn_in = {k: v for k, v in _L0_ffn_all.items() if k in ('gate_w', 'w1', 'w2')}
    del _L0_ffn_all

    def _L1_xcond_setup():
        import jax, jax.numpy as jnp
        import numpy as np
        D_MODEL = 256
        N_HEADS = 16
        key = jax.random.key(seed)
        ks = jax.random.split(key, 16)
        B, L, S, D = (4, 512, 512, D_MODEL)
        inp = {'q': jax.random.normal(ks[0], (B, L, D), jnp.float32), 'k': jax.random.normal(ks[1], (B, S, D), jnp.float32), 'v': jax.random.normal(ks[2], (B, S, D), jnp.float32), 'tau': jax.random.uniform(ks[3], (B, 1), jnp.float32, 0.5, 1.5), 'delta': jax.random.normal(ks[4], (B, S), jnp.float32)}
        s = 1.0 / np.sqrt(D)
        inp['Wq'] = jax.random.normal(ks[5], (D, D), jnp.float32) * s
        inp['bq'] = jnp.zeros((D,), jnp.float32)
        inp['Wk'] = jax.random.normal(ks[6], (D, D), jnp.float32) * s
        inp['bk'] = jnp.zeros((D,), jnp.float32)
        inp['Wv'] = jax.random.normal(ks[7], (D, D), jnp.float32) * s
        inp['bv'] = jnp.zeros((D,), jnp.float32)
        inp['Wo'] = jax.random.normal(ks[8], (D, D), jnp.float32) * s
        inp['bo'] = jnp.zeros((D,), jnp.float32)
        return inp
    _L1_xcond_all = _L1_xcond_setup()
    _L1_xcond_in = {k: v for k, v in _L1_xcond_all.items() if k in ('Wq', 'bq', 'Wk', 'bk', 'Wv', 'bv', 'Wo', 'bo')}
    del _L1_xcond_all

    def _L1_ffn_setup():
        import jax, jax.numpy as jnp
        import numpy as np
        BEST_K = 2

        def _expert(xf, w1, w3, w2):
            return jax.nn.silu(xf @ w1) * (xf @ w3) @ w2
        key = jax.random.key(seed)
        ks = jax.random.split(key, 9)
        E, S_sh, D, H = (8, 2, 256, 128)
        B, S = (2, 512)
        w = lambda k, shape: jax.random.normal(k, shape, dtype=jnp.float32) * 0.02
        return {'x': jax.random.normal(ks[0], (B, S, D), dtype=jnp.float32), 'router_w': w(ks[1], (D, E)), 'router_b': jnp.zeros((E,), dtype=jnp.float32), 'routed_w1': w(ks[2], (E, D, H)), 'routed_w3': w(ks[3], (E, D, H)), 'routed_w2': w(ks[4], (E, H, D)), 'shared_w1': w(ks[5], (S_sh, D, H)), 'shared_w3': w(ks[6], (S_sh, D, H)), 'shared_w2': w(ks[7], (S_sh, H, D))}
    _L1_ffn_all = _L1_ffn_setup()
    _L1_ffn_in = {k: v for k, v in _L1_ffn_all.items() if k in ('router_w', 'router_b', 'routed_w1', 'routed_w3', 'routed_w2', 'shared_w1', 'shared_w3', 'shared_w2')}
    del _L1_ffn_all

    def _L2_xcond_setup():
        import jax, jax.numpy as jnp
        import numpy as np
        N, L, H, Q = (64, 258, 256, 64)
        WINDOW = 16.0
        DEV_POW = 128.0
        key = jax.random.key(seed)
        k1, k2, k3, k4, k5, k6 = jax.random.split(key, 6)
        encoder_outputs = jax.random.normal(k1, (N, L, H), dtype=jnp.float32)
        decoder_h_t = jax.random.normal(k2, (N, Q, H), dtype=jnp.float32)
        src_len = jax.random.randint(k3, (N,), 32, L + 1).astype(jnp.int32)
        p_t = jax.random.uniform(k4, (N,), dtype=jnp.float32) * (src_len.astype(jnp.float32) - 1.0)
        W_a = jax.random.normal(k5, (H, H), dtype=jnp.float32) * (1.0 / np.sqrt(H))
        W_c = jax.random.normal(k6, (H, 2 * H), dtype=jnp.float32) * (1.0 / np.sqrt(2 * H))
        return {'encoder_outputs': encoder_outputs, 'decoder_h_t': decoder_h_t, 'src_len': src_len, 'p_t': p_t, 'W_a': W_a, 'W_c': W_c}
    _L2_xcond_all = _L2_xcond_setup()
    _L2_xcond_in = {k: v for k, v in _L2_xcond_all.items() if k in ('W_a', 'W_c')}
    del _L2_xcond_all

    def _L2_ffn_setup():
        import math
        import jax, jax.numpy as jnp
        import numpy as np
        B, L, D, FF, E, K = (4, 512, 256, 1024, 8, 2)
        CAPACITY_FACTOR = 1.25
        T = B * L
        CAP = math.ceil(CAPACITY_FACTOR * T * K / E)
        key = jax.random.key(seed)
        ks = jax.random.split(key, 7)
        return {'h': jax.random.normal(ks[0], (B, L, D), dtype=jnp.float32), 'gate_w': 0.02 * jax.random.normal(ks[1], (E, D), dtype=jnp.float32), 'gate_b': jnp.zeros((E,), dtype=jnp.float32), 'W1': 0.02 * jax.random.normal(ks[2], (E, D, FF), dtype=jnp.float32), 'b1': jnp.zeros((E, FF), dtype=jnp.float32), 'W2': 0.02 * jax.random.normal(ks[3], (E, FF, D), dtype=jnp.float32), 'b2': jnp.zeros((E, D), dtype=jnp.float32)}
    _L2_ffn_all = _L2_ffn_setup()
    _L2_ffn_in = {k: v for k, v in _L2_ffn_all.items() if k in ('gate_w', 'gate_b', 'W1', 'b1', 'W2', 'b2')}
    del _L2_ffn_all

    def _L3_xcond_setup():
        import jax, jax.numpy as jnp
        import numpy as np
        B, S, D, H = (2, 512, 256, 16)
        DK = D // H

        def _split_heads(x):
            b, s, _ = x.shape
            return x.reshape(b, s, H, DK).transpose(0, 2, 1, 3)
        key = jax.random.key(seed)
        ks = jax.random.split(key, 14)
        inp = {'query': jax.random.normal(ks[0], (B, S, D), jnp.float32), 'key': jax.random.normal(ks[1], (B, S, D), jnp.float32), 'value': jax.random.normal(ks[2], (B, S, D), jnp.float32), 'tau': jax.random.uniform(ks[3], (B, 1), jnp.float32, 0.5, 1.5), 'delta': jax.random.normal(ks[4], (B, S), jnp.float32)}
        sc = 1.0 / np.sqrt(D)
        for i, name in enumerate(['q', 'k', 'v', 'o']):
            inp[f'W{name}'] = jax.random.normal(ks[5 + 2 * i], (D, D), jnp.float32) * sc
            inp[f'b{name}'] = jax.random.normal(ks[6 + 2 * i], (D,), jnp.float32) * 0.01
        return inp
    _L3_xcond_all = _L3_xcond_setup()
    _L3_xcond_in = {k: v for k, v in _L3_xcond_all.items() if k in ('Wq', 'bq', 'Wk', 'bk', 'Wv', 'bv', 'Wo', 'bo')}
    del _L3_xcond_all

    def _L3_ffn_setup():
        import jax, jax.numpy as jnp
        import numpy as np
        NUM_EXPERTS = 8
        TOP_K = 2
        CAPACITY_FACTOR = 1.25
        key = jax.random.key(seed)
        k1, k2, k3, k4, k5 = jax.random.split(key, 5)
        B, S, H, I, E = (4, 512, 256, 1024, NUM_EXPERTS)
        return {'hidden_states': jax.random.normal(k1, (B, S, H), dtype=jnp.float32), 'router_gate': jax.random.normal(k2, (H, E), dtype=jnp.float32) * 0.02, 'gate_w': jax.random.normal(k3, (E, H, I), dtype=jnp.float32) * 0.02, 'up_w': jax.random.normal(k4, (E, H, I), dtype=jnp.float32) * 0.02, 'down_w': jax.random.normal(k5, (E, I, H), dtype=jnp.float32) * 0.02}
    _L3_ffn_all = _L3_ffn_setup()
    _L3_ffn_in = {k: v for k, v in _L3_ffn_all.items() if k in ('router_gate', 'gate_w', 'up_w', 'down_w')}
    del _L3_ffn_all
    return {'x': x, 'ctx_1024': ctx_1024, 'condB_tau': condB_tau, 'fside_BxS2_0': fside_BxS2_0, 'condB_pt': condB_pt, '_lenS2': _lenS2, 'L0_xcond_Wq': _L0_xcond_in['Wq'], 'L0_xcond_bq': _L0_xcond_in['bq'], 'L0_xcond_Wk': _L0_xcond_in['Wk'], 'L0_xcond_bk': _L0_xcond_in['bk'], 'L0_xcond_Wv': _L0_xcond_in['Wv'], 'L0_xcond_bv': _L0_xcond_in['bv'], 'L0_xcond_Wo': _L0_xcond_in['Wo'], 'L0_xcond_bo': _L0_xcond_in['bo'], 'L0_ffn_gate_w': _L0_ffn_in['gate_w'], 'L0_ffn_w1': _L0_ffn_in['w1'], 'L0_ffn_w2': _L0_ffn_in['w2'], 'L1_xcond_Wq': _L1_xcond_in['Wq'], 'L1_xcond_bq': _L1_xcond_in['bq'], 'L1_xcond_Wk': _L1_xcond_in['Wk'], 'L1_xcond_bk': _L1_xcond_in['bk'], 'L1_xcond_Wv': _L1_xcond_in['Wv'], 'L1_xcond_bv': _L1_xcond_in['bv'], 'L1_xcond_Wo': _L1_xcond_in['Wo'], 'L1_xcond_bo': _L1_xcond_in['bo'], 'L1_ffn_router_w': _L1_ffn_in['router_w'], 'L1_ffn_router_b': _L1_ffn_in['router_b'], 'L1_ffn_routed_w1': _L1_ffn_in['routed_w1'], 'L1_ffn_routed_w3': _L1_ffn_in['routed_w3'], 'L1_ffn_routed_w2': _L1_ffn_in['routed_w2'], 'L1_ffn_shared_w1': _L1_ffn_in['shared_w1'], 'L1_ffn_shared_w3': _L1_ffn_in['shared_w3'], 'L1_ffn_shared_w2': _L1_ffn_in['shared_w2'], 'L2_xcond_W_a': _L2_xcond_in['W_a'], 'L2_xcond_W_c': _L2_xcond_in['W_c'], 'L2_ffn_gate_w': _L2_ffn_in['gate_w'], 'L2_ffn_gate_b': _L2_ffn_in['gate_b'], 'L2_ffn_W1': _L2_ffn_in['W1'], 'L2_ffn_b1': _L2_ffn_in['b1'], 'L2_ffn_W2': _L2_ffn_in['W2'], 'L2_ffn_b2': _L2_ffn_in['b2'], 'L3_xcond_Wq': _L3_xcond_in['Wq'], 'L3_xcond_bq': _L3_xcond_in['bq'], 'L3_xcond_Wk': _L3_xcond_in['Wk'], 'L3_xcond_bk': _L3_xcond_in['bk'], 'L3_xcond_Wv': _L3_xcond_in['Wv'], 'L3_xcond_bv': _L3_xcond_in['bv'], 'L3_xcond_Wo': _L3_xcond_in['Wo'], 'L3_xcond_bo': _L3_xcond_in['bo'], 'L3_ffn_router_gate': _L3_ffn_in['router_gate'], 'L3_ffn_gate_w': _L3_ffn_in['gate_w'], 'L3_ffn_up_w': _L3_ffn_in['up_w'], 'L3_ffn_down_w': _L3_ffn_in['down_w']}

def reference(x, ctx_1024, condB_tau, fside_BxS2_0, condB_pt, _lenS2, L0_xcond_Wq, L0_xcond_bq, L0_xcond_Wk, L0_xcond_bk, L0_xcond_Wv, L0_xcond_bv, L0_xcond_Wo, L0_xcond_bo, L0_ffn_gate_w, L0_ffn_w1, L0_ffn_w2, L1_xcond_Wq, L1_xcond_bq, L1_xcond_Wk, L1_xcond_bk, L1_xcond_Wv, L1_xcond_bv, L1_xcond_Wo, L1_xcond_bo, L1_ffn_router_w, L1_ffn_router_b, L1_ffn_routed_w1, L1_ffn_routed_w3, L1_ffn_routed_w2, L1_ffn_shared_w1, L1_ffn_shared_w3, L1_ffn_shared_w2, L2_xcond_W_a, L2_xcond_W_c, L2_ffn_gate_w, L2_ffn_gate_b, L2_ffn_W1, L2_ffn_b1, L2_ffn_W2, L2_ffn_b2, L3_xcond_Wq, L3_xcond_bq, L3_xcond_Wk, L3_xcond_bk, L3_xcond_Wv, L3_xcond_bv, L3_xcond_Wo, L3_xcond_bo, L3_ffn_router_gate, L3_ffn_gate_w, L3_ffn_up_w, L3_ffn_down_w):
    import jax
    import jax.numpy as jnp

    def _L0_xcond_ref(query, key, value, tau, delta, Wq, bq, Wk, bk, Wv, bv, Wo, bo):
        import jax, jax.numpy as jnp
        import numpy as np
        B, S, D, H = (2, 512, 256, 16)
        DK = D // H

        def _split_heads(x):
            b, s, _ = x.shape
            return x.reshape(b, s, H, DK).transpose(0, 2, 1, 3)
        q = _split_heads(query @ Wq.T + bq)
        k = _split_heads(key @ Wk.T + bk)
        v = _split_heads(value @ Wv.T + bv)
        scores = jnp.einsum('bhqd,bhkd->bhqk', q, k)
        scores = scores * tau[:, :, None, None] + delta[:, None, None, :]
        scores = scores / jnp.sqrt(jnp.asarray(DK, scores.dtype))
        p_attn = jax.nn.softmax(scores, axis=-1)
        x = jnp.einsum('bhqk,bhkd->bhqd', p_attn, v)
        x = x.transpose(0, 2, 1, 3).reshape(query.shape[0], -1, H * DK)
        return x @ Wo.T + bo

    def _L0_ffn_ref(x, gate_w, w1, w2):
        import jax, jax.numpy as jnp
        import numpy as np
        TOP_K = 2
        E = gate_w.shape[-1]
        gate_logits = jnp.einsum('bnd,de->bne', x, gate_w)
        gate_probs = jax.nn.softmax(gate_logits, axis=-1)
        top_k_probs, top_k_idx = jax.lax.top_k(gate_probs, TOP_K)
        top_k_weights = top_k_probs / jnp.sum(top_k_probs, axis=-1, keepdims=True)
        comb = jnp.sum(jax.nn.one_hot(top_k_idx, E, dtype=x.dtype) * top_k_weights[..., None], axis=2)
        h = jax.nn.gelu(jnp.einsum('bnd,edf->benf', x, w1))
        expert_out = jnp.einsum('benf,efd->bend', h, w2)
        output = jnp.einsum('bne,bend->bnd', comb, expert_out)
        return output

    def _L1_xcond_ref(q, k, v, tau, delta, Wq, bq, Wk, bk, Wv, bv, Wo, bo):
        import jax, jax.numpy as jnp
        import numpy as np
        D_MODEL = 256
        N_HEADS = 16
        B, L, D = q.shape
        S = k.shape[1]
        H = N_HEADS
        E = D // H
        qh = (q @ Wq.T + bq).reshape(B, L, H, E)
        kh = (k @ Wk.T + bk).reshape(B, S, H, E)
        vh = (v @ Wv.T + bv).reshape(B, S, H, E)
        scale = 1.0 / np.sqrt(E).astype(np.float32)
        scores = jnp.einsum('blhe,bshe->bhls', qh, kh)
        scores = scores * tau[:, None, None, :] + delta[:, None, None, :]
        a = jax.nn.softmax(scale * scores, axis=-1)
        out = jnp.einsum('bhls,bshd->blhd', a, vh).reshape(B, L, D)
        return out @ Wo.T + bo

    def _L1_ffn_ref(x, router_w, router_b, routed_w1, routed_w3, routed_w2, shared_w1, shared_w3, shared_w2):
        import jax, jax.numpy as jnp
        import numpy as np
        BEST_K = 2

        def _expert(xf, w1, w3, w2):
            return jax.nn.silu(xf @ w1) * (xf @ w3) @ w2
        B, S, D = x.shape
        T = B * S
        xf = x.reshape(T, D)
        logits = xf @ router_w + router_b
        topk_vals, topk_idx = jax.lax.top_k(logits, BEST_K)
        sparse = jnp.full_like(logits, -jnp.inf)
        sparse = sparse.at[jnp.arange(T)[:, None], topk_idx].set(topk_vals)
        gates = jax.nn.softmax(sparse, axis=-1)
        routed = jax.vmap(_expert, in_axes=(None, 0, 0, 0))(xf, routed_w1, routed_w3, routed_w2)
        routed_out = jnp.einsum('etd,te->td', routed, gates)
        shared_out = jax.vmap(_expert, in_axes=(None, 0, 0, 0))(xf, shared_w1, shared_w3, shared_w2).sum(axis=0)
        return (routed_out + shared_out).reshape(B, S, D)

    def _L2_xcond_ref(encoder_outputs, decoder_h_t, src_len, p_t, W_a, W_c):
        import jax, jax.numpy as jnp
        import numpy as np
        N, L, H, Q = (64, 258, 256, 64)
        WINDOW = 16.0
        DEV_POW = 128.0
        n, l, h = encoder_outputs.shape
        idx = jnp.arange(l, dtype=jnp.float32)
        src_end = src_len.astype(jnp.float32)
        attn_start = jnp.maximum(p_t - WINDOW, 0.0)
        attn_end = jnp.minimum(p_t + WINDOW, src_end)
        mask = (idx[None, :] < attn_start[:, None]) | (idx[None, :] > attn_end[:, None])
        score = jnp.einsum('nqh,hk,nlk->nql', decoder_h_t, W_a, encoder_outputs)
        score = jnp.where(mask[:, None, :], -1000000000.0, score)
        align = jax.nn.softmax(score, axis=2)
        gauss = jnp.exp(-(idx[None, :] - p_t[:, None]) ** 2 / DEV_POW)
        align = align * gauss[:, None, :]
        context = jnp.einsum('nql,nlh->nqh', align, encoder_outputs)
        cat = jnp.concatenate([context, decoder_h_t], axis=2)
        return jnp.tanh(cat @ W_c.T)

    def _L2_ffn_ref(h, gate_w, gate_b, W1, b1, W2, b2):
        import math
        import jax, jax.numpy as jnp
        import numpy as np
        B, L, D, FF, E, K = (4, 512, 256, 1024, 8, 2)
        CAPACITY_FACTOR = 1.25
        T = B * L
        CAP = math.ceil(CAPACITY_FACTOR * T * K / E)
        Bb, Ll, Dm = h.shape
        Tt = Bb * Ll
        x = h.reshape(Tt, Dm)
        logits = x @ gate_w.T + gate_b
        probs = jax.nn.softmax(logits, axis=-1)
        topk_prob, topk_idx = jax.lax.top_k(probs, K)
        y = jnp.zeros((Tt, Dm), dtype=h.dtype)
        n_slots = E * CAP
        for c in range(K):
            idx = topk_idx[:, c]
            prb = topk_prob[:, c]
            oh = jax.nn.one_hot(idx, E, dtype=jnp.int32)
            pos = jnp.take_along_axis(jnp.cumsum(oh, axis=0) - 1, idx[:, None], axis=1)[:, 0]
            keep = pos < CAP
            buf_idx = jnp.where(keep, idx * CAP + pos, n_slots)
            xbuf = jnp.zeros((n_slots, Dm), x.dtype).at[buf_idx].set(x, mode='drop')
            xb = xbuf.reshape(E, CAP, Dm)
            hmid = jax.nn.relu(jnp.einsum('ecd,edf->ecf', xb, W1) + b1[:, None, :])
            yb = jnp.einsum('ecf,efd->ecd', hmid, W2) + b2[:, None, :]
            ytok = yb.reshape(n_slots, Dm)[jnp.clip(buf_idx, 0, n_slots - 1)]
            y = y + ytok * (prb * keep.astype(prb.dtype))[:, None]
        return y.reshape(Bb, Ll, Dm)

    def _L3_xcond_ref(query, key, value, tau, delta, Wq, bq, Wk, bk, Wv, bv, Wo, bo):
        import jax, jax.numpy as jnp
        import numpy as np
        B, S, D, H = (2, 512, 256, 16)
        DK = D // H

        def _split_heads(x):
            b, s, _ = x.shape
            return x.reshape(b, s, H, DK).transpose(0, 2, 1, 3)
        q = _split_heads(query @ Wq.T + bq)
        k = _split_heads(key @ Wk.T + bk)
        v = _split_heads(value @ Wv.T + bv)
        scores = jnp.einsum('bhqd,bhkd->bhqk', q, k)
        scores = scores * tau[:, :, None, None] + delta[:, None, None, :]
        scores = scores / jnp.sqrt(jnp.asarray(DK, scores.dtype))
        p_attn = jax.nn.softmax(scores, axis=-1)
        x = jnp.einsum('bhqk,bhkd->bhqd', p_attn, v)
        x = x.transpose(0, 2, 1, 3).reshape(query.shape[0], -1, H * DK)
        return x @ Wo.T + bo

    def _L3_ffn_ref(hidden_states, router_gate, gate_w, up_w, down_w):
        import jax, jax.numpy as jnp
        import numpy as np
        NUM_EXPERTS = 8
        TOP_K = 2
        CAPACITY_FACTOR = 1.25
        B, S, H = hidden_states.shape
        E = router_gate.shape[1]
        K = TOP_K
        x = hidden_states.reshape(-1, H)
        T = x.shape[0]
        cap = int(CAPACITY_FACTOR * ((T * K + E - 1) // E))
        probs = jax.nn.softmax(x @ router_gate, axis=-1)
        topw, topi = jax.lax.top_k(probs, K)
        topw = topw / (topw.sum(-1, keepdims=True) + 1e-09)
        gates = jnp.zeros((T, E), x.dtype).at[jnp.arange(T)[:, None], topi].set(topw)
        top_g, tok_idx = jax.lax.top_k(gates.T, cap)
        xe = x[tok_idx]
        h = jax.nn.silu(jnp.einsum('ech,ehi->eci', xe, gate_w)) * jnp.einsum('ech,ehi->eci', xe, up_w)
        ye = jnp.einsum('eci,eih->ech', h, down_w) * top_g[..., None]
        out = jnp.zeros_like(x).at[tok_idx.reshape(-1)].add(ye.reshape(-1, H))
        return out.reshape(B, S, H)
    x = x + _L0_xcond_ref(_layernorm(x, axis=-1), ctx_1024, ctx_1024, condB_tau[:, None], fside_BxS2_0, L0_xcond_Wq, L0_xcond_bq, L0_xcond_Wk, L0_xcond_bk, L0_xcond_Wv, L0_xcond_bv, L0_xcond_Wo, L0_xcond_bo)
    x = x + _L0_ffn_ref(_layernorm(x, axis=-1), L0_ffn_gate_w, L0_ffn_w1, L0_ffn_w2)
    x = x + _L1_xcond_ref(_layernorm(x, axis=-1), ctx_1024, ctx_1024, condB_tau[:, None], fside_BxS2_0, L1_xcond_Wq, L1_xcond_bq, L1_xcond_Wk, L1_xcond_bk, L1_xcond_Wv, L1_xcond_bv, L1_xcond_Wo, L1_xcond_bo)
    x = x + _L1_ffn_ref(_layernorm(x, axis=-1), L1_ffn_router_w, L1_ffn_router_b, L1_ffn_routed_w1, L1_ffn_routed_w3, L1_ffn_routed_w2, L1_ffn_shared_w1, L1_ffn_shared_w3, L1_ffn_shared_w2)
    x = x + _L2_xcond_ref(ctx_1024, _layernorm(x, axis=-1), _lenS2, condB_pt, L2_xcond_W_a, L2_xcond_W_c)
    x = x + _L2_ffn_ref(_layernorm(x, axis=-1), L2_ffn_gate_w, L2_ffn_gate_b, L2_ffn_W1, L2_ffn_b1, L2_ffn_W2, L2_ffn_b2)
    x = x + _L3_xcond_ref(_layernorm(x, axis=-1), ctx_1024, ctx_1024, condB_tau[:, None], fside_BxS2_0, L3_xcond_Wq, L3_xcond_bq, L3_xcond_Wk, L3_xcond_bk, L3_xcond_Wv, L3_xcond_bv, L3_xcond_Wo, L3_xcond_bo)
    x = x + _L3_ffn_ref(_layernorm(x, axis=-1), L3_ffn_router_gate, L3_ffn_gate_w, L3_ffn_up_w, L3_ffn_down_w)
    return x

_drawn_inputs = setup_inputs


def setup_inputs(seed=0):
    import zlib

    import numpy as np

    out = dict(_drawn_inputs(seed))
    spreads = {'L1_xcond_bq': (0.0, 0.667),
     'L1_xcond_bk': (0.0, 2.0),
     'L1_xcond_bv': (0.0, 0.1),
     'L1_xcond_bo': (0.0, 0.1),
     'L1_ffn_router_b': (0.0, 0.8),
     'L2_ffn_gate_b': (0.0, 0.472),
     'L2_ffn_b1': (0.0, 2.0),
     'L2_ffn_b2': (0.0, 0.499)}
    factors = {'condB_pt': 8.0,
     'L0_xcond_bq': 7.48,
     'L0_xcond_bk': 64.0,
     'L0_xcond_bv': 2.701,
     'L0_xcond_bo': 4.167,
     'L1_ffn_router_w': 8.0,
     'L1_ffn_routed_w1': 8.0,
     'L1_ffn_routed_w3': 8.0,
     'L1_ffn_routed_w2': 8.0,
     'L1_ffn_shared_w1': 5.096,
     'L1_ffn_shared_w3': 5.197,
     'L1_ffn_shared_w2': 5.156,
     'L2_ffn_W1': 3.021,
     'L3_xcond_bq': 64.0,
     'L3_xcond_bk': 64.0,
     'L3_xcond_bv': 21.44,
     'L3_xcond_bo': 25.802,
     'L3_ffn_router_gate': 4.637,
     'L3_ffn_gate_w': 4.18,
     'L3_ffn_up_w': 4.105,
     'L3_ffn_down_w': 4.089}
    for name, (base, spread) in spreads.items():
        noise = np.random.default_rng([zlib.crc32(name.encode()), seed]).standard_normal(out[name].shape)
        drawn = base * np.exp(spread * noise) if base else spread * noise
        out[name] = jnp.asarray(drawn.astype(out[name].dtype))
    for name, factor in factors.items():
        out[name] = (out[name] * factor).astype(out[name].dtype)
    return out
```

```python
import math
from contextlib import ExitStack

import numpy as np

import concourse.bass as bass
from concourse import mybir

FP32 = mybir.dt.float32
FP32R = mybir.dt.float32r
BF16 = mybir.dt.bfloat16
I32 = mybir.dt.int32
ALU = mybir.AluOpType
ACT = mybir.ActivationFunctionType
AX = mybir.AxisListType

P = 128
B, SEQ, D = 4, 512, 256
T = B * SEQ
TILES = T // P
TPB = SEQ // P
DC = D // P
HEADS, DK = 16, 16
HPC = HEADS // DC
PAIRS = HEADS // 2
KEYS = 64
VW = 2 * DK + 2
E = 8
F = 1024
FC = F // P
FPAIRS = FC // 2
HID = 128
SHARED = 2
E_ALL = E + SHARED
SLOTS = 256
SB = SLOTS // P
KMAX = T // SLOTS
NT = (2 * T + E * (SLOTS - 1)) // SLOTS
CAP = math.ceil(1.25 * T * 2 / E)
CAP3 = int(1.25 * ((T * 2 + E - 1) // E))
EPS = 1e-5
WINDOW, DEV_POW = 16.0, 128.0
BANK = 512
LOWEST = -3.0e38
ARENA = 15360


class Signal:

    def __init__(self, semaphore, base):
        self.sem, self.base = semaphore, base

    def __call__(self, n):
        return self.sem, self.base + n


class Chain:

    def __init__(self, eng, sig, base=0):
        self.eng, self.sig, self.base, self.n = eng, sig, base, 0

    def add(self, ins):
        self.n += 1
        ins.then_inc(self.sig.sem, 1)

    def wait(self):
        self.eng.wait_ge(*self.sig(self.base + self.n))

    def link(self, ins):
        self.add(ins)
        self.wait()


class Stage:

    def __init__(self, sync, gpsimd, scalar, vector, tensor):
        self.sync, self.gpsimd, self.scalar, self.vector, self.tensor = sync, gpsimd, scalar, vector, tensor


def build(nc, io, out, stages=8):
    with ExitStack() as ctx:
        def sb(name, shape, dt=FP32):
            return ctx.enter_context(nc.sbuf_tensor(name, shape, dt))

        sems = {}

        def signal(name, total):
            if name not in sems:
                sems[name] = [ctx.enter_context(nc.semaphore(name)), 0]
            entry = sems[name]
            entry[1] += total
            return Signal(entry[0], entry[1] - total)

        x = sb("x", [P, TILES, D])
        ident = sb("ident", [P, P])
        ones_row = sb("ones_row", [1, P])
        before = sb("before", [P, P], BF16)
        ones_bf = sb("ones_bf", [P, P], BF16)
        head_of = sb("head_of", [P, HPC])
        rank_of = sb("rank_of", [P, E])
        key_no = sb("key_no", [P, KEYS])
        tile_no = sb("tile_no", [P, NT])
        step_no = sb("step_no", [P, KMAX])
        neg_half = sb("neg_half", [P, TPB])
        ctxT = sb("ctxT", [P, DC, B, 2, KEYS])
        tau_q = sb("tau_q", [P, B])
        delta_q = sb("delta_q", [1, B, KEYS])
        small = sb("small", [P, 16])
        stats = sb("stats", [P, TPB, 6])
        moments = sb("moments", [P, TPB, 2])
        var_eps = sb("var_eps", [P, TPB])
        rstd = sb("rstd", [P, TPB])
        scrap = sb("scrap", [P, 1])

        arena = sb("arena", [P, ARENA])

        def view(at, *shape, parts=P):
            n = int(np.prod(shape))
            v = arena[0:parts, at:at + n]
            if len(shape) == 1:
                return v
            names = "abcd"[:len(shape)]
            return v.rearrange(f"p ({' '.join(names)}) -> p {' '.join(names)}",
                               **dict(zip(names[1:], shape[1:])))

        w_parts = sb("w_parts", [P, 20480], FP32R)
        h_parts = sb("h_parts", [P, 8192], FP32R)
        xT_parts = sb("xT_parts", [P, 2048], FP32R)

        psum = ctx.enter_context(nc.psum_tensor("psum", [P, 8 * BANK], FP32))

        def bank(b, n=1):
            return psum[:, b * BANK:(b + n) * BANK]

        xs = nc.dram_tensor("xs_scratch", (NT * SLOTS, D), FP32).ap()
        ys = nc.dram_tensor("ys_scratch", (NT * SLOTS, D), FP32).ap()

        IN_DMAS = 3 + 2 * DC
        ROWS = P * 8
        zero_dmas = -(-NT * SLOTS // ROWS)
        zeros = view(0, 2048)
        s_in = signal("shared_inputs", 16 * IN_DMAS)
        s_memset, s_const = signal("memset", 8), signal("constants", 8)
        s_scaled, s_zeroed = signal("scaled_inputs", 2), signal("slots_zeroed", 16 * zero_dmas)

        def sync(sp):
            sp.dma_start(x[:, :, :], io["x"].rearrange("b (t p) d -> p (b t) d", p=P)).then_inc(s_in.sem, 16)
            for c in range(DC):
                for twice in range(2):
                    sp.dma_start(ctxT[:, c, :, twice, :], io["ctxT"][c * P:(c + 1) * P, :].rearrange("p (b k) -> p b k", b=B))\
                        .then_inc(s_in.sem, 16)
            sp.dma_start(tau_q[:, :], io["condB_tau"].to_broadcast([P, B])).then_inc(s_in.sem, 16)
            sp.dma_start(delta_q[:, :, :], io["fside_BxS2_0"].rearrange("(o b) k -> o b k", o=1)).then_inc(s_in.sem, 16)
            sp.wait_ge(*s_memset(8))
            for n in range(zero_dmas):
                rows = min(ROWS, NT * SLOTS - n * ROWS)
                sp.dma_start(xs[n * ROWS:n * ROWS + rows, :].rearrange("(p r) d -> p (r d)", p=P),
                             zeros[:, 0:rows // P * D]).then_inc(s_zeroed.sem, 16)

        def gpsimd(g):
            g.memset(ident[:, :], 0.0).then_inc(s_memset.sem, 1)
            g.memset(before[:, :], 1.0).then_inc(s_memset.sem, 1)
            g.memset(head_of[:, :], 1.0).then_inc(s_memset.sem, 1)
            g.memset(ones_row[:, :], 1.0).then_inc(s_memset.sem, 1)
            g.memset(ones_bf[:, :], 1.0).then_inc(s_memset.sem, 1)
            g.memset(neg_half[:, :], -0.5).then_inc(s_memset.sem, 1)
            g.memset(small[:, :], 0.0).then_inc(s_memset.sem, 1)
            g.memset(zeros, 0.0).then_inc(s_memset.sem, 1)
            g.wait_ge(*s_memset(8))
            g.affine_select(out=ident[:, :], in_=ident[:, :], compare_op=ALU.not_equal, fill=1.0,
                            base=0, pattern=[[-1, P]], channel_multiplier=1).then_inc(s_const.sem, 1)
            g.affine_select(out=before[:, :], in_=before[:, :], compare_op=ALU.is_gt, fill=0.0,
                            base=0, pattern=[[1, P]], channel_multiplier=-1).then_inc(s_const.sem, 1)
            g.affine_select(out=head_of[:, :], in_=head_of[:, :], compare_op=ALU.is_ge, fill=0.0,
                            base=0, pattern=[[-DK, HPC]], channel_multiplier=1).then_inc(s_const.sem, 1)
            g.wait_ge(*s_const(3))
            g.affine_select(out=head_of[:, :], in_=head_of[:, :], compare_op=ALU.is_ge, fill=0.0,
                            base=DK - 1, pattern=[[DK, HPC]], channel_multiplier=-1).then_inc(s_const.sem, 1)
            for t, pattern, base in ((rank_of, [[-1, E]], E), (key_no, [[1, KEYS]], 0),
                                     (tile_no, [[1, NT]], 0), (step_no, [[SLOTS, KMAX]], 0)):
                g.iota(t[:, :], pattern=pattern, base=base, channel_multiplier=0,
                       allow_small_or_imprecise_dtypes=True).then_inc(s_const.sem, 1)

        def vector(v):
            v.wait_ge(*s_in(IN_DMAS * 16))
            v.tensor_scalar(tau_q[:, :], tau_q[:, :], 1.0 / math.sqrt(DK), None, ALU.mult).then_inc(s_scaled.sem, 1)
            v.tensor_scalar(delta_q[:, :, :], delta_q[:, :, :], 1.0 / math.sqrt(DK), None, ALU.mult).then_inc(s_scaled.sem, 1)
            v.wait_ge(*s_scaled(2))
            v.wait_ge(*s_const(8))

        def tensor(t):
            t.wait_ge(*s_in(IN_DMAS * 16))
            t.wait_ge(*s_const(8))
            t.wait_ge(*s_scaled(2))

        def scalar(a):
            a.wait_ge(*s_const(8))

        start = Stage(sync, gpsimd, scalar, vector, tensor)

        def norm_vector(v, ch, i, dst, s_var, s_rstd, s_norm):
            for j in range(TPB):
                ch.add(v.bn_stats(stats[:, j, :], tile_of(i, j)))
            ch.wait()
            v.memset(scrap[:, :], 0.0)
            for j in range(TPB):
                ch.add(v.bn_aggr(moments[:, j, :], stats[:, j, :]))
            ch.wait()
            v.tensor_scalar(var_eps[:, :], moments[:, :, 1], EPS, None, ALU.add).then_inc(s_var.sem, 1)
            v.wait_ge(*s_rstd(i + 1))
            for j in range(TPB):
                v.tensor_scalar(dst[:, j, :], tile_of(i, j), moments[:, j, 0:1], rstd[:, j:j + 1],
                                ALU.subtract, ALU.mult).then_inc(s_norm.sem, 1)

        def tile_of(i, j):
            return x[:, bass.ds(i * TPB + j, 1), :].rearrange("p a d -> p (a d)")

        def norm_gpsimd(g, i, s_var, s_rstd):
            g.wait_ge(*s_var(i + 1))
            g.tensor_tensor(rstd[:, :], var_eps[:, :], neg_half[:, :], ALU.pow).then_inc(s_rstd.sem, 1)

        def attention(L, x_before):
            LINKS = 4 * TPB
            SPREAD = DC * B + DC + 2 * B
            kbd = view(0, DC, B, HPC * KEYS)
            vbd = view(4096, B, PAIRS, VW)
            at = 4096 + B * PAIRS * VW
            wq, wk, wv, wo = (view(at + k * 512, DC, D) for k in range(4))
            at += 2048
            xnb = view(at, TPB, D)
            xnT = view(at + 1024, DC, SEQ)
            qT = view(at + 2048, DC, SEQ)
            probs = view(at + 3072, 2, HEADS * KEYS)
            probsT = view(at + 5120, PAIRS, P)
            heads_out = view(at + 6144, D)
            headsT = view(at + 6400, DC, P)
            kt = qT
            bq, bk = small[:, 0:2], small[:, 2:4]
            assert at + 6656 + 576 <= ARENA
            rows = view(at + 6656, 2 * D, parts=1)
            sums_r = view(at + 6656 + 512, PAIRS * 2)
            top = view(at + 6656 + 544, 2, HEADS)
            io_w = {k: io[f"L{L}_xcond_W{k}"] for k in "qkvo"}

            s_w = signal("attn_weights", 8 * 16)
            s_clear = signal("attn_values_cleared", 3)
            s_k_ps, s_v_ps = signal("attn_keys_in_psum", 1), signal("attn_values_in_psum", 1)
            s_ch = signal("attn_dve_chain", SPREAD + LINKS * B)
            s_var, s_rstd, s_norm = signal("variance", B), signal("rstd", B), signal("attn_normed", TILES)
            s_xT_ps, s_xT = signal("attn_xT_in_psum", B), signal("attn_xT", 2 * B)
            s_q_ps, s_q = signal("attn_q_in_psum", 2 * B), signal("attn_q", 2 * B)
            s_sc, s_sub, s_exp = signal("attn_scores", TILES), signal("attn_shifted", TILES), signal("attn_exp", TILES)
            s_pT_ps, s_pT = signal("attn_pT_in_psum", 2 * TILES), signal("attn_pT", 2 * TILES)
            s_pv, s_o = signal("attn_pv", TILES), signal("attn_heads_out", TILES)
            s_oT_ps, s_oT = signal("attn_oT_in_psum", TILES), signal("attn_oT", TILES)
            s_y, s_x = signal("attn_y", TILES), signal("attn_x_updated", TILES)

            def sync(sp):
                if x_before is not None:
                    sp.wait_ge(*x_before)
                else:
                    sp.wait_ge(*s_zeroed(16 * zero_dmas))
                for dst, k in ((wk, "k"), (wv, "v"), (wq, "q"), (wo, "o")):
                    sp.dma_start(dst, io_w[k].rearrange("(c p) o -> p c o", p=P)).then_inc(s_w.sem, 16)
                sp.dma_start(bq, io[f"L{L}_xcond_bq"].rearrange("(c p) -> p c", p=P),
                             allow_slow_non_contiguous=True).then_inc(s_w.sem, 16)
                sp.dma_start(bk, io[f"L{L}_xcond_bk"].rearrange("(c p) -> p c", p=P),
                             allow_slow_non_contiguous=True).then_inc(s_w.sem, 16)
                sp.dma_start(rows[:, 0:D], io[f"L{L}_xcond_bv"].rearrange("(o d) -> o d", o=1)).then_inc(s_w.sem, 16)
                sp.dma_start(rows[:, D:2 * D], io[f"L{L}_xcond_bo"].rearrange("(o d) -> o d", o=1)).then_inc(s_w.sem, 16)

            def gpsimd(g):
                if x_before is not None:
                    g.wait_ge(*x_before)
                else:
                    g.wait_ge(*s_zeroed(16 * zero_dmas))
                g.memset(vbd, 0.0).then_inc(s_clear.sem, 1)
                g.wait_ge(*s_clear(1))
                g.memset(vbd[0:64, :, :, 2 * DK], 1.0).then_inc(s_clear.sem, 1)
                g.memset(vbd[64:128, :, :, 2 * DK + 1], 1.0).then_inc(s_clear.sem, 1)
                with g.Fori(0, B) as i:
                    norm_gpsimd(g, i, s_var, s_rstd)

            def tensor(t):
                t.wait_ge(*s_w(128))
                if x_before is not None:
                    t.wait_ge(*x_before)
                for oc in range(DC):
                    for kc in range(DC):
                        ins = t.matmul(bank(0)[:, oc * 256:(oc + 1) * 256], wk[:, kc, oc * P:(oc + 1) * P],
                                       ctxT[:, kc, :, 0, :], start=(kc == 0), stop=(kc == DC - 1))
                ins.then_inc(s_k_ps.sem, 1)
                for b in range(B):
                    o = bank(1 + b // 2)[:, (b % 2) * 256:(b % 2 + 1) * 256]
                    for kc in range(DC):
                        t.matmul(o, ctxT[:, kc, b, :, :].rearrange("p two k -> p (two k)"), wv[:, kc, :], start=(kc == 0), stop=False)
                    ins = t.matmul(o, ones_row[:, :], rows[:, 0:D], start=False, stop=True)
                ins.then_inc(s_v_ps.sem, 1)
                t.wait_ge(*s_ch(SPREAD))
                with t.Fori(0, B) as i:
                    for j in range(TPB):
                        t.wait_ge(*s_norm(TPB * i + j + 1))
                        for c in range(DC):
                            ins = t.transpose(bank(c)[:, j * P:(j + 1) * P], xnb[:, j, c * P:(c + 1) * P], ident[:, :])
                    ins.then_inc(s_xT_ps.sem, 1)
                    t.wait_ge(*s_xT(2 * i + 2))
                    t.wait_ge(*s_x(TPB * i))
                    for oc in range(DC):
                        for kc in range(DC):
                            ins = t.matmul(bank(2 + oc), wq[:, kc, oc * P:(oc + 1) * P], xnT[:, kc, :],
                                           start=(kc == 0), stop=(kc == DC - 1))
                        ins.then_inc(s_q_ps.sem, 1)
                    t.wait_ge(*s_q(2 * i + 2))

                    def scores(j):
                        if j >= 2:
                            t.wait_ge(*s_sub(TPB * i + j - 1))
                        for c in range(DC):
                            o = bank(4 + 2 * (j % 2) + c)
                            t.matmul(o, qT[:, c, j * P:(j + 1) * P],
                                     kbd[:, c, bass.ds(i, 1), :].rearrange("p a n -> p (a n)"),
                                     start=True, stop=False)
                            ins = t.matmul(o, ones_row[:, :],
                                           delta_q[:, bass.ds(i, 1), :].to_broadcast([1, HPC, KEYS]),
                                           start=False, stop=True)
                        ins.then_inc(s_sc.sem, 1)

                    scores(0)
                    for j in range(TPB):
                        m = TPB * i + j
                        if j + 1 < TPB:
                            scores(j + 1)
                        t.wait_ge(*s_exp(m + 1))
                        for h in range(2):
                            for c in range(4):
                                hp = 4 * h + c
                                ins = t.transpose(bank(h)[:, c * P:(c + 1) * P],
                                                  probs[:, j % 2, hp * P:(hp + 1) * P], ident[:, :])
                            ins.then_inc(s_pT_ps.sem, 1)
                        t.wait_ge(*s_pT(2 * m + 2))
                        for hp in range(PAIRS):
                            ins = t.matmul(bank(2)[:, hp * VW:(hp + 1) * VW], probsT[:, hp, :],
                                           vbd[:, bass.ds(i, 1), hp, :].rearrange("p a n -> p (a n)"),
                                           start=True, stop=True)
                        ins.then_inc(s_pv.sem, 1)
                        t.wait_ge(*s_o(m + 1))
                        t.wait_ge(*s_x(m))
                        for c in range(DC):
                            ins = t.transpose(bank(3)[:, c * P:(c + 1) * P], heads_out[:, c * P:(c + 1) * P], ident[:, :])
                        ins.then_inc(s_oT_ps.sem, 1)
                        t.wait_ge(*s_oT(m + 1))
                        for c in range(DC):
                            t.matmul(bank(3)[:, D:2 * D], headsT[:, c, :], wo[:, c, :], start=(c == 0), stop=False)
                        t.matmul(bank(3)[:, D:2 * D], ones_row[:, :], rows[:, D:2 * D],
                                 start=False, stop=True).then_inc(s_y.sem, 1)

            def scalar(a):
                with a.Fori(0, B) as i:
                    a.wait_ge(*s_xT_ps(i + 1))
                    for c in range(DC):
                        a.copy(xnT[:, c, :], bank(c)).then_inc(s_xT.sem, 1)
                    for c in range(DC):
                        a.wait_ge(*s_q_ps(2 * i + c + 1))
                        a.activation(qT[:, c, :], bank(2 + c), ACT.Identity, bias=bq[:, c:c + 1]).then_inc(s_q.sem, 1)

                    def exp(j):
                        a.wait_ge(*s_sub(TPB * i + j + 1))
                        a.activation(probs[:, j % 2, :], probs[:, j % 2, :], ACT.Exp).then_inc(s_exp.sem, 1)

                    exp(0)
                    for j in range(TPB):
                        m = TPB * i + j
                        a.wait_ge(*s_pv(m))
                        for h in range(2):
                            a.wait_ge(*s_pT_ps(2 * m + h + 1))
                            a.copy(probsT[:, 4 * h:4 * h + 4, :],
                                   bank(h).rearrange("p (c q) -> p c q", c=4)).then_inc(s_pT.sem, 1)
                        if j + 1 < TPB:
                            exp(j + 1)
                        a.wait_ge(*s_y(m))
                        a.wait_ge(*s_oT_ps(m + 1))
                        a.copy(headsT[:, :, :], bank(3)[:, 0:D].rearrange("p (c q) -> p c q", c=DC)).then_inc(s_oT.sem, 1)

            def vector(v):
                ch = Chain(v, s_ch)
                v.wait_ge(*s_k_ps(1))
                for oc in range(DC):
                    for b in range(B):
                        o = oc * 256 + b * KEYS
                        v.tensor_scalar(kt[:, oc, b * KEYS:(b + 1) * KEYS], bank(0)[:, o:o + KEYS],
                                        bk[:, oc:oc + 1], tau_q[:, b:b + 1], ALU.add, ALU.mult).then_inc(s_ch.sem, 1)
                        ch.n += 1
                v.wait_ge(*s_ch(ch.n))
                for oc in range(DC):
                    v.tensor_tensor(kbd[:, oc, :, :].rearrange("p b (h k) -> p b h k", h=HPC),
                                    kt[:, oc, 0:B * KEYS].rearrange("p (b k) -> p b k", b=B)
                                    .unsqueeze(2).to_broadcast([P, B, HPC, KEYS]),
                                    head_of[:, :].unsqueeze(1).unsqueeze(3).to_broadcast([P, B, HPC, KEYS]),
                                    ALU.mult).then_inc(s_ch.sem, 1)
                    ch.n += 1
                v.wait_ge(*s_v_ps(1))
                v.wait_ge(*s_clear(3))
                for b in range(B):
                    ps_v = bank(1 + b // 2)[:, (b % 2) * 256:(b % 2 + 1) * 256].rearrange(
                        "p (hp two k) -> p hp two k", two=2, k=DK)
                    for half in range(2):
                        rows_of = slice(64 * half, 64 * half + 64)
                        v.tensor_copy(vbd[rows_of, b, :, half * DK:(half + 1) * DK], ps_v[rows_of, :, half, :])\
                            .then_inc(s_ch.sem, 1)
                        ch.n += 1
                assert ch.n == SPREAD
                with v.Fori(0, B) as i:
                    ch = Chain(v, s_ch, SPREAD + i * LINKS)
                    norm_vector(v, ch, i, xnb, s_var, s_rstd, s_norm)

                    def shift(j):
                        m = TPB * i + j
                        v.wait_ge(*s_sc(m + 1))
                        sc = bank(4 + 2 * (j % 2), 2).rearrange("p (h k) -> p h k", k=KEYS)
                        ch.link(v.reduce_max(top[:, j % 2, :], sc, AX.X))
                        v.tensor_tensor(probs[:, j % 2, :].rearrange("p (h k) -> p h k", k=KEYS), sc,
                                        top[:, j % 2, :].unsqueeze(2).to_broadcast([P, HEADS, KEYS]),
                                        ALU.subtract).then_inc(s_sub.sem, 1)

                    shift(0)
                    for j in range(TPB):
                        m = TPB * i + j
                        if j + 1 < TPB:
                            shift(j + 1)
                        v.wait_ge(*s_pv(m + 1))
                        pv = bank(2)[:, 0:PAIRS * VW].rearrange("p (h w) -> p h w", w=VW)
                        ch.link(v.reciprocal(sums_r.rearrange("p (h two) -> p h two", two=2), pv[:, :, 2 * DK:VW]))
                        v.tensor_tensor(heads_out.rearrange("p (h k) -> p h k", k=DK).rearrange("p (h two) k -> p h two k", two=2),
                                        pv[:, :, 0:2 * DK].rearrange("p h (two k) -> p h two k", two=2),
                                        sums_r.rearrange("p (h two) -> p h two", two=2).unsqueeze(3)
                                        .to_broadcast([P, PAIRS, 2, DK]), ALU.mult).then_inc(s_o.sem, 1)
                        v.wait_ge(*s_y(m + 1))
                        v.tensor_tensor(tile_of(i, j), tile_of(i, j), bank(3)[:, D:2 * D], ALU.add).then_inc(s_x.sem, 1)
                    assert ch.n == LINKS
                v.wait_ge(*s_x(TILES))

            return Stage(sync, gpsimd, scalar, vector, tensor), s_x(TILES)

        raw = [view(k * 2048, 2048) for k in range(3)]
        x_rows = view(6144, 2, SB, D)
        y_rows = view(7168, 2, SB, D)
        h_raw = view(8192, 2, 2 * SLOTS)
        h_gate = view(9216, 2, 2 * SLOTS)
        work = [view(7168 + k * TILES * E, TILES, E) for k in range(16)]
        route_xn = view(9216, TPB, D)
        route_xT = view(10240, DC, SEQ)
        xn = view(11264, TILES, D)
        assert 11264 + TILES * D <= ARENA

        masks = sb("masks", [P, 2, TILES, E])
        masks_bf = sb("masks_bf", [P, 2, TILES, E], BF16)
        best = sb("best", [P, 2, TILES])
        gates = sb("gates", [P, TILES, E_ALL])
        slot_f = sb("slot_f", [P, 2, TILES])
        slot = sb("slot", [P, 2, TILES], I32)
        expert_f = sb("expert_f", [1, NT])
        expert = sb("expert", [1, NT], I32)
        counts = sb("counts", [P, 8, E])
        limit = sb("limit", [P, E], I32)
        tries = sb("tries", [P, 3, E], I32)
        tile_rows = [sb(f"tile_row{k}", [P, TILES]) for k in range(3)]
        router_w = sb("router_w", [P, DC, E])
        router_b = sb("router_b", [1, E])

        def router(L, weight, bias, x_before):
            SEARCH = 15 if L == 3 else 0
            LOOP_LINKS = 2 * TPB
            s_w = signal("route_weights", 16 * (2 if bias is not None else 1))
            s_ch = signal(f"route_chain{L}", 0)
            s_var, s_rstd, s_norm = signal("variance", B), signal("rstd", B), signal("route_normed", TILES)
            s_xT_ps, s_xT, s_xn = signal("route_xT_in_psum", B), signal("route_xT", 2 * B), signal("route_xn", B)
            s_lg_ps, s_lg = signal("route_logits_in_psum", B), signal("route_logits", B)
            s_less, s_exp = signal("route_shifted", 1), signal("route_exp", 1)
            rounds = {0: 1, 1: 0, 2: 1, 3: SEARCH + 2}[L]
            s_mask, s_count = signal("route_masks", rounds), signal("route_counts", rounds)
            s_slot = signal("route_slots", 1)

            def sync(sp):
                sp.wait_ge(*x_before)
                sp.dma_start(router_w[:, :, :], weight.rearrange("(c p) e -> p c e", p=P)).then_inc(s_w.sem, 16)
                if bias is not None:
                    sp.dma_start(router_b[:, :], bias.rearrange("(o e) -> o e", o=1)).then_inc(s_w.sem, 16)

            def gpsimd(g):
                with g.Fori(0, B) as i:
                    norm_gpsimd(g, i, s_var, s_rstd)

            def tensor(t):
                t.wait_ge(*s_w(16 * (2 if bias is not None else 1)))
                t.wait_ge(*x_before)
                with t.Fori(0, B) as i:
                    t.wait_ge(*s_lg(i))
                    for j in range(TPB):
                        t.wait_ge(*s_norm(TPB * i + j + 1))
                        for c in range(DC):
                            ins = t.transpose(bank(c)[:, j * P:(j + 1) * P], route_xn[:, j, c * P:(c + 1) * P], ident[:, :])
                    ins.then_inc(s_xT_ps.sem, 1)
                    t.wait_ge(*s_xT(2 * i + 2))
                    for j in range(TPB):
                        o = bank(2)[:, j * E:(j + 1) * E]
                        for c in range(DC):
                            ins = t.matmul(o, route_xT[:, c, j * P:(j + 1) * P], router_w[:, c, :], start=(c == 0),
                                           stop=(c == DC - 1 and bias is None))
                        if bias is not None:
                            ins = t.matmul(o, ones_row[:, :], router_b[:, :], start=False, stop=True)
                    ins.then_inc(s_lg_ps.sem, 1)
                if L == 1:
                    return
                for n in range(SEARCH):
                    t.wait_ge(*s_mask(n + 1))
                    t.matmul(bank(5)[:, 0:3 * E], ones_bf[:, :], masks_bf[:, 0, 0:3, :],
                             start=True, stop=True).then_inc(s_count.sem, 1)
                if SEARCH:
                    t.wait_ge(*s_mask(SEARCH + 1))
                    t.matmul(bank(3)[:, 0:256], before[:, :], masks_bf[:, :, :, :], start=True, stop=True)
                    t.matmul(bank(4)[:, 0:256], ones_bf[:, :], masks_bf[:, :, :, :],
                             start=True, stop=True).then_inc(s_count.sem, 1)
                t.wait_ge(*s_mask((SEARCH + 2) if SEARCH else 1))
                t.matmul(bank(3)[:, 0:256], before[:, :], masks_bf[:, :, :, :], start=True, stop=True)
                t.matmul(bank(4)[:, 0:256], ones_bf[:, :], masks_bf[:, :, :, :],
                         start=True, stop=True).then_inc(s_count.sem, 1)

            def scalar(a):
                with a.Fori(0, B) as i:
                    a.wait_ge(*s_norm(TPB * i + TPB))
                    a.copy(xn[:, bass.ds(TPB * i, TPB), :], route_xn).then_inc(s_xn.sem, 1)
                    a.wait_ge(*s_xT_ps(i + 1))
                    for c in range(DC):
                        a.copy(route_xT[:, c, :], bank(c)).then_inc(s_xT.sem, 1)
                a.wait_ge(*s_less(1))
                if L == 1:
                    a.activation(tile_rows[0][:, :], tile_rows[0][:, :], ACT.Exp).then_inc(s_exp.sem, 1)
                else:
                    a.activation(work[0], work[0], ACT.Exp).then_inc(s_exp.sem, 1)

            def per_tile(row):
                return row.unsqueeze(2).to_broadcast([P, TILES, E])

            def vector(v):
                with v.Fori(0, B) as i:
                    ch = Chain(v, s_ch, i * LOOP_LINKS)
                    v.wait_ge(*s_xn(i))
                    norm_vector(v, ch, i, route_xn, s_var, s_rstd, s_norm)
                    v.wait_ge(*s_lg_ps(i + 1))
                    v.tensor_copy(work[0][:, bass.ds(TPB * i, TPB), :],
                                  bank(2)[:, 0:TPB * E].rearrange("p (j e) -> p j e", e=E)).then_inc(s_lg.sem, 1)
                    assert ch.n == LOOP_LINKS
                ch = Chain(v, s_ch, B * LOOP_LINKS)
                v.wait_ge(*s_lg(B))
                values, hit, ranked, second = work[0], work[1], work[2], work[3]
                top_row, rank_row, sum_row = (r[:, :] for r in tile_rows)
                if L != 1:
                    ch.link(v.reduce_max(top_row, values, AX.X))
                    v.tensor_tensor(values, values, per_tile(top_row), ALU.subtract).then_inc(s_less.sem, 1)
                    v.wait_ge(*s_exp(1))
                    ch.link(v.reduce_sum(sum_row, values, AX.X))
                    ch.link(v.reciprocal(rank_row, sum_row))
                    ch.link(v.tensor_tensor(values, values, per_tile(rank_row), ALU.mult))
                for c in range(2):
                    source = values if c == 0 else second
                    ch.link(v.reduce_max(best[:, c, :], source, AX.X))
                    ch.link(v.tensor_tensor(hit, source, per_tile(best[:, c, :]), ALU.is_equal))
                    ch.link(v.tensor_tensor(ranked, hit, rank_of[:, :].unsqueeze(1).to_broadcast([P, TILES, E]), ALU.mult))
                    ch.link(v.reduce_max(rank_row, ranked, AX.X))
                    ch.link(v.tensor_tensor(masks[:, c, :, :], ranked, per_tile(rank_row), ALU.is_equal))
                    if c == 0:
                        ch.link(v.scalar_tensor_tensor(second, masks[:, 0, :, :], LOWEST, values, ALU.mult, ALU.add))
                if L in (0, 3):
                    ch.link(v.tensor_tensor(sum_row, best[:, 0, :], best[:, 1, :], ALU.add))
                    if L == 3:
                        ch.link(v.tensor_scalar(sum_row, sum_row, 1e-9, None, ALU.add))
                    ch.link(v.reciprocal(rank_row, sum_row))
                    ch.link(v.tensor_tensor(best[:, :, :], best[:, :, :],
                                            rank_row.unsqueeze(1).to_broadcast([P, 2, TILES]), ALU.mult))
                if L == 1:
                    v.tensor_tensor(top_row, best[:, 1, :], best[:, 0, :], ALU.subtract).then_inc(s_less.sem, 1)
                    v.wait_ge(*s_exp(1))
                    ch.link(v.tensor_scalar(sum_row, top_row, 1.0, None, ALU.add))
                    ch.link(v.reciprocal(best[:, 0, :], sum_row))
                    ch.link(v.tensor_tensor(best[:, 1, :], best[:, 0, :], top_row, ALU.mult))
                if L in (1, 3):
                    for c in range(2):
                        ch.link(v.tensor_tensor(work[4 + c], masks[:, c, :, :], per_tile(best[:, c, :]), ALU.mult))
                if L == 1:
                    ch.link(v.memset(gates[:, :, :], 1.0))
                    v.tensor_tensor(gates[:, :, 0:E], work[4], work[5], ALU.add).then_inc(s_slot.sem, 1)
                    v.wait_ge(*s_slot(1))
                    return

                def over_tiles():
                    a, b = (view(7168 + k * TILES * E, 2, TILES, E) for k in (8, 10))
                    ch.link(v.tensor_copy(a, bank(4)[:, 0:256].rearrange("p (c t e) -> p c t e", c=2, e=E)))
                    step = 1
                    while step < TILES:
                        ch.add(v.tensor_copy(b[:, :, 0:step, :], a[:, :, 0:step, :]))
                        ch.link(v.tensor_tensor(b[:, :, step:, :], a[:, :, step:, :], a[:, :, :TILES - step, :], ALU.add))
                        a, b = b, a
                        step *= 2
                    ch.link(v.tensor_tensor(b, a, bank(4)[:, 0:256].rearrange("p (c t e) -> p c t e", c=2, e=E), ALU.subtract))
                    ch.link(v.tensor_tensor(b, b, bank(3)[:, 0:256].rearrange("p (c t e) -> p c t e", c=2, e=E), ALU.add))
                    return a, b

                if L == 3:
                    gate, over, at_limit = work[4], work[6], work[7]
                    ch.link(v.tensor_tensor(gate, work[4], work[5], ALU.add))
                    ch.link(v.memset(limit[:, :], 0))
                    passed = view(7168 + 8 * TILES * E, 3, TILES, E)
                    for n in range(SEARCH):
                        shift = 2 * (SEARCH - 1 - n)
                        for k in range(3):
                            ch.add(v.tensor_scalar(tries[:, k, :], limit[:, :], (k + 1) << shift, None, ALU.bitwise_or))
                        ch.wait()
                        ch.link(v.tensor_tensor(passed, gate.unsqueeze(1).to_broadcast([P, 3, TILES, E]),
                                                tries[:, :, :].bitcast(FP32).unsqueeze(2).to_broadcast([P, 3, TILES, E]),
                                                ALU.is_ge))
                        with nc.allow_low_precision("whole numbers up to 16"):
                            v.reduce_sum(masks_bf[:, 0, 0:3, :], passed.rearrange("p k t e -> p k e t"), AX.X)\
                                .then_inc(s_mask.sem, 1)
                        v.wait_ge(*s_count(n + 1))
                        ch.link(v.tensor_scalar(counts[:, 0:3, :], bank(5)[:, 0:3 * E].rearrange("p (k e) -> p k e", e=E),
                                                CAP3 - 0.5, float(1 << shift), ALU.is_gt, ALU.mult))
                        with nc.allow_low_precision("one of four multiples of a power of two"):
                            ch.link(v.reduce_sum(tries[:, 0, :], counts[:, 0:3, :].rearrange("p k e -> p e k"), AX.X))
                        ch.link(v.tensor_tensor(limit[:, :], limit[:, :], tries[:, 0, :], ALU.bitwise_or))
                    limit_f = limit[:, :].bitcast(FP32).unsqueeze(1).to_broadcast([P, TILES, E])
                    ch.add(v.tensor_tensor(over, gate, limit_f, ALU.is_gt))
                    ch.link(v.tensor_tensor(at_limit, gate, limit_f, ALU.is_equal))
                    ch.add(v.tensor_copy(masks_bf[:, 0, :, :], over))
                    v.tensor_copy(masks_bf[:, 1, :, :], at_limit).then_inc(s_mask.sem, 1)
                    v.wait_ge(*s_count(SEARCH + 1))
                    total, place = over_tiles()
                    room = counts[:, 0, :]
                    ch.link(v.tensor_scalar(room, total[:, 0, TILES - 1, :], -1.0, float(CAP3), ALU.mult, ALU.add))
                    ch.link(v.tensor_tensor(work[4], place[:, 1, :, :], room.unsqueeze(1).to_broadcast([P, TILES, E]), ALU.is_lt))
                    ch.link(v.tensor_tensor(work[5], work[4], at_limit, ALU.mult))
                    ch.link(v.tensor_tensor(work[4], work[5], over, ALU.add))
                    kept = view(7168 + 12 * TILES * E, 2, TILES, E)
                    ch.link(v.tensor_tensor(kept, masks[:, :, :, :], work[4].unsqueeze(1).to_broadcast([P, 2, TILES, E]), ALU.mult))
                    ch.link(v.reduce_sum(slot_f[:, :, :], kept, AX.X))
                    ch.link(v.tensor_tensor(best[:, :, :], best[:, :, :], slot_f[:, :, :], ALU.mult))

                v.tensor_copy(masks_bf[:, :, :, :], masks[:, :, :, :]).then_inc(s_mask.sem, 1)
                v.wait_ge(*s_count(SEARCH + 2 if SEARCH else 1))
                total, place = over_tiles()
                picked = view(7168 + 12 * TILES * E, 2, TILES, E)
                if L == 2:
                    ch.link(v.tensor_tensor(picked, masks[:, :, :, :], place, ALU.mult))
                    ch.link(v.reduce_sum(slot_f[:, :, :], picked, AX.X))
                    ch.link(v.scalar_tensor_tensor(best[:, :, :], slot_f[:, :, :], CAP - 0.5, best[:, :, :], ALU.is_lt, ALU.mult))
                number, tiles, end, other, first = (counts[:, k, :] for k in range(5))
                ch.link(v.tensor_tensor(number, total[:, 0, TILES - 1, :], total[:, 1, TILES - 1, :], ALU.add))
                more = work[0].rearrange("p t e -> p (t e)")[:, 0:E * KMAX].rearrange("p (e k) -> p e k", k=KMAX)
                ch.link(v.tensor_tensor(more, number.unsqueeze(2).to_broadcast([P, E, KMAX]),
                                        step_no[:, :].unsqueeze(1).to_broadcast([P, E, KMAX]), ALU.is_gt))
                ch.link(v.reduce_sum(tiles, more, AX.X))
                ch.link(v.tensor_copy(end, tiles))
                a, b = end, other
                for step in (1, 2, 4):
                    ch.add(v.tensor_copy(b[:, 0:step], a[:, 0:step]))
                    ch.link(v.tensor_tensor(b[:, step:], a[:, step:], a[:, :E - step], ALU.add))
                    a, b = b, a
                end = a
                ch.link(v.tensor_tensor(first, end, tiles, ALU.subtract))
                ch.link(v.tensor_scalar(first, first, float(SLOTS), None, ALU.mult))
                ch.link(v.tensor_tensor(work[1], place[:, 0, :, :], place[:, 1, :, :], ALU.add))
                ch.link(v.tensor_tensor(work[2], work[1], first.unsqueeze(1).to_broadcast([P, TILES, E]), ALU.add))
                ch.link(v.tensor_tensor(picked, masks[:, :, :, :], work[2].unsqueeze(1).to_broadcast([P, 2, TILES, E]), ALU.mult))
                ch.link(v.reduce_sum(slot_f[:, :, :], picked, AX.X))
                ch.link(v.tensor_copy(slot[:, :, :], slot_f[:, :, :]))
                ended = view(7168, NT, E, parts=1)
                ch.link(v.tensor_tensor(ended, end[0:1, :].unsqueeze(1).to_broadcast([1, NT, E]),
                                        tile_no[0:1, :].unsqueeze(2).to_broadcast([1, NT, E]), ALU.is_le))
                ch.link(v.reduce_sum(expert_f[:, :], ended, AX.X))
                v.tensor_scalar(expert[:, :], expert_f[:, :], float(E - 1), None, ALU.min).then_inc(s_slot.sem, 1)
                v.wait_ge(*s_slot(1))

            return Stage(sync, gpsimd, scalar, vector, tensor), s_slot(1)

        def moe(L, kind, w1, w2, w3=None, b1=None, b2=None, routed=None):
            lead = 0 if w3 is not None else 1
            w_ins = [w1] + ([w3] if w3 is not None else [])
            n_in = len(w_ins)
            def parts(k):
                v = w_parts[:, k * 2048:(k + 1) * 2048]
                return v
            in_parts = [[[parts(4 * m + 2 * u + q).rearrange("p (c f) -> p c f", c=DC) for q in range(2)]
                         for u in range(2)] for m in range(n_in)]
            out_parts = [[parts(4 * n_in + 2 * u + q).rearrange("p (c o) -> p c o", c=FC) for q in range(2)]
                         for u in range(lead + 1)]
            h_part = [[h_parts[:, (2 * u + q) * 2048:(2 * u + q + 1) * 2048].rearrange("p (c s) -> p c s", c=FC)
                       for q in range(2)] for u in range(2)]
            x_part = [[xT_parts[:, (2 * u + q) * 512:(2 * u + q + 1) * 512].rearrange("p (c s) -> p c s", c=DC)
                       for q in range(2)] for u in range(2)]
            half = [(NT + 1 - u) // 2 for u in range(2)]
            per_x = 16 * (2 if b1 is not None else 1)

            s_disp = signal("moe_dispatched", 16 * 2 * TILES)
            s_raw = [signal(f"moe_raw{m}", 16 * NT) for m in range(n_in)]
            s_raw2 = signal("moe_raw_w2", 16 * NT)
            s_xin = [signal(f"moe_x_in{u}", per_x * half[u]) for u in range(2)]
            s_b2 = [signal(f"moe_b2_in{u}", 16 * half[u]) for u in range(2)] if b2 is not None else None
            s_hi = [signal(f"moe_w_high{m}", 4 * NT) for m in range(n_in)]
            s_hi2 = signal("moe_w2_high", 4 * NT)
            s_split = [signal(f"moe_w_split{m}", NT) for m in range(n_in)]
            s_split2 = signal("moe_w2_split", NT)
            s_xT_ps = [signal(f"moe_xT_in_psum{u}", half[u]) for u in range(2)]
            s_xhi, s_xsplit = signal("moe_x_high", NT), signal("moe_x_split", NT)
            s_hps = signal("moe_h_in_psum", FPAIRS * NT)
            s_act = signal("moe_activated", FPAIRS * NT)
            s_gated = signal("moe_gated", FPAIRS * NT if kind == "swiglu" else 0)
            s_hhi, s_hsplit = signal("moe_h_high", FPAIRS * NT), signal("moe_h_split", FPAIRS * NT)
            s_mm2 = [signal(f"moe_mm2{u}", half[u]) for u in range(2)]
            s_y = [signal(f"moe_y_in_sbuf{u}", half[u]) for u in range(2)]
            s_stored = [signal(f"moe_y_stored{u}", 16 * half[u]) for u in range(2)]
            GROUP, GROUPS = 4, 4
            s_back = [signal(f"moe_gathered{k}", 16 * 2 * TILES // GROUPS) for k in range(GROUPS)]
            s_comb = signal("moe_combined", 2 * TILES)

            def exists(t):
                return not isinstance(t, int) or 0 <= t < NT

            def tiles(eng, step):
                pairs = (NT - 2) // 2
                with eng.Fori(0, pairs) as it:
                    step(2 * it, 0, it)
                    step(2 * it + 1, 1, it)
                for t in range(2 * pairs, NT):
                    step(t, t % 2, t // 2)

            def sync(sp):
                sp.wait_ge(*routed)

                def expert_of(t):
                    return sp.value_load(expert[0:1, bass.ds(t, 1)] if not isinstance(t, int) else expert[0:1, t:t + 1],
                                         min_val=0, max_val=E - 1)

                def load_in(t, u, it):
                    e = expert_of(t)
                    for m in range(n_in):
                        sp.wait_ge(*s_split[m](t))
                        sp.dma_start(raw[m].rearrange("p (c f) -> p c f", c=DC),
                                     w_ins[m][bass.ds(e, 1), :, :].rearrange("a (c p) f -> p (a c) f", p=P))\
                            .then_inc(s_raw[m].sem, 16)
                    if isinstance(t, int) and t == 0:
                        sp.wait_ge(*s_disp(16 * 2 * TILES))
                    sp.wait_ge(*s_xT_ps[u](it))
                    sp.dma_start(x_rows[:, u, :, :], xs[bass.ds(t * SLOTS, SLOTS), :].rearrange("(s p) d -> p s d", p=P))\
                        .then_inc(s_xin[u].sem, 16)
                    if b1 is not None:
                        if not isinstance(t, int) or t > 0:
                            sp.wait_ge(*s_act(FPAIRS * (t - 1)))
                        sp.dma_start(b1_buf[:, u, :], b1[bass.ds(e, 1), :, :].rearrange("a p c -> p (a c)"))\
                            .then_inc(s_xin[u].sem, 16)

                def load_out(t, u, it):
                    e = expert_of(t)
                    sp.wait_ge(*s_split2(t))
                    sp.dma_start(raw[2].rearrange("p (c o) -> p c o", c=FC),
                                 w2[bass.ds(e, 1), :, :].rearrange("a (c p) o -> p (a c) o", p=P))\
                        .then_inc(s_raw2.sem, 16)
                    if b2 is not None:
                        sp.wait_ge(*s_mm2[u](it))
                        sp.dma_start(b2_buf[:, u, :], b2[bass.ds(e, 1), :]).then_inc(s_b2[u].sem, 16)

                load_in(0, 0, 0)

                def step(t, u, it):
                    if exists(t + 1):
                        load_in(t + 1, 1 - u, it + u)
                    load_out(t, u, it)

                tiles(sp, step)

            def gpsimd(g):
                g.wait_ge(*routed)
                for t in range(TILES):
                    for c in range(2):
                        g.indirect_dma_start(out=xs, out_offset=bass.IndirectOffsetOnAxis(ap=slot[:, c, t:t + 1], axis=0),
                                             in_=xn[:, t, :], in_offset=None).then_inc(s_disp.sem, 16)

                def step(t, u, it):
                    g.wait_ge(*s_y[u](it + 1))
                    g.dma_start(ys[bass.ds(t * SLOTS, SLOTS), :].rearrange("(s p) d -> p s d", p=P),
                                y_rows[:, u, :, :]).then_inc(s_stored[u].sem, 16)

                tiles(g, step)
                for u in range(2):
                    g.wait_ge(*s_stored[u](16 * half[u]))
                for t in range(TILES):
                    for c in range(2):
                        n = 2 * t + c
                        if n % GROUP == 0 and n >= GROUP * GROUPS:
                            g.wait_ge(*s_comb(n - GROUP * (GROUPS - 1)))
                        g.indirect_dma_start(out=y_back[:, n % 16, :], out_offset=None, in_=ys,
                                             in_offset=bass.IndirectOffsetOnAxis(ap=slot[:, c, t:t + 1], axis=0))\
                            .then_inc(s_back[n // GROUP % GROUPS].sem, 16)

            def tensor(t_eng):
                def product(o, pairs, first, last):
                    (ah, al), (bh, bl) = pairs
                    t_eng.matmul(o, ah, bh, start=first, stop=False)
                    t_eng.matmul(o, ah, bl, start=False, stop=False)
                    return t_eng.matmul(o, al, bh, start=False, stop=last)

                def transposes(t, u, it):
                    t_eng.wait_ge(*s_xin[u](per_x * (it + 1)))
                    t_eng.wait_ge(*s_xsplit(t))
                    for s in range(SB):
                        for c in range(DC):
                            o = bank(6)[:, c * SLOTS + s * P:c * SLOTS + (s + 1) * P]
                            ins = t_eng.transpose(o, x_rows[:, u, s, c * P:(c + 1) * P], ident[:, :])
                    ins.then_inc(s_xT_ps[u].sem, 1)

                def hidden(t, u, it):
                    for m in range(n_in):
                        t_eng.wait_ge(*s_split[m](t + 1))
                    t_eng.wait_ge(*s_xsplit(t + 1))
                    for p in range(FPAIRS):
                        for m in range(n_in):
                            k = p if n_in == 1 else 2 * m + p % 2
                            if n_in == 1 and (not isinstance(t, int) or t > 0):
                                t_eng.wait_ge(*s_act(FPAIRS * (t - 1) + p + 1))
                            if n_in == 2 and (not isinstance(t, int) or t > 0 or p >= 2):
                                t_eng.wait_ge(*(s_act, s_gated)[m](FPAIRS * t + p - 1))
                            for q in range(2):
                                f = 2 * p + q
                                for c in range(DC):
                                    ins = product(bank(k)[:, q * SLOTS:(q + 1) * SLOTS],
                                                  ([in_parts[m][u][z][:, c, f * P:(f + 1) * P] for z in range(2)],
                                                   [x_part[u][z][:, c, :] for z in range(2)]), c == 0, c == DC - 1)
                        ins.then_inc(s_hps.sem, 1)

                def output(t, u, it):
                    t_eng.wait_ge(*s_split2(t + 1))
                    t_eng.wait_ge(*s_y[u](it))
                    if b2 is not None:
                        t_eng.wait_ge(*s_b2[u](16 * (it + 1)))
                    for s in range(SB):
                        o = bank(4 + u)[:, s * D:(s + 1) * D]
                        for f in range(FC):
                            if s == 0 and f % 2 == 0:
                                t_eng.wait_ge(*s_hsplit(FPAIRS * t + f // 2 + 1))
                            ins = product(o, ([h_part[u][z][:, f, s * P:(s + 1) * P] for z in range(2)],
                                              [out_parts[u * lead][z][:, f, :] for z in range(2)]),
                                          f == 0, f == FC - 1 and b2 is None)
                        if b2 is not None:
                            ins = t_eng.matmul(o, ones_row[:, :], b2_buf[:, u, :], start=False, stop=True)
                    ins.then_inc(s_mm2[u].sem, 1)

                transposes(0, 0, 0)
                hidden(0, 0, 0)
                transposes(1, 1, 0)

                def step(t, u, it):
                    if exists(t + 1):
                        hidden(t + 1, 1 - u, it + u)
                    if exists(t + 2):
                        transposes(t + 2, u, it + 1)
                    output(t, u, it)

                tiles(t_eng, step)

            def scalar(a):
                def high(m, t, u, it, q):
                    if q == 0:
                        a.wait_ge(*s_raw[m](16 * (t + 1)))
                        if not isinstance(t, int) or t >= 2:
                            a.wait_ge(*s_hps(FPAIRS * (t - 1)))
                    a.copy(in_parts[m][u][0].rearrange("p c f -> p (c f)")[:, q * 512:(q + 1) * 512],
                           raw[m][:, q * 512:(q + 1) * 512]).then_inc(s_hi[m].sem, 1)

                def high2(t, u, it, q):
                    if q == 0:
                        a.wait_ge(*s_raw2(16 * (t + 1)))
                        if lead:
                            a.wait_ge(*s_mm2[u](it))
                        elif not isinstance(t, int) or t > 0:
                            a.wait_ge(*s_mm2[1 - u](it + u))
                    a.copy(out_parts[u * lead][0].rearrange("p c o -> p (c o)")[:, q * 512:(q + 1) * 512],
                           raw[2][:, q * 512:(q + 1) * 512]).then_inc(s_hi2.sem, 1)

                def high_x(t, u, it):
                    a.wait_ge(*s_xT_ps[u](it + 1))
                    a.copy(x_part[u][0], bank(6).rearrange("p (c s) -> p c s", c=DC)).then_inc(s_xhi.sem, 1)

                def activate(t, u, it, p):
                    a.wait_ge(*s_hps(FPAIRS * t + p + 1))
                    first = isinstance(t, int) and t == 0 and p < 2
                    if kind == "swiglu":
                        if not first:
                            a.wait_ge(*s_gated(FPAIRS * t + p - 1))
                        a.activation(h_gate[:, p % 2, :], bank(p % 2), ACT.Silu).then_inc(s_act.sem, 1)
                        return
                    if not first:
                        a.wait_ge(*s_hsplit(FPAIRS * t + p - 1))
                    if kind == "gelu":
                        a.activation(h_raw[:, p % 2, :], bank(p), ACT.Gelu_apprx_tanh).then_inc(s_act.sem, 1)
                    else:
                        for q in range(2):
                            f = 2 * p + q
                            ins = a.activation(h_raw[:, p % 2, q * SLOTS:(q + 1) * SLOTS], bank(p)[:, q * SLOTS:(q + 1) * SLOTS],
                                               ACT.Relu, bias=b1_buf[:, u, f:f + 1])
                        ins.then_inc(s_act.sem, 1)

                def evict(t, u, it):
                    a.wait_ge(*s_mm2[u](it + 1))
                    a.wait_ge(*s_stored[u](16 * it))
                    a.copy(y_rows[:, u, :, :], bank(4 + u).rearrange("p (s d) -> p s d", s=SB)).then_inc(s_y[u].sem, 1)

                for t in range(2):
                    if t == 1 and lead:
                        for q in range(4):
                            high2(0, 0, 0, q)
                    for q in range(4):
                        for m in range(n_in):
                            high(m, t, t, 0, q)
                    if t == 1:
                        for p in range(FPAIRS):
                            activate(0, 0, 0, p)
                    high_x(t, t, 0)

                def step(t, u, it):
                    for q in range(4):
                        if exists(t + lead):
                            high2(t + lead, (1 - u) if lead else u, (it + u) if lead else it, q)
                        if exists(t + 1):
                            activate(t + 1, 1 - u, it + u, q)
                        if exists(t + 2):
                            for m in range(n_in):
                                high(m, t + 2, u, it + 1, q)
                    if exists(t + 2):
                        high_x(t + 2, u, it + 1)
                    evict(t, u, it)

                tiles(a, step)

            def vector(v):
                def low(m, t, u, it, q):
                    v.wait_ge(*s_hi[m](4 * t + q + 1))
                    part = slice(q * 512, (q + 1) * 512)
                    hi, lo = (z.rearrange("p c f -> p (c f)")[:, part] for z in in_parts[m][u])
                    ins = v.tensor_tensor(lo, raw[m][:, part], hi.bitcast(FP32), ALU.subtract)
                    if q == 3:
                        ins.then_inc(s_split[m].sem, 1)

                def low2(t, u, it, q):
                    v.wait_ge(*s_hi2(4 * t + q + 1))
                    part = slice(q * 512, (q + 1) * 512)
                    hi, lo = (z.rearrange("p c o -> p (c o)")[:, part] for z in out_parts[u * lead])
                    ins = v.tensor_tensor(lo, raw[2][:, part], hi.bitcast(FP32), ALU.subtract)
                    if q == 3:
                        ins.then_inc(s_split2.sem, 1)

                def low_x(t, u, it):
                    v.wait_ge(*s_xhi(t + 1))
                    v.tensor_tensor(x_part[u][1], bank(6).rearrange("p (c s) -> p c s", c=DC),
                                    x_part[u][0].bitcast(FP32), ALU.subtract).then_inc(s_xsplit.sem, 1)

                def high_h(t, u, it, p):
                    if p == 0:
                        v.wait_ge(*s_mm2[u](it))
                    v.wait_ge(*s_act(FPAIRS * t + p + 1))
                    hi, lo = (h_part[u][z][:, 2 * p:2 * p + 2, :].rearrange("p c s -> p (c s)") for z in range(2))
                    if kind == "swiglu":
                        if not isinstance(t, int) or t > 0 or p >= 2:
                            v.wait_ge(*s_hsplit(FPAIRS * t + p - 1))
                        v.tensor_tensor(h_raw[:, p % 2, :], h_gate[:, p % 2, :], bank(2 + p % 2), ALU.mult)\
                            .then_inc(s_gated.sem, 1)
                        v.wait_ge(*s_gated(FPAIRS * t + p + 1))
                    v.tensor_copy(hi, h_raw[:, p % 2, :]).then_inc(s_hhi.sem, 1)

                def low_h(t, u, it, p):
                    hi, lo = (h_part[u][z][:, 2 * p:2 * p + 2, :].rearrange("p c s -> p (c s)") for z in range(2))
                    v.wait_ge(*s_hhi(FPAIRS * t + p + 1))
                    v.tensor_tensor(lo, h_raw[:, p % 2, :], hi.bitcast(FP32), ALU.subtract).then_inc(s_hsplit.sem, 1)

                for t in range(2):
                    if t == 1 and lead:
                        for q in range(4):
                            low2(0, 0, 0, q)
                    for q in range(4):
                        for m in range(n_in):
                            low(m, t, t, 0, q)
                    if t == 1:
                        for p in range(FPAIRS):
                            high_h(0, 0, 0, p)
                            low_h(0, 0, 0, p)
                    low_x(t, t, 0)

                def step(t, u, it):
                    for q in range(4):
                        if exists(t + 1):
                            high_h(t + 1, 1 - u, it + u, q)
                        if exists(t + lead):
                            low2(t + lead, (1 - u) if lead else u, (it + u) if lead else it, q)
                        if exists(t + 1):
                            low_h(t + 1, 1 - u, it + u, q)
                        if exists(t + 2):
                            for m in range(n_in):
                                low(m, t + 2, u, it + 1, q)
                    if exists(t + 2):
                        low_x(t + 2, u, it + 1)

                tiles(v, step)
                for t in range(TILES):
                    for c in range(2):
                        n = 2 * t + c
                        if n % GROUP == 0:
                            v.wait_ge(*s_back[n // GROUP % GROUPS](16 * GROUP * (n // (GROUP * GROUPS) + 1)))
                        if c == 1:
                            v.wait_ge(*s_comb(n))
                        v.scalar_tensor_tensor(x[:, t, :], y_back[:, n % 16, :], best[:, c, t:t + 1], x[:, t, :],
                                               ALU.mult, ALU.add).then_inc(s_comb.sem, 1)
                v.wait_ge(*s_comb(2 * TILES))

            return Stage(sync, gpsimd, scalar, vector, tensor), s_comb(2 * TILES)

        def dense_experts(routed_w, shared_w, routed):
            n_w = E_ALL * DC * HID
            raw_w = [view(k * n_w, n_w) for k in range(3)]
            silu = view(7680, 2, SEQ)
            xnb = view(9216, TPB, D)
            h_mid = view(10240, 2, SEQ)
            part = [[w_parts[:, (2 * k + z) * n_w:(2 * k + z + 1) * n_w] for z in range(2)] for k in range(3)]
            w1p, w3p = ([z.rearrange("p (e c h) -> p e c h", e=E_ALL, c=DC) for z in part[k]] for k in range(2))
            w2p = [z.rearrange("p (e o) -> p e o", e=E_ALL) for z in part[2]]
            xp = [xT_parts[:, z * 1024:(z + 1) * 1024].rearrange("p (c s) -> p c s", c=DC) for z in range(2)]
            hp = [[h_parts[:, (2 * u + z) * SEQ:(2 * u + z + 1) * SEQ] for z in range(2)] for u in range(2)]
            N = B * E_ALL
            s_raw, s_high, s_low = signal("dense_weights", 16 * 6), signal("dense_w_high", 3), signal("dense_w_split", 3)
            s_blk, s_xT_ps, s_xhi, s_xlo = (signal("dense_block", B), signal("dense_xT_in_psum", B),
                                            signal("dense_x_high", 2 * B), signal("dense_x_split", 2 * B))
            s_hps, s_act, s_mid, s_hhi, s_hlo = (signal(f"dense_{k}", N) for k in
                                                 ("h_in_psum", "silu", "gated", "h_high", "h_split"))
            s_y, s_add = signal("dense_y", N), signal("dense_added", N * TPB)

            def sync(sp):
                sp.wait_ge(*routed)
                for k, (name, of) in enumerate(zip(("w1", "w3", "w2"), (P, P, HID))):
                    form = "e (c p) h -> p (e c) h" if k < 2 else "e p o -> p e o"
                    kw = {"p": P} if k < 2 else {}
                    last = HID if k < 2 else D
                    dst = raw_w[k].rearrange("p (n h) -> p n h", h=last)
                    cut = E * DC if k < 2 else E
                    sp.dma_start(dst[:, 0:cut, :], routed_w[k].rearrange(form, **kw)).then_inc(s_raw.sem, 16)
                    sp.dma_start(dst[:, cut:, :], shared_w[k].rearrange(form, **kw)).then_inc(s_raw.sem, 16)

            def gpsimd(g):
                pass

            def tensor(t):
                def product(o, a, b, first, last):
                    t.matmul(o, a[0], b[0], start=first, stop=False)
                    t.matmul(o, a[0], b[1], start=False, stop=False)
                    return t.matmul(o, a[1], b[0], start=False, stop=last)

                with t.Fori(0, B) as i:
                    t.wait_ge(*s_blk(i + 1))
                    t.wait_ge(*s_add(i * (E_ALL * TPB)))
                    for j in range(TPB):
                        for c in range(DC):
                            ins = t.transpose(bank(6 + c)[:, j * P:(j + 1) * P], xnb[:, j, c * P:(c + 1) * P], ident[:, :])
                    ins.then_inc(s_xT_ps.sem, 1)
                    t.wait_ge(*s_xlo(2 * i + 2))
                    t.wait_ge(*s_low(2))

                    def hidden(e):
                        if e >= 2:
                            t.wait_ge(*s_mid(i * E_ALL + e - 1))
                        for m, w in enumerate((w1p, w3p)):
                            for c in range(DC):
                                ins = product(bank(2 * (e % 2) + m), [z[:, e, c, :] for z in w],
                                              [z[:, c, :] for z in xp], c == 0, c == DC - 1)
                        ins.then_inc(s_hps.sem, 1)

                    hidden(0)
                    for e in range(E_ALL):
                        if e + 1 < E_ALL:
                            hidden(e + 1)
                        if e == 0:
                            t.wait_ge(*s_low(3))
                        t.wait_ge(*s_hlo(i * E_ALL + e + 1))
                        if e >= 2:
                            t.wait_ge(*s_add(TPB * (i * E_ALL + e - 1)))
                        for j in range(TPB):
                            o = bank(4 + 2 * (e % 2) + j // 2)[:, (j % 2) * D:(j % 2 + 1) * D]
                            ins = product(o, [z[:, j * P:(j + 1) * P] for z in hp[e % 2]], [z[:, e, :] for z in w2p], True, True)
                        ins.then_inc(s_y.sem, 1)

            def scalar(a):
                for k in range(3):
                    a.wait_ge(*s_raw(16 * 6))
                    a.copy(part[k][0], raw_w[k]).then_inc(s_high.sem, 1)
                with a.Fori(0, B) as i:
                    a.copy(xnb, xn[:, bass.ds(TPB * i, TPB), :]).then_inc(s_blk.sem, 1)
                    a.wait_ge(*s_xT_ps(i + 1))
                    for c in range(DC):
                        a.copy(xp[0][:, c, :], bank(6 + c)).then_inc(s_xhi.sem, 1)
                    for e in range(E_ALL):
                        a.wait_ge(*s_hps(i * E_ALL + e + 1))
                        if e >= 2:
                            a.wait_ge(*s_mid(i * E_ALL + e - 1))
                        a.activation(silu[:, e % 2, :], bank(2 * (e % 2)), ACT.Silu).then_inc(s_act.sem, 1)

            def vector(v):
                for k in range(3):
                    v.wait_ge(*s_high(k + 1))
                    v.tensor_tensor(part[k][1], raw_w[k], part[k][0].bitcast(FP32), ALU.subtract).then_inc(s_low.sem, 1)
                with v.Fori(0, B) as i:
                    for c in range(DC):
                        v.wait_ge(*s_xhi(2 * i + c + 1))
                        v.tensor_tensor(xp[1][:, c, :], bank(6 + c), xp[0][:, c, :].bitcast(FP32),
                                        ALU.subtract).then_inc(s_xlo.sem, 1)

                    def middle(e):
                        n = i * E_ALL + e
                        v.wait_ge(*s_act(n + 1))
                        if e >= 2:
                            v.wait_ge(*s_hlo(n - 1))
                        v.tensor_tensor(h_mid[:, e % 2, :], silu[:, e % 2, :], bank(2 * (e % 2) + 1), ALU.mult)\
                            .then_inc(s_mid.sem, 1)
                        v.wait_ge(*s_mid(n + 1))
                        v.tensor_copy(hp[e % 2][0], h_mid[:, e % 2, :]).then_inc(s_hhi.sem, 1)
                        v.wait_ge(*s_hhi(n + 1))
                        v.tensor_tensor(hp[e % 2][1], h_mid[:, e % 2, :], hp[e % 2][0].bitcast(FP32), ALU.subtract)\
                            .then_inc(s_hlo.sem, 1)

                    def add(e):
                        n = i * E_ALL + e
                        v.wait_ge(*s_y(n + 1))
                        for j in range(TPB):
                            if e:
                                v.wait_ge(*s_add(TPB * (n - 1) + j + 1))
                            v.scalar_tensor_tensor(tile_of(i, j),
                                                   bank(4 + 2 * (e % 2) + j // 2)[:, (j % 2) * D:(j % 2 + 1) * D],
                                                   gates[:, bass.ds(TPB * i + j, 1), e], tile_of(i, j),
                                                   ALU.mult, ALU.add).then_inc(s_add.sem, 1)

                    middle(0)
                    for e in range(E_ALL):
                        if e + 1 < E_ALL:
                            middle(e + 1)
                        add(e)
                v.wait_ge(*s_add(N * TPB))

            return Stage(sync, gpsimd, scalar, vector, tensor), s_add(N * TPB)

        def local_attention(x_before):
            wa = view(0, DC, D)
            wc = view(512, 2 * DC, D)
            ctx_rows = view(1536, B, D, parts=KEYS)
            keep, masked, gauss = (view(2560 + k * 256, B, KEYS) for k in range(3))
            xnb, xnT, qT = view(3328, TPB, D), view(4352, DC, SEQ), view(5376, DC, SEQ)
            align = view(6400, TPB, KEYS)
            alignT = view(6656, SEQ, parts=KEYS)
            contextT = view(7168, DC, SEQ)
            tanh = view(8192, 2, D)
            ctx_now = view(8704, D, parts=KEYS)
            centre, begin, finish, length = (view(8960 + k * B, B) for k in range(4))
            top, total, inverse = (view(8992 + k * TPB, TPB) for k in range(3))

            s_w = signal("local_weights", 16 * 5)
            s_ch = signal("local_chain", 0)
            s_dist, s_gauss = signal("local_distance", 1), signal("local_gauss", 1)
            s_now = signal("local_context_now", B)
            s_var, s_rstd, s_norm = signal("variance", B), signal("rstd", B), signal("local_normed", TILES)
            s_xT_ps, s_xT, s_q_ps, s_q = (signal(f"local_{k}", n * B) for k, n in
                                          (("xT_in_psum", 1), ("xT", 2), ("q_in_psum", 2), ("q", 2)))
            s_sc, s_less, s_exp, s_al = (signal(f"local_{k}", B) for k in ("scores", "shifted", "exp", "aligned"))
            s_aT_ps, s_aT, s_c_ps, s_c = (signal(f"local_{k}", B) for k in ("alignT_in_psum", "alignT", "context_in_psum", "context"))
            s_y, s_tanh, s_x = (signal(f"local_{k}", TILES) for k in ("y", "tanh", "x_updated"))

            def sync(sp):
                sp.wait_ge(*x_before)
                sp.dma_start(wa, io["L2_xcond_W_a"].rearrange("(c p) k -> p c k", p=P)).then_inc(s_w.sem, 16)
                sp.dma_start(wc, io["L2_xcond_W_c"].rearrange("(c p) o -> p c o", p=P)).then_inc(s_w.sem, 16)
                sp.dma_start(ctx_rows, io["ctx_1024"].rearrange("b k d -> k b d")).then_inc(s_w.sem, 16)
                sp.dma_start(centre, io["condB_pt"].to_broadcast([P, B])).then_inc(s_w.sem, 16)
                sp.dma_start(lens[:, :], io["_lenS2"].to_broadcast([P, B])).then_inc(s_w.sem, 16)

            def gpsimd(g):
                g.wait_ge(*s_w(16 * 5))
                with g.Fori(0, B) as i:
                    norm_gpsimd(g, i, s_var, s_rstd)
                    g.wait_ge(*s_c_ps(i))
                    g.tensor_copy(ctx_now, ctx_rows[:, bass.ds(i, 1), :].rearrange("p a d -> p (a d)"))\
                        .then_inc(s_now.sem, 1)

            def tensor(t):
                t.wait_ge(*s_w(16 * 5))
                with t.Fori(0, B) as i:
                    t.wait_ge(*s_tanh(TPB * i))
                    for j in range(TPB):
                        t.wait_ge(*s_norm(TPB * i + j + 1))
                        for c in range(DC):
                            ins = t.transpose(bank(c)[:, j * P:(j + 1) * P], xnb[:, j, c * P:(c + 1) * P], ident[:, :])
                    ins.then_inc(s_xT_ps.sem, 1)
                    t.wait_ge(*s_xT(2 * i + 2))
                    for oc in range(DC):
                        for kc in range(DC):
                            ins = t.matmul(bank(2 + oc), wa[:, kc, oc * P:(oc + 1) * P], xnT[:, kc, :],
                                           start=(kc == 0), stop=(kc == DC - 1))
                        ins.then_inc(s_q_ps.sem, 1)
                    t.wait_ge(*s_q(2 * i + 2))
                    for j in range(TPB):
                        for c in range(DC):
                            ins = t.matmul(bank(4)[:, j * KEYS:(j + 1) * KEYS], qT[:, c, j * P:(j + 1) * P],
                                           ctxT[:, c, bass.ds(i, 1), 0, :].rearrange("p a k -> p (a k)"),
                                           start=(c == 0), stop=(c == DC - 1))
                    ins.then_inc(s_sc.sem, 1)
                    t.wait_ge(*s_al(i + 1))
                    t.transpose(bank(5)[:, 0:P], align[:, 0:2, :].rearrange("p j k -> p (j k)"), ident[:, :])
                    for j in range(1, TPB):
                        ins = t.transpose(bank(5)[0:KEYS, j * P:(j + 1) * P], align[:, j, :], ident[:, :])
                    ins.then_inc(s_aT_ps.sem, 1)
                    t.wait_ge(*s_aT(i + 1))
                    t.wait_ge(*s_now(i + 1))
                    for c in range(DC):
                        ins = t.matmul(bank(6 + c), ctx_now[:, c * P:(c + 1) * P], alignT, start=True, stop=True)
                    ins.then_inc(s_c_ps.sem, 1)
                    t.wait_ge(*s_c(i + 1))
                    for j in range(TPB):
                        o = bank(j)[:, 0:D]
                        for c in range(2 * DC):
                            left = contextT if c < DC else xnT
                            ins = t.matmul(o, left[:, c % DC, j * P:(j + 1) * P], wc[:, c, :],
                                           start=(c == 0), stop=(c == 2 * DC - 1))
                        ins.then_inc(s_y.sem, 1)

            def scalar(a):
                a.wait_ge(*s_dist(1))
                a.activation(gauss, gauss, ACT.Exp, scale=-1.0 / DEV_POW).then_inc(s_gauss.sem, 1)
                with a.Fori(0, B) as i:
                    a.wait_ge(*s_xT_ps(i + 1))
                    for c in range(DC):
                        a.copy(xnT[:, c, :], bank(c)).then_inc(s_xT.sem, 1)
                    for c in range(DC):
                        a.wait_ge(*s_q_ps(2 * i + c + 1))
                        a.copy(qT[:, c, :], bank(2 + c)).then_inc(s_q.sem, 1)
                    a.wait_ge(*s_less(i + 1))
                    a.activation(align, align, ACT.Exp).then_inc(s_exp.sem, 1)
                    a.wait_ge(*s_aT_ps(i + 1))
                    a.copy(alignT, bank(5)[0:KEYS, :]).then_inc(s_aT.sem, 1)
                    a.wait_ge(*s_c_ps(i + 1))
                    a.copy(contextT, bank(6, 2).rearrange("p (c s) -> p c s", c=DC)).then_inc(s_c.sem, 1)
                    for j in range(TPB):
                        a.wait_ge(*s_y(TPB * i + j + 1))
                        if j >= 2:
                            a.wait_ge(*s_x(TPB * i + j - 1))
                        a.activation(tanh[:, j % 2, :], bank(j)[:, 0:D], ACT.Tanh)\
                            .then_inc(s_tanh.sem, 1)

            def vector(v):
                v.wait_ge(*s_w(16 * 5))
                pre = Chain(v, s_ch)
                pre.link(v.tensor_copy(length, lens[:, :]))
                pre.add(v.tensor_scalar(begin, centre, -WINDOW, 0.0, ALU.add, ALU.max))
                pre.link(v.tensor_scalar(finish, centre, WINDOW, None, ALU.add))
                pre.link(v.tensor_tensor(finish, finish, length, ALU.min))
                for b in range(B):
                    pre.add(v.tensor_scalar(keep[:, b, :], key_no[:, :], begin[:, b:b + 1], None, ALU.is_ge))
                    pre.add(v.tensor_scalar(gauss[:, b, :], key_no[:, :], centre[:, b:b + 1], None, ALU.subtract))
                pre.wait()
                for b in range(B):
                    pre.add(v.scalar_tensor_tensor(keep[:, b, :], key_no[:, :], finish[:, b:b + 1], keep[:, b, :],
                                                   ALU.is_le, ALU.mult))
                pre.wait()
                pre.link(v.tensor_scalar(masked, keep, -1.0, 1e9, ALU.add, ALU.mult))
                v.tensor_tensor(gauss, gauss, gauss, ALU.mult).then_inc(s_dist.sem, 1)
                v.wait_ge(*s_gauss(1))
                LINKS = 2 * TPB + 6
                with v.Fori(0, B) as i:
                    ch = Chain(v, s_ch, pre.n + i * LINKS)
                    norm_vector(v, ch, i, xnb, s_var, s_rstd, s_norm)
                    v.wait_ge(*s_sc(i + 1))

                    def of_batch(table):
                        return table[:, bass.ds(i, 1), :].to_broadcast([P, TPB, KEYS])

                    def of_row(row):
                        return row.unsqueeze(2).to_broadcast([P, TPB, KEYS])

                    ch.link(v.tensor_tensor(align, bank(4)[:, 0:TPB * KEYS].rearrange("p (j k) -> p j k", k=KEYS),
                                            of_batch(keep), ALU.mult))
                    ch.link(v.tensor_tensor(align, align, of_batch(masked), ALU.add))
                    ch.link(v.reduce_max(top, align, AX.X))
                    v.tensor_tensor(align, align, of_row(top), ALU.subtract).then_inc(s_less.sem, 1)
                    v.wait_ge(*s_exp(i + 1))
                    ch.link(v.reduce_sum(total, align, AX.X))
                    ch.link(v.reciprocal(inverse, total))
                    ch.link(v.tensor_tensor(align, align, of_row(inverse), ALU.mult))
                    v.tensor_tensor(align, align, of_batch(gauss), ALU.mult).then_inc(s_al.sem, 1)
                    for j in range(TPB):
                        v.wait_ge(*s_tanh(TPB * i + j + 1))
                        v.tensor_tensor(tile_of(i, j), tile_of(i, j), tanh[:, j % 2, :], ALU.add).then_inc(s_x.sem, 1)
                    assert ch.n == LINKS
                v.wait_ge(*s_x(TILES))

            return Stage(sync, gpsimd, scalar, vector, tensor), s_x(TILES)

        b1_buf = view(9216, 2, FC)
        b2_buf = view(9232, 2, D, parts=1)
        y_back = view(0, 16, D)
        lens = sb("lens", [P, B], I32)

        def layer_router(L):
            return {0: lambda: router(0, io["L0_ffn_gate_w"], None, x_done),
                    1: lambda: router(1, io["L1_ffn_router_w"], io["L1_ffn_router_b"], x_done),
                    2: lambda: router(2, io["L2_ffn_gate_w"], io["L2_ffn_gate_b"], x_done),
                    3: lambda: router(3, io["L3_ffn_router_gate"], None, x_done)}[L]

        def layer_experts(L):
            return {0: lambda: moe(0, "gelu", io["L0_ffn_w1"], io["L0_ffn_w2"], routed=x_done),
                    1: lambda: dense_experts([io[f"L1_ffn_routed_{k}"] for k in ("w1", "w3", "w2")],
                                             [io[f"L1_ffn_shared_{k}"] for k in ("w1", "w3", "w2")], x_done),
                    2: lambda: moe(2, "relu", io["L2_ffn_W1"], io["L2_ffn_W2"], b1=io["L2_ffn_b1"],
                                   b2=io["L2_ffn_b2"], routed=x_done),
                    3: lambda: moe(3, "swiglu", io["L3_ffn_gate_w"], io["L3_ffn_down_w"], w3=io["L3_ffn_up_w"],
                                   routed=x_done)}[L]

        plan = [start]
        x_done = None
        for L in range((stages + 1) // 2):
            parts = [(lambda: local_attention(x_done)) if L == 2 else (lambda: attention(L, x_done))]
            if 2 * L + 1 < stages:
                parts += [layer_router(L), layer_experts(L)]
            for make in parts:
                stage, x_done = make()
                plan.append(stage)

        s_out = signal("output", 16)

        def store(sp):
            sp.wait_ge(*x_done)
            sp.dma_start(out.rearrange("b (t p) d -> p (b t) d", p=P), x[:, :, :]).then_inc(s_out.sem, 16)
            sp.wait_ge(*s_out(16))

        block = ctx.enter_context(nc.Block())

        @block.sync
        def _(sp):
            for stage in plan:
                stage.sync(sp)
            store(sp)

        @block.gpsimd
        def _(g):
            for stage in plan:
                stage.gpsimd(g)

        @block.scalar
        def _(a):
            for stage in plan:
                stage.scalar(a)

        @block.vector
        def _(v):
            for stage in plan:
                stage.vector(v)

        @block.tensor
        def _(t):
            for stage in plan:
                stage.tensor(t)


_TRANSPOSED = [f"L{l}_xcond_W{k}" for l in (0, 1, 3) for k in "qkvo"] + ["L2_xcond_W_c", "L2_ffn_gate_w"]


def kernel(**inputs):
    import concourse.bacc as _bacc
    from concourse.bass_utils import run_bass_kernel_spmd as _run

    nc = _bacc.Bacc("TRN2", target_bir_lowering=False, num_devices=1)
    laid = {k: np.asarray(v) for k, v in inputs.items()}
    for k in _TRANSPOSED:
        laid[k] = laid[k].T
    laid["ctxT"] = laid["ctx_1024"].reshape(B * KEYS, D).T
    laid["condB_tau"] = laid["condB_tau"].reshape(1, B)
    laid["condB_pt"] = laid["condB_pt"].reshape(1, B)
    laid["_lenS2"] = laid["_lenS2"].reshape(1, B)
    laid["L2_ffn_b1"] = laid["L2_ffn_b1"].reshape(E, FC, P).transpose(0, 2, 1)
    arrays, io = {}, {}
    for name, a in laid.items():
        a = np.ascontiguousarray(a)
        arrays[f"in_{name}"] = a
        io[name] = nc.dram_tensor(f"in_{name}", a.shape, mybir.dt.from_np(a.dtype), kind="ExternalInput").ap()
    out = nc.dram_tensor("out_x", (B, SEQ, D), FP32, kind="ExternalOutput").ap()
    build(nc, io, out)
    r = _run(nc, [arrays], core_ids=[0])
    return r.results[0]["out_x"]
```

```python
import math
from contextlib import ExitStack

import numpy as np

import concourse.bass as bass
from concourse import mybir

FP32 = mybir.dt.float32
FP32R = mybir.dt.float32r
BF16 = mybir.dt.bfloat16
I32 = mybir.dt.int32
ALU = mybir.AluOpType
ACT = mybir.ActivationFunctionType
AX = mybir.AxisListType

P = 128
B, SEQ, D = 4, 512, 256
T = B * SEQ
TILES = T // P
TPB = SEQ // P
DC = D // P
HEADS, DK = 16, 16
HPC = HEADS // DC
PAIRS = HEADS // 2
KEYS = 64
VW = 2 * DK + 2
E = 8
F = 1024
FC = F // P
FPAIRS = FC // 2
HID = 128
SHARED = 2
E_ALL = E + SHARED
SLOTS = 256
SB = SLOTS // P
KMAX = T // SLOTS
NT = (2 * T + E * (SLOTS - 1)) // SLOTS
CAP = math.ceil(1.25 * T * 2 / E)
CAP3 = int(1.25 * ((T * 2 + E - 1) // E))
EPS = 1e-5
WINDOW, DEV_POW = 16.0, 128.0
BANK = 512
LOWEST = -3.0e38
ARENA = 15360


class Signal:

    def __init__(self, semaphore, base):
        self.sem, self.base = semaphore, base

    def __call__(self, n):
        return self.sem, self.base + n


class Chain:

    def __init__(self, eng, sig, base=0):
        self.eng, self.sig, self.base, self.n = eng, sig, base, 0

    def add(self, ins):
        self.n += 1
        ins.then_inc(self.sig.sem, 1)

    def wait(self):
        self.eng.wait_ge(*self.sig(self.base + self.n))

    def link(self, ins):
        self.add(ins)
        self.wait()


class Stage:

    def __init__(self, sync, gpsimd, scalar, vector, tensor):
        self.sync, self.gpsimd, self.scalar, self.vector, self.tensor = sync, gpsimd, scalar, vector, tensor


def build(nc, io, out, stages=8):
    with ExitStack() as ctx:
        def sb(name, shape, dt=FP32):
            return ctx.enter_context(nc.sbuf_tensor(name, shape, dt))

        sems, begins = {}, {}

        def signal(name, total, first=1):
            if name not in sems:
                sems[name] = [ctx.enter_context(nc.semaphore(name)), first]
                begins[name] = first
            entry = sems[name]
            entry[1] += total
            return Signal(entry[0], entry[1] - total)

        x = sb("x", [P, TILES, D])
        ident = sb("ident", [P, P])
        ones_row = sb("ones_row", [1, P])
        before = sb("before", [P, P], BF16)
        ones_bf = sb("ones_bf", [P, P], BF16)
        head_of = sb("head_of", [P, HPC])
        rank_of = sb("rank_of", [P, E])
        key_no = sb("key_no", [P, KEYS])
        tile_no = sb("tile_no", [P, NT])
        step_no = sb("step_no", [P, KMAX])
        neg_half = sb("neg_half", [P, TPB])
        ctxT = sb("ctxT", [P, DC, B, 2, KEYS])
        tau_q = sb("tau_q", [P, B])
        delta_q = sb("delta_q", [33, B, KEYS])
        zeros = sb("zeros", [P, D])
        small = sb("small", [P, 16])
        stats = sb("stats", [P, TPB, 6])
        moments = sb("moments", [P, TPB, 2])
        var_eps = sb("var_eps", [P, TPB])
        rstd = sb("rstd", [P, TPB])
        scrap = sb("scrap", [P, 1])

        with ExitStack() as shared:
            def at_sb(name, shape, dt=FP32):
                return shared.enter_context(nc.sbuf_tensor(name, shape, dt))

            def both(name, *shape):
                names = "abcd"[:len(shape)]
                t = at_sb(name, [P, 2, int(np.prod(shape))], FP32R)
                if len(shape) == 1:
                    return [t[:, z, :] for z in range(2)]
                return [t[:, z, :].rearrange(f"p ({' '.join(names)}) -> p {' '.join(names)}",
                                             **dict(zip(names[1:], shape[1:]))) for z in range(2)]

            kbd = both("kbd", DC, B, HPC * KEYS)
            vbd = both("vbd", PAIRS * P)
            wp = [both(f"w{k}", DC, D) for k in "kvqo"]
            ctxp = both("ctx_parts", DC, B, 2, KEYS)
            pT = [both(f"probsT{k}", PAIRS, 2 * P) for k in range(2)]
            qT = [both(f"qT{k}", DC, 2 * P) for k in range(2)]
            xnT, hT = (both(k, DC, 2 * P) for k in ("xnT", "headsT"))
            vp = both("values", B, D)
            rows = at_sb("rows", [33, 4 * D], FP32R)
            ones33 = at_sb("ones33", [33, 2 * P], FP32R)
            rows_raw = at_sb("rows_raw", [33, 3 * D])
            w_raw_t = at_sb("w_raw", [P, 4, DC, D])
            w_raw = [w_raw_t[:, n] for n in range(4)]
            zero_one = at_sb("zero_one", [P, 2, 256])
            kt_t, kt_low_t = at_sb("kt", [P, DC, B * KEYS]), at_sb("kt_low", [P, DC, B * KEYS])
            kt_high_t = at_sb("kt_high", [P, DC, B * KEYS], FP32R)
            kt, kt_low, kt_high = kt_t[:, :, :], kt_low_t[:, :, :], kt_high_t[:, :, :]
            probs_t, top_t = at_sb("probs", [P, 2, HEADS * KEYS]), at_sb("top", [P, 2, HEADS])
            probs, top = ([z[:, n, :] for n in range(2)] for z in (probs_t, top_t))
            xnb_t = at_sb("xnb", [P, 2, 2, D])
            xnb = [xnb_t[:, n] for n in range(2)]
            total_t, inverse_t = at_sb("sums", [P, 2, HEADS]), at_sb("inverse", [P, 2, HEADS])
            total, inverse = ([z[:, n, :] for n in range(2)] for z in (total_t, inverse_t))

        arena = sb("arena", [P, ARENA])

        def view(at, *shape, parts=P):
            n = int(np.prod(shape))
            v = arena[0:parts, at:at + n]
            if len(shape) == 1:
                return v
            names = "abcd"[:len(shape)]
            return v.rearrange(f"p ({' '.join(names)}) -> p {' '.join(names)}",
                               **dict(zip(names[1:], shape[1:])))

        w_parts = sb("w_parts", [P, 20480], FP32R)
        h_parts = sb("h_parts", [P, 8192], FP32R)
        xT_parts = sb("xT_parts", [P, 2048], FP32R)

        psum = ctx.enter_context(nc.psum_tensor("psum", [P, 8 * BANK], FP32))

        def bank(b, n=1):
            return psum[:, b * BANK:(b + n) * BANK]

        xs = nc.dram_tensor("xs_scratch", (NT * SLOTS, D), FP32).ap()
        ys = nc.dram_tensor("ys_scratch", (NT * SLOTS, D), FP32).ap()

        IN_DMAS = 3 + 2 * DC
        ROWS = P * 8
        zero_dmas = -(-NT * SLOTS // ROWS)
        s_in, s_x_in = signal("shared_inputs", 16 * IN_DMAS), signal("x_input", 16)
        s_memset, s_const = signal("memset", 9), signal("constants", 8)
        s_scaled, s_zeroed = signal("scaled_inputs", 2), signal("slots_zeroed", 16 * zero_dmas)

        def sync(sp):
            for c in range(DC):
                for twice in range(2):
                    sp.dma_start(ctxT[:, c, :, twice, :], io["ctxT"][c * P:(c + 1) * P, :].rearrange("p (b k) -> p b k", b=B))\
                        .then_inc(s_in.sem, 16)
            sp.dma_start(tau_q[:, :], io["condB_tau"].to_broadcast([P, B])).then_inc(s_in.sem, 16)
            sp.wait_ge(*s_memset(9))
            for row in (0, 32):
                sp.dma_start(delta_q[row:row + 1, :, :], io["fside_BxS2_0"].rearrange("(o b) k -> o b k", o=1))\
                    .then_inc(s_in.sem, 16)

        def load_x_and_clear_slots(sp):
            sp.dma_start(x[:, :, :], io["x"].rearrange("b (t p) d -> p (b t) d", p=P)).then_inc(s_x_in.sem, 16)
            for n in range(zero_dmas):
                rows = min(ROWS, NT * SLOTS - n * ROWS)
                sp.dma_start(xs[n * ROWS:n * ROWS + rows, :].rearrange("(p r) d -> p r d", p=P),
                             zeros[:, :].unsqueeze(1).to_broadcast([P, rows // P, D])).then_inc(s_zeroed.sem, 16)

        def gpsimd(g):
            for name, (semaphore, _) in sems.items():
                if begins[name]:
                    g.sem_inc(semaphore, begins[name])
            g.memset(delta_q[:, :, :], 0.0).then_inc(s_memset.sem, 1)
            g.memset(ident[:, :], 0.0).then_inc(s_memset.sem, 1)
            g.memset(before[:, :], 1.0).then_inc(s_memset.sem, 1)
            g.memset(head_of[:, :], 1.0).then_inc(s_memset.sem, 1)
            g.memset(ones_row[:, :], 1.0).then_inc(s_memset.sem, 1)
            g.memset(ones_bf[:, :], 1.0).then_inc(s_memset.sem, 1)
            g.memset(neg_half[:, :], -0.5).then_inc(s_memset.sem, 1)
            g.memset(small[:, :], 0.0).then_inc(s_memset.sem, 1)
            g.memset(zeros[:, :], 0.0).then_inc(s_memset.sem, 1)
            g.wait_ge(*s_memset(9))
            g.affine_select(out=ident[:, :], in_=ident[:, :], compare_op=ALU.not_equal, fill=1.0,
                            base=0, pattern=[[-1, P]], channel_multiplier=1).then_inc(s_const.sem, 1)
            g.affine_select(out=before[:, :], in_=before[:, :], compare_op=ALU.is_gt, fill=0.0,
                            base=0, pattern=[[1, P]], channel_multiplier=-1).then_inc(s_const.sem, 1)
            g.affine_select(out=head_of[:, :], in_=head_of[:, :], compare_op=ALU.is_ge, fill=0.0,
                            base=0, pattern=[[-DK, HPC]], channel_multiplier=1).then_inc(s_const.sem, 1)
            g.wait_ge(*s_const(3))
            g.affine_select(out=head_of[:, :], in_=head_of[:, :], compare_op=ALU.is_ge, fill=0.0,
                            base=DK - 1, pattern=[[DK, HPC]], channel_multiplier=-1).then_inc(s_const.sem, 1)
            for t, pattern, base in ((rank_of, [[-1, E]], E), (key_no, [[1, KEYS]], 0),
                                     (tile_no, [[1, NT]], 0), (step_no, [[SLOTS, KMAX]], 0)):
                g.iota(t[:, :], pattern=pattern, base=base, channel_multiplier=0,
                       allow_small_or_imprecise_dtypes=True).then_inc(s_const.sem, 1)

        def vector(v):
            v.wait_ge(*s_in(IN_DMAS * 16))
            v.tensor_scalar(tau_q[:, :], tau_q[:, :], 1.0 / math.sqrt(DK), None, ALU.mult).then_inc(s_scaled.sem, 1)
            v.tensor_scalar(delta_q[:, :, :], delta_q[:, :, :], 1.0 / math.sqrt(DK), None, ALU.mult).then_inc(s_scaled.sem, 1)
            v.wait_ge(*s_scaled(2))
            v.wait_ge(*s_const(8))

        def tensor(t):
            t.wait_ge(*s_in(IN_DMAS * 16))
            t.wait_ge(*s_const(8))
            t.wait_ge(*s_scaled(2))

        def scalar(a):
            a.wait_ge(*s_in(IN_DMAS * 16))
            a.wait_ge(*s_scaled(2))
            a.wait_ge(*s_const(8))

        def nothing(eng):
            pass

        start = Stage(sync, gpsimd, scalar, vector, tensor)
        load_x = Stage(load_x_and_clear_slots, nothing, nothing, nothing, nothing)

        def norm_vector(v, ch, i, dst, s_var, s_rstd, s_norm):
            for j in range(TPB):
                ch.add(v.bn_stats(stats[:, j, :], tile_of(i, j)))
            ch.wait()
            v.memset(scrap[:, :], 0.0)
            for j in range(TPB):
                ch.add(v.bn_aggr(moments[:, j, :], stats[:, j, :]))
            ch.wait()
            v.tensor_scalar(var_eps[:, :], moments[:, :, 1], EPS, None, ALU.add).then_inc(s_var.sem, 1)
            v.wait_ge(*s_rstd(i + 1))
            for j in range(TPB):
                v.tensor_scalar(dst[:, j, :], tile_of(i, j), moments[:, j, 0:1], rstd[:, j:j + 1],
                                ALU.subtract, ALU.mult).then_inc(s_norm.sem, 1)

        def tile_of(i, j):
            return x[:, bass.ds(i * TPB + j, 1), :].rearrange("p a d -> p (a d)")

        def norm_gpsimd(g, i, s_var, s_rstd):
            g.wait_ge(*s_var(i + 1))
            g.tensor_tensor(rstd[:, :], var_eps[:, :], neg_half[:, :], ALU.pow).then_inc(s_rstd.sem, 1)

        UNIT = 2 * P
        UNITS = T // UNIT

        def attention(L, x_before, x_here=None):
            LINKS = 4 + 2
            io_w = {k: io[f"L{L}_xcond_W{k}"] for k in "kvqo"}

            s_w = signal("attn_weights", 11 * 16)
            s_rows0 = signal("attn_rows_cleared", 1)
            s_high = signal("attn_high_parts", 6 + 2)
            s_low = signal("attn_split", 6 + 2)
            s_rows = signal("attn_delta_row", 2)
            s_clear = signal("attn_values_cleared", 5)
            s_k_ps, s_v_ps = signal("attn_keys_in_psum", 1), signal("attn_values_in_psum", 1)
            s_kt, s_kbd = signal("attn_keys_scaled", DC), signal("attn_keys_spread", 2 * DC)
            s_kbd_later = signal("attn_keys_spread_later", 2 * DC * (B - 1))
            s_vbd = signal("attn_values_spread", 16 * B)
            s_ch = signal("attn_dve_chain", LINKS * UNITS)
            s_var, s_rstd, s_norm = signal("attn_variance", UNITS), signal("attn_rstd", UNITS), signal("attn_normed", TILES)
            s_xT_ps, s_xhi, s_xT = (signal(f"attn_xT_{k}", UNITS) for k in ("in_psum", "high", "split"))
            s_q_ps, s_qhi, s_q = (signal(f"attn_q_{k}", UNITS) for k in ("in_psum", "high", "split"))
            s_sc, s_sub, s_exp = signal("attn_scores", TILES), signal("attn_shifted", TILES), signal("attn_exp", TILES)
            s_pT_ps, s_phi, s_pT = (signal(f"attn_pT_{k}", 2 * TILES) for k in ("in_psum", "high", "split"))
            s_sum, s_inv = signal("attn_sums", TILES), signal("attn_inverse_sums", TILES)
            s_prob = signal("attn_probs", TILES)
            s_pv = signal("attn_pv", UNITS)
            s_hhi, s_hT = signal("attn_heads_high", UNITS), signal("attn_heads_split", UNITS)
            s_y, s_x = signal("attn_y", UNITS), signal("attn_x_updated", TILES)

            def pipeline(eng, step):
                for i in (-1, 0):
                    for k in range(2):
                        step(i, k)
                with eng.Fori(1, B - 1) as i:
                    for k in range(2):
                        step(i, k)
                for i in (B - 1, B):
                    for k in range(2):
                        step(i, k)

            def has(u):
                return not isinstance(u, int) or 0 <= u < UNITS

            def first(i):
                return isinstance(i, int) and i == -1

            def none_if_first(n):
                return max(n, 0) if isinstance(n, int) else n

            def x_tile(n):
                return x[:, bass.ds(n, 1), :].rearrange("p a d -> p (a d)")

            def sync(sp):
                if x_before is not None:
                    sp.wait_ge(*x_before)
                for n, k in enumerate("kvqo"):
                    sp.dma_start(w_raw[n], io_w[k].rearrange("(c p) o -> p c o", p=P)).then_inc(s_w.sem, 16)
                sp.dma_start(small[:, 0:DC], io[f"L{L}_xcond_bk"].rearrange("(c p) -> p c", p=P),
                             allow_slow_non_contiguous=True).then_inc(s_w.sem, 16)
                sp.wait_ge(*s_rows0(1))
                for at in (0, 32):
                    for n, k in enumerate("qvo"):
                        sp.dma_start(rows_raw[at:at + 1, n * D:(n + 1) * D],
                                     io[f"L{L}_xcond_b{k}"].rearrange("(o d) -> o d", o=1)).then_inc(s_w.sem, 16)

            def gpsimd(g):
                if x_before is not None:
                    g.wait_ge(*x_before)
                g.memset(rows_raw[:, :], 0.0).then_inc(s_rows0.sem, 1)
                g.memset(zero_one[:, 0, :], 0.0).then_inc(s_clear.sem, 1)
                g.memset(zero_one[:, 1, :], 1.0).then_inc(s_clear.sem, 1)

                def step(i, k):
                    s = 2 * i + k - 1
                    if has(s):
                        normalise(s, 1)
                    if has(s + 3):
                        u = s + 3
                        g.wait_ge(*s_var(u + 1))
                        g.tensor_tensor(rstd[:, 0:2], var_eps[:, 0:2], neg_half[:, 0:2], ALU.pow).then_inc(s_rstd.sem, 1)
                    if first(i) and k == 1:
                        g.wait_ge(*s_low(7))
                        later_keys(1)
                    if has(s + 1):
                        normalise(s + 1, 0)
                    if isinstance(i, int) and i == 0 and k == 1:
                        for b in range(2, B):
                            later_keys(b)

                def later_keys(b):
                    for z in range(2):
                        for c in range(DC):
                            spread_keys(g, z, c, b).then_inc(s_kbd_later.sem, 1)

                def normalise(u, n):
                    tile = 2 * u + n
                    p = probs[n].rearrange("p (h k) -> p h k", k=KEYS)
                    g.wait_ge(*s_inv(tile + 1))
                    g.tensor_tensor(p, p, inverse[n].unsqueeze(2).to_broadcast([P, HEADS, KEYS]), ALU.mult)\
                        .then_inc(s_prob.sem, 1)

                pipeline(g, step)

            def spread_keys(eng, z, c, b):
                return eng.tensor_tensor(kbd[z][:, c, b, :].rearrange("p (h k) -> p h k", h=HPC),
                                         (kt_high, kt_low)[z].bitcast(FP32)[:, c, b * KEYS:(b + 1) * KEYS]
                                         .unsqueeze(1).to_broadcast([P, HPC, KEYS]),
                                         head_of[:, :].unsqueeze(2).to_broadcast([P, HPC, KEYS]), ALU.mult)

            PASSES = ((0, 0), (0, 1), (1, 0))

            def tensor(t_eng):
                t = t_eng
                t.wait_ge(*s_clear(3))
                t.wait_ge(*s_low(4))
                for oc in range(DC):
                    for kc in range(DC):
                        for a, b in PASSES:
                            ins = t.matmul(bank(0)[:, oc * 256:(oc + 1) * 256], wp[0][a][:, kc, oc * P:(oc + 1) * P],
                                           ctxp[b][:, kc, :, 0, :], start=(kc == 0 and (a, b) == (0, 0)),
                                           stop=(kc == DC - 1 and (a, b) == (1, 0)))
                ins.then_inc(s_k_ps.sem, 1)
                for b in range(B):
                    o = bank(2 + b // 2)[:, (b % 2) * 256:(b % 2 + 1) * 256]
                    for kc in range(DC):
                        for za, zb in PASSES:
                            t.matmul(o, ctxp[za][:, kc, b, :, :].rearrange("p two k -> p (two k)"), wp[1][zb][:, kc, :],
                                     start=(kc == 0 and (za, zb) == (0, 0)), stop=False)
                    ins = t.matmul(o, ones33[:, 0:P], rows[:, 2 * D:3 * D], start=False, stop=True)
                ins.then_inc(s_v_ps.sem, 1)

                def scores(i, k, n):
                    u, b = 2 * i + k, i
                    if n == 0:
                        t.wait_ge(*s_q(u + 1))
                        if k == 0:
                            if isinstance(i, int) and i == 0:
                                t.wait_ge(*s_kbd(2 * DC))
                            else:
                                t.wait_ge(*s_kbd_later(2 * DC * b))
                    t.wait_ge(*s_sub(2 * u + n))
                    for c in range(DC):
                        for za, zb in PASSES:
                            t.matmul(bank(c), qT[k % 2][za][:, c, n * P:(n + 1) * P],
                                     kbd[zb][:, c, bass.ds(b, 1), :].rearrange("p a n -> p (a n)"),
                                     start=(za, zb) == (0, 0), stop=False)
                        ins = t.matmul(bank(c), ones33[:, 0:P],
                                       rows[:, 0:D].rearrange("p (b k) -> p b k", b=B)[:, bass.ds(b, 1), :]
                                       .to_broadcast([33, HPC, KEYS]), start=False, stop=True)
                    ins.then_inc(s_sc.sem, 1)

                def transpose_probs(s, n):
                    tile = 2 * s + n
                    t.wait_ge(*s_prob(tile + 1))
                    for h in range(2):
                        t.wait_ge(*s_pT(none_if_first(2 * tile + h - 1)))
                        for c in range(4):
                            ins = t.transpose(bank(2 + h)[:, c * P:(c + 1) * P],
                                              probs[n][:, (4 * h + c) * P:(4 * h + c + 1) * P], ident[:, :])
                        ins.then_inc(s_pT_ps.sem, 1)

                def step(i, k):
                    s = 2 * i + k - 1
                    if has(s):
                        transpose_probs(s, 0)
                    if has(s - 1):
                        u = s - 1
                        t.wait_ge(*s_pT(4 * u + 4))
                        t.wait_ge(*s_vbd(16 * i))
                        t.wait_ge(*s_hT(u))
                        for c in range(DC):
                            o = bank(4)[:, c * UNIT:(c + 1) * UNIT]
                            for j in range(4):
                                for za, zb in PASSES:
                                    ins = t.matmul(o, vbd[za][:, (4 * c + j) * P:(4 * c + j + 1) * P],
                                                   pT[k % 2][zb][:, 4 * c + j, :],
                                                   start=(j == 0 and (za, zb) == (0, 0)), stop=(j == 3 and (za, zb) == (1, 0)))
                        ins.then_inc(s_pv.sem, 1)
                    if has(s + 1):
                        scores(i, k, 0)
                    if has(s + 2):
                        u = s + 2
                        if first(i) and k == 1:
                            t.wait_ge(*s_low(6))
                        t.wait_ge(*s_xT(u + 1))
                        t.wait_ge(*s_q(u))
                        for oc in range(DC):
                            o = bank(5)[:, oc * UNIT:(oc + 1) * UNIT]
                            for kc in range(DC):
                                for za, zb in PASSES:
                                    t.matmul(o, wp[2][za][:, kc, oc * P:(oc + 1) * P], xnT[zb][:, kc, :],
                                             start=(kc == 0 and (za, zb) == (0, 0)), stop=False)
                            ins = t.matmul(o, rows[:, D + oc * P:D + (oc + 1) * P], ones33[:, :], start=False, stop=True)
                        ins.then_inc(s_q_ps.sem, 1)
                    if has(s):
                        transpose_probs(s, 1)
                    if has(s + 1):
                        scores(i, k, 1)
                    if has(s + 3):
                        u = s + 3
                        t.wait_ge(*s_norm(2 * u + 2))
                        t.wait_ge(*s_xT(u))
                        for n in range(2):
                            for c in range(DC):
                                ins = t.transpose(bank(6)[:, c * UNIT + n * P:c * UNIT + (n + 1) * P],
                                                  xnb[k % 2][:, n, c * P:(c + 1) * P], ident[:, :])
                        ins.then_inc(s_xT_ps.sem, 1)
                    if has(s - 1):
                        u = s - 1
                        t.wait_ge(*s_hT(u + 1))
                        t.wait_ge(*s_x(2 * u))
                        for n in range(2):
                            o = bank(7)[:, n * D:(n + 1) * D]
                            for c in range(DC):
                                for za, zb in PASSES:
                                    t.matmul(o, hT[za][:, c, n * P:(n + 1) * P], wp[3][zb][:, c, :],
                                             start=(c == 0 and (za, zb) == (0, 0)), stop=False)
                            ins = t.matmul(o, ones33[:, 0:P], rows[:, 3 * D:4 * D], start=False, stop=True)
                        ins.then_inc(s_y.sem, 1)

                pipeline(t, step)

            def flat(z):
                return z.rearrange("p c n -> p (c n)")

            def scalar(a):
                if x_before is not None:
                    a.wait_ge(*x_before)
                a.copy(ctxp[0], ctxT[:, :, :, :, :]).then_inc(s_high.sem, 1)
                a.wait_ge(*s_clear(2))
                a.copy(ones33[:, :], zero_one[0:33, 1, :]).then_inc(s_clear.sem, 1)
                for z in range(2):
                    a.copy(vbd[z].rearrange("p (g n) -> p g n", g=4),
                           zero_one[:, 0, :].unsqueeze(1).to_broadcast([P, 4, 256])).then_inc(s_clear.sem, 1)
                a.wait_ge(*s_w(11 * 16))
                a.copy(rows[:, 0:D], delta_q[:, :, :].rearrange("p b k -> p (b k)")).then_inc(s_rows.sem, 1)
                a.copy(rows[:, D:4 * D], rows_raw[:, :]).then_inc(s_high.sem, 1)
                for n in range(4):
                    a.copy(wp[n][0], w_raw[n]).then_inc(s_high.sem, 1)
                a.wait_ge(*s_kt(DC))
                a.copy(kt_high, kt).then_inc(s_high.sem, 1)
                a.wait_ge(*s_v_ps(1))
                a.copy(vp[0], bank(2, 2).rearrange("p (b d) -> p b d", b=B)).then_inc(s_high.sem, 1)

                def spread_values(b):
                    for z in range(2):
                        of = vp[z][:, bass.ds(b, 1), :].rearrange("p a (c j two k) -> p (a c) j two k", c=DC, j=4, two=2)
                        to = vbd[z].rearrange("p (c j m) -> p c j m", c=DC, m=P)
                        for j in range(4):
                            for half in range(2):
                                keys, at = slice(64 * half, 64 * half + 64), (2 * j + half) * DK
                                a.copy(to[keys, :, j, at:at + DK], of[keys, :, j, half, :]).then_inc(s_vbd.sem, 1)

                def probs_high(s, k, n):
                    p, tile = (k - 1) % 2, 2 * s + n
                    if n == 0:
                        a.wait_ge(*s_pv(none_if_first(s - 1)))
                    for h in range(2):
                        a.wait_ge(*s_pT_ps(2 * tile + h + 1))
                        a.copy(pT[p][0][:, 4 * h:4 * h + 4, n * P:(n + 1) * P],
                               bank(2 + h).rearrange("p (c q) -> p c q", c=4)).then_inc(s_phi.sem, 1)

                def exp(u, n):
                    a.wait_ge(*s_sub(2 * u + n + 1))
                    a.activation(probs[n], probs[n], ACT.Exp).then_inc(s_exp.sem, 1)

                def step(i, k):
                    s = 2 * i + k - 1
                    if has(s):
                        probs_high(s, k, 0)
                    if has(s - 1):
                        u = s - 1
                        a.wait_ge(*s_pv(u + 1))
                        a.wait_ge(*s_y(u))
                        a.copy(flat(hT[0]), bank(4)).then_inc(s_hhi.sem, 1)
                    if k == 1 and has(s):
                        if has(s - 1):
                            a.wait_ge(*s_pv(s))
                        else:
                            a.wait_ge(*s_clear(5))
                            a.wait_ge(*s_high(8))
                            a.wait_ge(*s_low(8))
                        spread_values(i)
                    if has(s + 2):
                        u = s + 2
                        a.wait_ge(*s_q_ps(u + 1))
                        a.wait_ge(*s_sc(none_if_first(2 * u - 2)))
                        a.copy(flat(qT[(k - 1) % 2][0]), bank(5)).then_inc(s_qhi.sem, 1)
                    if has(s):
                        probs_high(s, k, 1)
                    if has(s + 1):
                        exp(s + 1, 0)
                    if has(s + 3):
                        u = s + 3
                        a.wait_ge(*s_xT_ps(u + 1))
                        a.wait_ge(*s_q_ps(u))
                        a.copy(flat(xnT[0]), bank(6)).then_inc(s_xhi.sem, 1)
                    if has(s + 1):
                        exp(s + 1, 1)

                pipeline(a, step)

            def vector(v):
                def low(dst, src, high):
                    return v.tensor_tensor(dst, src, high.bitcast(FP32), ALU.subtract)

                v.wait_ge(*s_high(1))
                low(ctxp[1], ctxT[:, :, :, :, :], ctxp[0]).then_inc(s_low.sem, 1)
                v.wait_ge(*s_high(2))
                low(rows[32:33, 0:D], delta_q[32:33, :, :].rearrange("p b k -> p (b k)"), rows[32:33, 0:D])\
                    .then_inc(s_rows.sem, 1)
                low(rows[32:33, D:4 * D], rows_raw[32:33, :], rows[32:33, D:4 * D]).then_inc(s_low.sem, 1)
                for n in range(4):
                    v.wait_ge(*s_high(n + 3))
                    low(wp[n][1], w_raw[n], wp[n][0]).then_inc(s_low.sem, 1)
                if x_here is not None:
                    v.wait_ge(*x_here)
                v.wait_ge(*s_k_ps(1))
                for oc in range(DC):
                    v.scalar_tensor_tensor(kt[:, oc, :].rearrange("p (b k) -> p b k", b=B),
                                           bank(0)[:, oc * 256:(oc + 1) * 256].rearrange("p (b k) -> p b k", b=B),
                                           small[:, oc:oc + 1], tau_q[:, :].unsqueeze(2).to_broadcast([P, B, KEYS]),
                                           ALU.add, ALU.mult).then_inc(s_kt.sem, 1)
                v.wait_ge(*s_high(7))
                low(kt_low, kt, kt_high).then_inc(s_low.sem, 1)
                v.wait_ge(*s_high(8))
                low(vp[1], bank(2, 2).rearrange("p (b d) -> p b d", b=B), vp[0]).then_inc(s_low.sem, 1)
                v.wait_ge(*s_low(7))

                def shift(s, k, n):
                    tile = 2 * (s + 1) + n
                    v.wait_ge(*s_sc(tile + 1))
                    sc = bank(0, 2).rearrange("p (h k) -> p h k", k=KEYS)
                    ch.link(v.reduce_max(top[n], sc, AX.X))
                    v.wait_ge(*s_pT_ps(none_if_first(2 * tile - 2)))
                    v.tensor_tensor(probs[n].rearrange("p (h k) -> p h k", k=KEYS), sc,
                                    top[n].unsqueeze(2).to_broadcast([P, HEADS, KEYS]), ALU.subtract)\
                        .then_inc(s_sub.sem, 1)

                def invert(u, n):
                    v.wait_ge(*s_exp(2 * u + n + 1))
                    v.reduce_sum(total[n], probs[n].rearrange("p (h k) -> p h k", k=KEYS), AX.X).then_inc(s_sum.sem, 1)
                    v.wait_ge(*s_sum(2 * u + n + 1))
                    v.reciprocal(inverse[n], total[n]).then_inc(s_inv.sem, 1)

                def probs_low(s, k, n):
                    p = (k - 1) % 2
                    for h in range(2):
                        v.wait_ge(*s_phi(2 * (2 * s + n) + h + 1))
                        low(pT[p][1][:, 4 * h:4 * h + 4, n * P:(n + 1) * P],
                            bank(2 + h).rearrange("p (c q) -> p c q", c=4),
                            pT[p][0][:, 4 * h:4 * h + 4, n * P:(n + 1) * P]).then_inc(s_pT.sem, 1)

                def step(i, k):
                    nonlocal ch
                    s = 2 * i + k - 1
                    ch = Chain(v, s_ch, chain_before(s))
                    if has(s):
                        invert(s, 1)
                    if has(s):
                        probs_low(s, k, 0)
                    if has(s + 3):
                        u = s + 3
                        for n in range(2):
                            ch.add(v.bn_stats(stats[:, n, :], x_tile(2 * u + n)))
                    if has(s - 1):
                        v.wait_ge(*s_hhi(s))
                        low(flat(hT[1]), bank(4), flat(hT[0])).then_inc(s_hT.sem, 1)
                    if has(s + 3):
                        u = s + 3
                        ch.wait()
                        v.wait_ge(*s_norm(2 * u))
                        v.memset(scrap[:, :], 0.0)
                        for n in range(2):
                            ch.add(v.bn_aggr(moments[:, n, :], stats[:, n, :]))
                        ch.wait()
                        v.tensor_scalar(var_eps[:, 0:2], moments[:, 0:2, 1], EPS, None, ALU.add).then_inc(s_var.sem, 1)
                    if has(s + 1):
                        shift(s, k, 0)
                    if has(s + 3):
                        u = s + 3
                        v.wait_ge(*s_rstd(u + 1))
                        v.wait_ge(*s_xT_ps(none_if_first(u - 1)))
                        for n in range(2):
                            v.tensor_scalar(xnb[k % 2][:, n, :], x_tile(2 * u + n), moments[:, n, 0:1], rstd[:, n:n + 1],
                                            ALU.subtract, ALU.mult).then_inc(s_norm.sem, 1)
                    if first(i) and k == 1:
                        v.wait_ge(*s_low(7))
                        for z in range(2):
                            for c in range(DC):
                                spread_keys(v, z, c, 0).then_inc(s_kbd.sem, 1)
                    if has(s):
                        probs_low(s, k, 1)
                    if has(s + 1):
                        invert(s + 1, 0)
                    if has(s + 2):
                        u = s + 2
                        v.wait_ge(*s_qhi(u + 1))
                        low(flat(qT[(k - 1) % 2][1]), bank(5), flat(qT[(k - 1) % 2][0])).then_inc(s_q.sem, 1)
                    if has(s + 1):
                        shift(s, k, 1)
                    if has(s + 3):
                        u = s + 3
                        v.wait_ge(*s_xhi(u + 1))
                        low(flat(xnT[1]), bank(6), flat(xnT[0])).then_inc(s_xT.sem, 1)
                    if has(s - 1):
                        u = s - 1
                        v.wait_ge(*s_y(u + 1))
                        for n in range(2):
                            v.tensor_tensor(x_tile(2 * u + n), x_tile(2 * u + n), bank(7)[:, n * D:(n + 1) * D],
                                            ALU.add).then_inc(s_x.sem, 1)

                def chain_before(s):
                    return 4 * upto(s + 3) + 2 * upto(s + 1)

                def upto(n):
                    return min(max(n, 0), UNITS) if isinstance(n, int) else n

                ch = None
                pipeline(v, step)
                v.wait_ge(*s_x(TILES))

            return Stage(sync, gpsimd, scalar, vector, tensor), s_x(TILES)

        raw = [view(k * 2048, 2048) for k in range(3)]
        x_rows = view(6144, 2, SB, D)
        y_rows = view(7168, 2, SB, D)
        h_raw = view(8192, 2, 2 * SLOTS)
        h_gate = view(9216, 2, 2 * SLOTS)
        work = [view(7168 + k * TILES * E, TILES, E) for k in range(16)]
        route_xn = view(9216, TPB, D)
        route_xT = view(10240, DC, SEQ)
        xn = view(11264, TILES, D)
        assert 11264 + TILES * D <= ARENA

        masks = sb("masks", [P, 2, TILES, E])
        masks_bf = sb("masks_bf", [P, 2, TILES, E], BF16)
        best = sb("best", [P, 2, TILES])
        gates = sb("gates", [P, TILES, E_ALL])
        slot_f = sb("slot_f", [P, 2, TILES])
        slot = sb("slot", [P, 2, TILES], I32)
        expert_f = sb("expert_f", [1, NT])
        expert = sb("expert", [1, NT], I32)
        counts = sb("counts", [P, 8, E])
        limit = sb("limit", [P, E], I32)
        tries = sb("tries", [P, 3, E], I32)
        tile_rows = [sb(f"tile_row{k}", [P, TILES]) for k in range(3)]
        router_w = sb("router_w", [P, DC, E])
        router_b = sb("router_b", [1, E])

        def router(L, weight, bias, x_before):
            SEARCH = 15 if L == 3 else 0
            LOOP_LINKS = 2 * TPB
            s_w = signal("route_weights", 16 * (2 if bias is not None else 1))
            s_ch = signal(f"route_chain{L}", 0)
            s_var, s_rstd, s_norm = signal("variance", B), signal("rstd", B), signal("route_normed", TILES)
            s_xT_ps, s_xT, s_xn = signal("route_xT_in_psum", B), signal("route_xT", 2 * B), signal("route_xn", B)
            s_lg_ps, s_lg = signal("route_logits_in_psum", B), signal("route_logits", B)
            s_less, s_exp = signal("route_shifted", 1), signal("route_exp", 1)
            rounds = {0: 1, 1: 0, 2: 1, 3: SEARCH + 2}[L]
            s_mask, s_count = signal("route_masks", rounds), signal("route_counts", rounds)
            s_slot = signal("route_slots", 1)

            def sync(sp):
                sp.wait_ge(*x_before)
                sp.dma_start(router_w[:, :, :], weight.rearrange("(c p) e -> p c e", p=P)).then_inc(s_w.sem, 16)
                if bias is not None:
                    sp.dma_start(router_b[:, :], bias.rearrange("(o e) -> o e", o=1)).then_inc(s_w.sem, 16)

            def gpsimd(g):
                with g.Fori(0, B) as i:
                    norm_gpsimd(g, i, s_var, s_rstd)

            def tensor(t):
                t.wait_ge(*s_w(16 * (2 if bias is not None else 1)))
                t.wait_ge(*x_before)
                with t.Fori(0, B) as i:
                    t.wait_ge(*s_lg(i))
                    for j in range(TPB):
                        t.wait_ge(*s_norm(TPB * i + j + 1))
                        for c in range(DC):
                            ins = t.transpose(bank(c)[:, j * P:(j + 1) * P], route_xn[:, j, c * P:(c + 1) * P], ident[:, :])
                    ins.then_inc(s_xT_ps.sem, 1)
                    t.wait_ge(*s_xT(2 * i + 2))
                    for j in range(TPB):
                        o = bank(2)[:, j * E:(j + 1) * E]
                        for c in range(DC):
                            ins = t.matmul(o, route_xT[:, c, j * P:(j + 1) * P], router_w[:, c, :], start=(c == 0),
                                           stop=(c == DC - 1 and bias is None))
                        if bias is not None:
                            ins = t.matmul(o, ones_row[:, :], router_b[:, :], start=False, stop=True)
                    ins.then_inc(s_lg_ps.sem, 1)
                if L == 1:
                    return
                for n in range(SEARCH):
                    t.wait_ge(*s_mask(n + 1))
                    t.matmul(bank(5)[:, 0:3 * E], ones_bf[:, :], masks_bf[:, 0, 0:3, :],
                             start=True, stop=True).then_inc(s_count.sem, 1)
                if SEARCH:
                    t.wait_ge(*s_mask(SEARCH + 1))
                    t.matmul(bank(3)[:, 0:256], before[:, :], masks_bf[:, :, :, :], start=True, stop=True)
                    t.matmul(bank(4)[:, 0:256], ones_bf[:, :], masks_bf[:, :, :, :],
                             start=True, stop=True).then_inc(s_count.sem, 1)
                t.wait_ge(*s_mask((SEARCH + 2) if SEARCH else 1))
                t.matmul(bank(3)[:, 0:256], before[:, :], masks_bf[:, :, :, :], start=True, stop=True)
                t.matmul(bank(4)[:, 0:256], ones_bf[:, :], masks_bf[:, :, :, :],
                         start=True, stop=True).then_inc(s_count.sem, 1)

            def scalar(a):
                with a.Fori(0, B) as i:
                    a.wait_ge(*s_norm(TPB * i + TPB))
                    a.copy(xn[:, bass.ds(TPB * i, TPB), :], route_xn).then_inc(s_xn.sem, 1)
                    a.wait_ge(*s_xT_ps(i + 1))
                    for c in range(DC):
                        a.copy(route_xT[:, c, :], bank(c)).then_inc(s_xT.sem, 1)
                a.wait_ge(*s_less(1))
                if L == 1:
                    a.activation(tile_rows[0][:, :], tile_rows[0][:, :], ACT.Exp).then_inc(s_exp.sem, 1)
                else:
                    a.activation(work[0], work[0], ACT.Exp).then_inc(s_exp.sem, 1)

            def per_tile(row):
                return row.unsqueeze(2).to_broadcast([P, TILES, E])

            def vector(v):
                with v.Fori(0, B) as i:
                    ch = Chain(v, s_ch, i * LOOP_LINKS)
                    v.wait_ge(*s_xn(i))
                    norm_vector(v, ch, i, route_xn, s_var, s_rstd, s_norm)
                    v.wait_ge(*s_lg_ps(i + 1))
                    v.tensor_copy(work[0][:, bass.ds(TPB * i, TPB), :],
                                  bank(2)[:, 0:TPB * E].rearrange("p (j e) -> p j e", e=E)).then_inc(s_lg.sem, 1)
                    assert ch.n == LOOP_LINKS
                ch = Chain(v, s_ch, B * LOOP_LINKS)
                v.wait_ge(*s_lg(B))
                values, hit, ranked, second = work[0], work[1], work[2], work[3]
                top_row, rank_row, sum_row = (r[:, :] for r in tile_rows)
                if L != 1:
                    ch.link(v.reduce_max(top_row, values, AX.X))
                    v.tensor_tensor(values, values, per_tile(top_row), ALU.subtract).then_inc(s_less.sem, 1)
                    v.wait_ge(*s_exp(1))
                    ch.link(v.reduce_sum(sum_row, values, AX.X))
                    ch.link(v.reciprocal(rank_row, sum_row))
                    ch.link(v.tensor_tensor(values, values, per_tile(rank_row), ALU.mult))
                for c in range(2):
                    source = values if c == 0 else second
                    ch.link(v.reduce_max(best[:, c, :], source, AX.X))
                    ch.link(v.tensor_tensor(hit, source, per_tile(best[:, c, :]), ALU.is_equal))
                    ch.link(v.tensor_tensor(ranked, hit, rank_of[:, :].unsqueeze(1).to_broadcast([P, TILES, E]), ALU.mult))
                    ch.link(v.reduce_max(rank_row, ranked, AX.X))
                    ch.link(v.tensor_tensor(masks[:, c, :, :], ranked, per_tile(rank_row), ALU.is_equal))
                    if c == 0:
                        ch.link(v.scalar_tensor_tensor(second, masks[:, 0, :, :], LOWEST, values, ALU.mult, ALU.add))
                if L in (0, 3):
                    ch.link(v.tensor_tensor(sum_row, best[:, 0, :], best[:, 1, :], ALU.add))
                    if L == 3:
                        ch.link(v.tensor_scalar(sum_row, sum_row, 1e-9, None, ALU.add))
                    ch.link(v.reciprocal(rank_row, sum_row))
                    ch.link(v.tensor_tensor(best[:, :, :], best[:, :, :],
                                            rank_row.unsqueeze(1).to_broadcast([P, 2, TILES]), ALU.mult))
                if L == 1:
                    v.tensor_tensor(top_row, best[:, 1, :], best[:, 0, :], ALU.subtract).then_inc(s_less.sem, 1)
                    v.wait_ge(*s_exp(1))
                    ch.link(v.tensor_scalar(sum_row, top_row, 1.0, None, ALU.add))
                    ch.link(v.reciprocal(best[:, 0, :], sum_row))
                    ch.link(v.tensor_tensor(best[:, 1, :], best[:, 0, :], top_row, ALU.mult))
                if L in (1, 3):
                    for c in range(2):
                        ch.link(v.tensor_tensor(work[4 + c], masks[:, c, :, :], per_tile(best[:, c, :]), ALU.mult))
                if L == 1:
                    ch.link(v.memset(gates[:, :, :], 1.0))
                    v.tensor_tensor(gates[:, :, 0:E], work[4], work[5], ALU.add).then_inc(s_slot.sem, 1)
                    v.wait_ge(*s_slot(1))
                    return

                def over_tiles():
                    a, b = (view(7168 + k * TILES * E, 2, TILES, E) for k in (8, 10))
                    ch.link(v.tensor_copy(a, bank(4)[:, 0:256].rearrange("p (c t e) -> p c t e", c=2, e=E)))
                    step = 1
                    while step < TILES:
                        ch.add(v.tensor_copy(b[:, :, 0:step, :], a[:, :, 0:step, :]))
                        ch.link(v.tensor_tensor(b[:, :, step:, :], a[:, :, step:, :], a[:, :, :TILES - step, :], ALU.add))
                        a, b = b, a
                        step *= 2
                    ch.link(v.tensor_tensor(b, a, bank(4)[:, 0:256].rearrange("p (c t e) -> p c t e", c=2, e=E), ALU.subtract))
                    ch.link(v.tensor_tensor(b, b, bank(3)[:, 0:256].rearrange("p (c t e) -> p c t e", c=2, e=E), ALU.add))
                    return a, b

                if L == 3:
                    gate, over, at_limit = work[4], work[6], work[7]
                    ch.link(v.tensor_tensor(gate, work[4], work[5], ALU.add))
                    ch.link(v.memset(limit[:, :], 0))
                    passed = view(7168 + 8 * TILES * E, 3, TILES, E)
                    for n in range(SEARCH):
                        shift = 2 * (SEARCH - 1 - n)
                        for k in range(3):
                            ch.add(v.tensor_scalar(tries[:, k, :], limit[:, :], (k + 1) << shift, None, ALU.bitwise_or))
                        ch.wait()
                        ch.link(v.tensor_tensor(passed, gate.unsqueeze(1).to_broadcast([P, 3, TILES, E]),
                                                tries[:, :, :].bitcast(FP32).unsqueeze(2).to_broadcast([P, 3, TILES, E]),
                                                ALU.is_ge))
                        with nc.allow_low_precision("whole numbers up to 16"):
                            v.reduce_sum(masks_bf[:, 0, 0:3, :], passed.rearrange("p k t e -> p k e t"), AX.X)\
                                .then_inc(s_mask.sem, 1)
                        v.wait_ge(*s_count(n + 1))
                        ch.link(v.tensor_scalar(counts[:, 0:3, :], bank(5)[:, 0:3 * E].rearrange("p (k e) -> p k e", e=E),
                                                CAP3 - 0.5, float(1 << shift), ALU.is_gt, ALU.mult))
                        with nc.allow_low_precision("one of four multiples of a power of two"):
                            ch.link(v.reduce_sum(tries[:, 0, :], counts[:, 0:3, :].rearrange("p k e -> p e k"), AX.X))
                        ch.link(v.tensor_tensor(limit[:, :], limit[:, :], tries[:, 0, :], ALU.bitwise_or))
                    limit_f = limit[:, :].bitcast(FP32).unsqueeze(1).to_broadcast([P, TILES, E])
                    ch.add(v.tensor_tensor(over, gate, limit_f, ALU.is_gt))
                    ch.link(v.tensor_tensor(at_limit, gate, limit_f, ALU.is_equal))
                    ch.add(v.tensor_copy(masks_bf[:, 0, :, :], over))
                    v.tensor_copy(masks_bf[:, 1, :, :], at_limit).then_inc(s_mask.sem, 1)
                    v.wait_ge(*s_count(SEARCH + 1))
                    total, place = over_tiles()
                    room = counts[:, 0, :]
                    ch.link(v.tensor_scalar(room, total[:, 0, TILES - 1, :], -1.0, float(CAP3), ALU.mult, ALU.add))
                    ch.link(v.tensor_tensor(work[4], place[:, 1, :, :], room.unsqueeze(1).to_broadcast([P, TILES, E]), ALU.is_lt))
                    ch.link(v.tensor_tensor(work[5], work[4], at_limit, ALU.mult))
                    ch.link(v.tensor_tensor(work[4], work[5], over, ALU.add))
                    kept = view(7168 + 12 * TILES * E, 2, TILES, E)
                    ch.link(v.tensor_tensor(kept, masks[:, :, :, :], work[4].unsqueeze(1).to_broadcast([P, 2, TILES, E]), ALU.mult))
                    ch.link(v.reduce_sum(slot_f[:, :, :], kept, AX.X))
                    ch.link(v.tensor_tensor(best[:, :, :], best[:, :, :], slot_f[:, :, :], ALU.mult))

                v.tensor_copy(masks_bf[:, :, :, :], masks[:, :, :, :]).then_inc(s_mask.sem, 1)
                v.wait_ge(*s_count(SEARCH + 2 if SEARCH else 1))
                total, place = over_tiles()
                picked = view(7168 + 12 * TILES * E, 2, TILES, E)
                if L == 2:
                    ch.link(v.tensor_tensor(picked, masks[:, :, :, :], place, ALU.mult))
                    ch.link(v.reduce_sum(slot_f[:, :, :], picked, AX.X))
                    ch.link(v.scalar_tensor_tensor(best[:, :, :], slot_f[:, :, :], CAP - 0.5, best[:, :, :], ALU.is_lt, ALU.mult))
                number, tiles, end, other, first = (counts[:, k, :] for k in range(5))
                ch.link(v.tensor_tensor(number, total[:, 0, TILES - 1, :], total[:, 1, TILES - 1, :], ALU.add))
                more = work[0].rearrange("p t e -> p (t e)")[:, 0:E * KMAX].rearrange("p (e k) -> p e k", k=KMAX)
                ch.link(v.tensor_tensor(more, number.unsqueeze(2).to_broadcast([P, E, KMAX]),
                                        step_no[:, :].unsqueeze(1).to_broadcast([P, E, KMAX]), ALU.is_gt))
                ch.link(v.reduce_sum(tiles, more, AX.X))
                ch.link(v.tensor_copy(end, tiles))
                a, b = end, other
                for step in (1, 2, 4):
                    ch.add(v.tensor_copy(b[:, 0:step], a[:, 0:step]))
                    ch.link(v.tensor_tensor(b[:, step:], a[:, step:], a[:, :E - step], ALU.add))
                    a, b = b, a
                end = a
                ch.link(v.tensor_tensor(first, end, tiles, ALU.subtract))
                ch.link(v.tensor_scalar(first, first, float(SLOTS), None, ALU.mult))
                ch.link(v.tensor_tensor(work[1], place[:, 0, :, :], place[:, 1, :, :], ALU.add))
                ch.link(v.tensor_tensor(work[2], work[1], first.unsqueeze(1).to_broadcast([P, TILES, E]), ALU.add))
                ch.link(v.tensor_tensor(picked, masks[:, :, :, :], work[2].unsqueeze(1).to_broadcast([P, 2, TILES, E]), ALU.mult))
                ch.link(v.reduce_sum(slot_f[:, :, :], picked, AX.X))
                ch.link(v.tensor_copy(slot[:, :, :], slot_f[:, :, :]))
                ended = view(7168, NT, E, parts=1)
                ch.link(v.tensor_tensor(ended, end[0:1, :].unsqueeze(1).to_broadcast([1, NT, E]),
                                        tile_no[0:1, :].unsqueeze(2).to_broadcast([1, NT, E]), ALU.is_le))
                ch.link(v.reduce_sum(expert_f[:, :], ended, AX.X))
                v.tensor_scalar(expert[:, :], expert_f[:, :], float(E - 1), None, ALU.min).then_inc(s_slot.sem, 1)
                v.wait_ge(*s_slot(1))

            return Stage(sync, gpsimd, scalar, vector, tensor), s_slot(1)

        def moe(L, kind, w1, w2, w3=None, b1=None, b2=None, routed=None):
            lead = 0 if w3 is not None else 1
            w_ins = [w1] + ([w3] if w3 is not None else [])
            n_in = len(w_ins)
            def parts(k):
                v = w_parts[:, k * 2048:(k + 1) * 2048]
                return v
            in_parts = [[[parts(4 * m + 2 * u + q).rearrange("p (c f) -> p c f", c=DC) for q in range(2)]
                         for u in range(2)] for m in range(n_in)]
            out_parts = [[parts(4 * n_in + 2 * u + q).rearrange("p (c o) -> p c o", c=FC) for q in range(2)]
                         for u in range(lead + 1)]
            h_part = [[h_parts[:, (2 * u + q) * 2048:(2 * u + q + 1) * 2048].rearrange("p (c s) -> p c s", c=FC)
                       for q in range(2)] for u in range(2)]
            x_part = [[xT_parts[:, (2 * u + q) * 512:(2 * u + q + 1) * 512].rearrange("p (c s) -> p c s", c=DC)
                       for q in range(2)] for u in range(2)]
            quarters2 = ((0,), (1,), (2,), (3,)) if lead else ((0, 1, 2, 3), (), (), ())
            quarters = ((0,), (1,), (2, 3), ())
            half = [(NT + 1 - u) // 2 for u in range(2)]
            per_x = 16 * (2 if b1 is not None else 1)

            s_disp = signal("moe_dispatched", 16 * 2 * TILES, first=0)
            s_raw = [[signal(f"moe_raw{m}_half{h}", 16 * NT) for h in range(2)] for m in range(n_in)]
            s_raw2 = [signal(f"moe_raw_w2_half{h}", 16 * NT) for h in range(2)]
            s_xin = [signal(f"moe_x_in{u}", per_x * half[u]) for u in range(2)]
            s_b2 = [signal(f"moe_b2_in{u}", 16 * half[u]) for u in range(2)] if b2 is not None else None
            s_hi = [signal(f"moe_w_high{m}", 4 * NT) for m in range(n_in)]
            s_hi2 = signal("moe_w2_high", 4 * NT)
            s_split = [signal(f"moe_w_split{m}", 2 * NT, first=2) for m in range(n_in)]
            s_split2 = signal("moe_w2_split", 2 * NT, first=2)
            s_xT_ps = [signal(f"moe_xT_in_psum{u}", half[u]) for u in range(2)]
            s_xhi, s_xsplit = signal("moe_x_high", NT), signal("moe_x_split", NT)
            s_hps = signal("moe_h_in_psum", FPAIRS * NT)
            s_act = signal("moe_activated", FPAIRS * NT)
            s_gated = signal("moe_gated", FPAIRS * NT if kind == "swiglu" else 0)
            s_hhi, s_hsplit = signal("moe_h_high", FPAIRS * NT), signal("moe_h_split", FPAIRS * NT)
            s_mm2 = [signal(f"moe_mm2{u}", half[u]) for u in range(2)]
            s_y = [signal(f"moe_y_in_sbuf{u}", half[u]) for u in range(2)]
            s_stored = [signal(f"moe_y_stored{u}", 16 * half[u], first=0) for u in range(2)]
            s_yfree = [signal(f"moe_y_buffer_free{u}", half[u]) for u in range(2)]
            GROUP, GROUPS = 4, 4
            s_back = [signal(f"moe_gathered{k}", 16 * 2 * TILES // GROUPS, first=0) for k in range(GROUPS)]
            s_comb = signal("moe_combined", 2 * TILES)

            def none_if_first(n):
                return max(n, 0) if isinstance(n, int) else n

            def exists(t):
                return not isinstance(t, int) or 0 <= t < NT

            def tiles(eng, step):
                pairs = (NT - 2) // 2
                for t in range(2):
                    step(t, t, 0)
                with eng.Fori(1, pairs) as it:
                    step(2 * it, 0, it)
                    step(2 * it + 1, 1, it)
                for t in range(2 * pairs, NT):
                    step(t, t % 2, t // 2)

            def sync(sp):
                sp.wait_ge(*routed)

                def expert_of(t):
                    return sp.value_load(expert[0:1, bass.ds(t, 1)] if not isinstance(t, int) else expert[0:1, t:t + 1],
                                         min_val=0, max_val=E - 1)

                def load_in(t, e, h):
                    for m in range(n_in):
                        sp.wait_ge(*s_split[m](none_if_first(2 * t - 1 + h)))
                        sp.dma_start(raw[m][:, h * F:(h + 1) * F],
                                     w_ins[m][bass.ds(e, 1), h * P:(h + 1) * P, :].rearrange("a p f -> p (a f)"))\
                            .then_inc(s_raw[m][h].sem, 16)

                def load_out(t, e, h):
                    sp.wait_ge(*s_split2(none_if_first(2 * t - 1 + h)))
                    sp.dma_start(raw[2][:, h * F:(h + 1) * F].rearrange("p (c o) -> p c o", c=FC // 2),
                                 w2[bass.ds(e, 1), h * F // 2:(h + 1) * F // 2, :].rearrange("a (c p) o -> p (a c) o", p=P))\
                        .then_inc(s_raw2[h].sem, 16)

                def load_x(t, u, it, e):
                    sp.wait_ge(*s_xT_ps[u](it))
                    sp.dma_start(x_rows[:, u, :, :], xs[bass.ds(t * SLOTS, SLOTS), :].rearrange("(s p) d -> p s d", p=P))\
                        .then_inc(s_xin[u].sem, 16)
                    if b1 is not None:
                        if not isinstance(t, int) or t > 1:
                            sp.wait_ge(*s_act(FPAIRS * (t - 1)))
                        sp.dma_start(b1_buf[:, u, :], b1[bass.ds(e, 1), :, :].rearrange("a p c -> p (a c)"))\
                            .then_inc(s_xin[u].sem, 16)

                def load_b2(t, u, it):
                    if b2 is not None:
                        e = expert_of(t)
                        sp.wait_ge(*s_mm2[u](it))
                        sp.dma_start(b2_buf[:, u, :], b2[bass.ds(e, 1), :]).then_inc(s_b2[u].sem, 16)

                for t in range(3):
                    if t > 0 and t - 1 < 1 + lead:
                        e = expert_of(t - 1)
                        for h in range(2):
                            load_out(t - 1, e, h)
                    e = expert_of(t)
                    for h in range(2):
                        load_in(t, e, h)
                    if t == 0:
                        sp.wait_ge(*s_disp(16 * 2 * TILES))
                    load_x(t, t % 2, t // 2, e)
                load_b2(0, 0, 0)

                def step(t, u, it):
                    if exists(t + 1 + lead):
                        e_out = expert_of(t + 1 + lead)
                    if exists(t + 3):
                        e_in = expert_of(t + 3)
                    for h in range(2):
                        if exists(t + 1 + lead):
                            load_out(t + 1 + lead, e_out, h)
                        if exists(t + 3):
                            load_in(t + 3, e_in, h)
                        if h == 0 and exists(t + 1):
                            load_b2(t + 1, 1 - u, it + u)
                    if exists(t + 3):
                        load_x(t + 3, 1 - u, it + 1 + u, e_in)

                tiles(sp, step)

            def gpsimd(g):
                g.wait_ge(*s_zeroed(16 * zero_dmas))
                g.wait_ge(*routed)
                for t in range(TILES):
                    for c in range(2):
                        g.indirect_dma_start(out=xs, out_offset=bass.IndirectOffsetOnAxis(ap=slot[:, c, t:t + 1], axis=0),
                                             in_=xn[:, t, :], in_offset=None).then_inc(s_disp.sem, 16)

                def step(t, u, it):
                    g.wait_ge(*s_y[u](it + 1))
                    g.dma_start(ys[bass.ds(t * SLOTS, SLOTS), :].rearrange("(s p) d -> p s d", p=P),
                                y_rows[:, u, :, :]).then_inc(s_stored[u].sem, 16)
                    g.wait_ge(*s_stored[u](16 * (it + 1)))
                    g.sem_inc(s_yfree[u].sem, 1)

                tiles(g, step)
                for t in range(TILES):
                    for c in range(2):
                        n = 2 * t + c
                        if n % GROUP == 0 and n >= GROUP * GROUPS:
                            g.wait_ge(*s_comb(n - GROUP * (GROUPS - 1)))
                        g.indirect_dma_start(out=y_back[:, n % 16, :], out_offset=None, in_=ys,
                                             in_offset=bass.IndirectOffsetOnAxis(ap=slot[:, c, t:t + 1], axis=0))\
                            .then_inc(s_back[n // GROUP % GROUPS].sem, 16)

            def tensor(t_eng):
                def product(o, pairs, first, last):
                    (ah, al), (bh, bl) = pairs
                    t_eng.matmul(o, ah, bh, start=first, stop=False)
                    t_eng.matmul(o, ah, bl, start=False, stop=False)
                    return t_eng.matmul(o, al, bh, start=False, stop=last)

                def transposes(t, u, it):
                    t_eng.wait_ge(*s_xin[u](per_x * (it + 1)))
                    t_eng.wait_ge(*s_xsplit(t))
                    for s in range(SB):
                        for c in range(DC):
                            o = bank(6)[:, c * SLOTS + s * P:c * SLOTS + (s + 1) * P]
                            ins = t_eng.transpose(o, x_rows[:, u, s, c * P:(c + 1) * P], ident[:, :])
                    ins.then_inc(s_xT_ps[u].sem, 1)

                def hidden(t, u, it):
                    for m in range(n_in):
                        t_eng.wait_ge(*s_split[m](2 * t + 2))
                    t_eng.wait_ge(*s_xsplit(t + 1))
                    for p in range(FPAIRS):
                        for m in range(n_in):
                            k = p if n_in == 1 else 2 * m + p % 2
                            if n_in == 1 and (not isinstance(t, int) or t > 0):
                                t_eng.wait_ge(*s_act(FPAIRS * (t - 1) + p + 1))
                            if n_in == 2 and (not isinstance(t, int) or t > 0 or p >= 2):
                                t_eng.wait_ge(*(s_act, s_gated)[m](FPAIRS * t + p - 1))
                            for q in range(2):
                                f = 2 * p + q
                                for c in range(DC):
                                    ins = product(bank(k)[:, q * SLOTS:(q + 1) * SLOTS],
                                                  ([in_parts[m][u][z][:, c, f * P:(f + 1) * P] for z in range(2)],
                                                   [x_part[u][z][:, c, :] for z in range(2)]), c == 0, c == DC - 1)
                        ins.then_inc(s_hps.sem, 1)

                def output(t, u, it):
                    t_eng.wait_ge(*s_split2(2 * t + 2))
                    t_eng.wait_ge(*s_y[u](it))
                    if b2 is not None:
                        t_eng.wait_ge(*s_b2[u](16 * (it + 1)))
                    for s in range(SB):
                        o = bank(4 + u)[:, s * D:(s + 1) * D]
                        for f in range(FC):
                            if s == 0 and f % 2 == 0:
                                t_eng.wait_ge(*s_hsplit(FPAIRS * t + f // 2 + 1))
                            ins = product(o, ([h_part[u][z][:, f, s * P:(s + 1) * P] for z in range(2)],
                                              [out_parts[u * lead][z][:, f, :] for z in range(2)]),
                                          f == 0, f == FC - 1 and b2 is None)
                        if b2 is not None:
                            ins = t_eng.matmul(o, ones_row[:, :], b2_buf[:, u, :], start=False, stop=True)
                    ins.then_inc(s_mm2[u].sem, 1)

                transposes(0, 0, 0)
                hidden(0, 0, 0)
                transposes(1, 1, 0)

                def step(t, u, it):
                    if exists(t + 1):
                        hidden(t + 1, 1 - u, it + u)
                    if exists(t + 2):
                        transposes(t + 2, u, it + 1)
                    output(t, u, it)

                tiles(t_eng, step)

            def scalar(a):
                def high(m, t, u, it, q):
                    if q % 2 == 0:
                        a.wait_ge(*s_raw[m][q // 2](16 * (t + 1)))
                    if q == 0:
                        if not isinstance(t, int) or t >= 2:
                            a.wait_ge(*s_hps(FPAIRS * (t - 1)))
                    a.copy(in_parts[m][u][0].rearrange("p c f -> p (c f)")[:, q * 512:(q + 1) * 512],
                           raw[m][:, q * 512:(q + 1) * 512]).then_inc(s_hi[m].sem, 1)

                def high2(t, u, it, q):
                    if q % 2 == 0:
                        a.wait_ge(*s_raw2[q // 2](16 * (t + 1)))
                    if q == 0:
                        if lead:
                            a.wait_ge(*s_mm2[u](it))
                        elif not isinstance(t, int) or t > 0:
                            a.wait_ge(*s_mm2[1 - u](it + u))
                    a.copy(out_parts[u * lead][0].rearrange("p c o -> p (c o)")[:, q * 512:(q + 1) * 512],
                           raw[2][:, q * 512:(q + 1) * 512]).then_inc(s_hi2.sem, 1)

                def high_x(t, u, it):
                    a.wait_ge(*s_xT_ps[u](it + 1))
                    a.copy(x_part[u][0], bank(6).rearrange("p (c s) -> p c s", c=DC)).then_inc(s_xhi.sem, 1)

                def activate(t, u, it, p):
                    a.wait_ge(*s_hps(FPAIRS * t + p + 1))
                    first = isinstance(t, int) and t == 0 and p < 2
                    if kind == "swiglu":
                        if not first:
                            a.wait_ge(*s_gated(FPAIRS * t + p - 1))
                        a.activation(h_gate[:, p % 2, :], bank(p % 2), ACT.Silu).then_inc(s_act.sem, 1)
                        return
                    if not first:
                        a.wait_ge(*s_hsplit(FPAIRS * t + p - 1))
                    if kind == "gelu":
                        a.activation(h_raw[:, p % 2, :], bank(p), ACT.Gelu_apprx_tanh).then_inc(s_act.sem, 1)
                    else:
                        for q in range(2):
                            f = 2 * p + q
                            ins = a.activation(h_raw[:, p % 2, q * SLOTS:(q + 1) * SLOTS], bank(p)[:, q * SLOTS:(q + 1) * SLOTS],
                                               ACT.Relu, bias=b1_buf[:, u, f:f + 1])
                        ins.then_inc(s_act.sem, 1)

                def evict(t, u, it):
                    a.wait_ge(*s_mm2[u](it + 1))
                    a.wait_ge(*s_yfree[u](it))
                    a.copy(y_rows[:, u, :, :], bank(4 + u).rearrange("p (s d) -> p s d", s=SB)).then_inc(s_y[u].sem, 1)

                for t in range(2):
                    if t == 1 and lead:
                        for q in range(4):
                            high2(0, 0, 0, q)
                    for q in range(4):
                        for m in range(n_in):
                            high(m, t, t, 0, q)
                    if t == 1:
                        for p in range(FPAIRS):
                            activate(0, 0, 0, p)
                    high_x(t, t, 0)

                def step(t, u, it):
                    for q in range(4):
                        for q2 in quarters2[q]:
                            if exists(t + lead):
                                high2(t + lead, (1 - u) if lead else u, (it + u) if lead else it, q2)
                        if exists(t + 1):
                            activate(t + 1, 1 - u, it + u, q)
                        for q1 in quarters[q]:
                            if exists(t + 2):
                                for m in range(n_in):
                                    high(m, t + 2, u, it + 1, q1)
                        if q == 0 and not (isinstance(t, int) and t == 0):
                            evict(t - 1, 1 - u, it - 1 + u)
                    if exists(t + 2):
                        high_x(t + 2, u, it + 1)

                tiles(a, step)
                evict(NT - 1, (NT - 1) % 2, (NT - 1) // 2)

            def vector(v):
                def low(m, t, u, it, q):
                    v.wait_ge(*s_hi[m](4 * t + q + 1))
                    part = slice(q * 512, (q + 1) * 512)
                    hi, lo = (z.rearrange("p c f -> p (c f)")[:, part] for z in in_parts[m][u])
                    ins = v.tensor_tensor(lo, raw[m][:, part], hi.bitcast(FP32), ALU.subtract)
                    if q % 2 == 1:
                        ins.then_inc(s_split[m].sem, 1)

                def low2(t, u, it, q):
                    v.wait_ge(*s_hi2(4 * t + q + 1))
                    part = slice(q * 512, (q + 1) * 512)
                    hi, lo = (z.rearrange("p c o -> p (c o)")[:, part] for z in out_parts[u * lead])
                    ins = v.tensor_tensor(lo, raw[2][:, part], hi.bitcast(FP32), ALU.subtract)
                    if q % 2 == 1:
                        ins.then_inc(s_split2.sem, 1)

                def low_x(t, u, it):
                    v.wait_ge(*s_xhi(t + 1))
                    v.tensor_tensor(x_part[u][1], bank(6).rearrange("p (c s) -> p c s", c=DC),
                                    x_part[u][0].bitcast(FP32), ALU.subtract).then_inc(s_xsplit.sem, 1)

                def high_h(t, u, it, p):
                    if p == 0:
                        v.wait_ge(*s_mm2[u](it))
                    v.wait_ge(*s_act(FPAIRS * t + p + 1))
                    hi, lo = (h_part[u][z][:, 2 * p:2 * p + 2, :].rearrange("p c s -> p (c s)") for z in range(2))
                    if kind == "swiglu":
                        if not isinstance(t, int) or t > 0 or p >= 2:
                            v.wait_ge(*s_hsplit(FPAIRS * t + p - 1))
                        v.tensor_tensor(h_raw[:, p % 2, :], h_gate[:, p % 2, :], bank(2 + p % 2), ALU.mult)\
                            .then_inc(s_gated.sem, 1)
                        v.wait_ge(*s_gated(FPAIRS * t + p + 1))
                    v.tensor_copy(hi, h_raw[:, p % 2, :]).then_inc(s_hhi.sem, 1)

                def low_h(t, u, it, p):
                    hi, lo = (h_part[u][z][:, 2 * p:2 * p + 2, :].rearrange("p c s -> p (c s)") for z in range(2))
                    v.wait_ge(*s_hhi(FPAIRS * t + p + 1))
                    v.tensor_tensor(lo, h_raw[:, p % 2, :], hi.bitcast(FP32), ALU.subtract).then_inc(s_hsplit.sem, 1)

                for t in range(2):
                    if t == 1 and lead:
                        for q in range(4):
                            low2(0, 0, 0, q)
                    for q in range(4):
                        for m in range(n_in):
                            low(m, t, t, 0, q)
                    if t == 1:
                        for p in range(FPAIRS):
                            high_h(0, 0, 0, p)
                            low_h(0, 0, 0, p)
                    low_x(t, t, 0)

                def step(t, u, it):
                    for q in range(4):
                        if not lead:
                            for q2 in quarters2[q]:
                                low2(t, u, it, q2)
                        if exists(t + 1):
                            high_h(t + 1, 1 - u, it + u, q)
                        if lead and exists(t + 1):
                            for q2 in quarters2[q]:
                                low2(t + 1, 1 - u, it + u, q2)
                        if exists(t + 1):
                            low_h(t + 1, 1 - u, it + u, q)
                        for q1 in quarters[q]:
                            if exists(t + 2):
                                for m in range(n_in):
                                    low(m, t + 2, u, it + 1, q1)
                    if exists(t + 2):
                        low_x(t + 2, u, it + 1)

                tiles(v, step)
                for t in range(TILES):
                    for c in range(2):
                        n = 2 * t + c
                        if n % GROUP == 0:
                            v.wait_ge(*s_back[n // GROUP % GROUPS](16 * GROUP * (n // (GROUP * GROUPS) + 1)))
                        if c == 1:
                            v.wait_ge(*s_comb(n))
                        v.scalar_tensor_tensor(x[:, t, :], y_back[:, n % 16, :], best[:, c, t:t + 1], x[:, t, :],
                                               ALU.mult, ALU.add).then_inc(s_comb.sem, 1)
                v.wait_ge(*s_comb(2 * TILES))

            return Stage(sync, gpsimd, scalar, vector, tensor), s_comb(2 * TILES)

        def dense_experts(routed_w, shared_w, routed):
            n_w = E_ALL * DC * HID
            raw_w = [view(k * n_w, n_w) for k in range(3)]
            silu = view(7680, 2, SEQ)
            xnb = view(9216, TPB, D)
            h_mid = view(10240, 2, SEQ)
            part = [[w_parts[:, (2 * k + z) * n_w:(2 * k + z + 1) * n_w] for z in range(2)] for k in range(3)]
            w1p, w3p = ([z.rearrange("p (e c h) -> p e c h", e=E_ALL, c=DC) for z in part[k]] for k in range(2))
            w2p = [z.rearrange("p (e o) -> p e o", e=E_ALL) for z in part[2]]
            xp = [xT_parts[:, z * 1024:(z + 1) * 1024].rearrange("p (c s) -> p c s", c=DC) for z in range(2)]
            hp = [[h_parts[:, (2 * u + z) * SEQ:(2 * u + z + 1) * SEQ] for z in range(2)] for u in range(2)]
            N = B * E_ALL
            s_raw, s_high, s_low = signal("dense_weights", 16 * 6), signal("dense_w_high", 3), signal("dense_w_split", 3)
            s_blk, s_xT_ps, s_xhi, s_xlo = (signal("dense_block", B), signal("dense_xT_in_psum", B),
                                            signal("dense_x_high", 2 * B), signal("dense_x_split", 2 * B))
            s_hps, s_act, s_mid, s_hhi, s_hlo = (signal(f"dense_{k}", N) for k in
                                                 ("h_in_psum", "silu", "gated", "h_high", "h_split"))
            s_y, s_add = signal("dense_y", N), signal("dense_added", N * TPB)

            def sync(sp):
                sp.wait_ge(*routed)
                for k, (name, of) in enumerate(zip(("w1", "w3", "w2"), (P, P, HID))):
                    form = "e (c p) h -> p (e c) h" if k < 2 else "e p o -> p e o"
                    kw = {"p": P} if k < 2 else {}
                    last = HID if k < 2 else D
                    dst = raw_w[k].rearrange("p (n h) -> p n h", h=last)
                    cut = E * DC if k < 2 else E
                    sp.dma_start(dst[:, 0:cut, :], routed_w[k].rearrange(form, **kw)).then_inc(s_raw.sem, 16)
                    sp.dma_start(dst[:, cut:, :], shared_w[k].rearrange(form, **kw)).then_inc(s_raw.sem, 16)

            def gpsimd(g):
                pass

            def tensor(t):
                def product(o, a, b, first, last):
                    t.matmul(o, a[0], b[0], start=first, stop=False)
                    t.matmul(o, a[0], b[1], start=False, stop=False)
                    return t.matmul(o, a[1], b[0], start=False, stop=last)

                with t.Fori(0, B) as i:
                    t.wait_ge(*s_blk(i + 1))
                    t.wait_ge(*s_add(i * (E_ALL * TPB)))
                    for j in range(TPB):
                        for c in range(DC):
                            ins = t.transpose(bank(6 + c)[:, j * P:(j + 1) * P], xnb[:, j, c * P:(c + 1) * P], ident[:, :])
                    ins.then_inc(s_xT_ps.sem, 1)
                    t.wait_ge(*s_xlo(2 * i + 2))
                    t.wait_ge(*s_low(2))

                    def hidden(e):
                        if e >= 2:
                            t.wait_ge(*s_mid(i * E_ALL + e - 1))
                        for m, w in enumerate((w1p, w3p)):
                            for c in range(DC):
                                ins = product(bank(2 * (e % 2) + m), [z[:, e, c, :] for z in w],
                                              [z[:, c, :] for z in xp], c == 0, c == DC - 1)
                        ins.then_inc(s_hps.sem, 1)

                    hidden(0)
                    for e in range(E_ALL):
                        if e + 1 < E_ALL:
                            hidden(e + 1)
                        if e == 0:
                            t.wait_ge(*s_low(3))
                        t.wait_ge(*s_hlo(i * E_ALL + e + 1))
                        if e >= 2:
                            t.wait_ge(*s_add(TPB * (i * E_ALL + e - 1)))
                        for j in range(TPB):
                            o = bank(4 + 2 * (e % 2) + j // 2)[:, (j % 2) * D:(j % 2 + 1) * D]
                            ins = product(o, [z[:, j * P:(j + 1) * P] for z in hp[e % 2]], [z[:, e, :] for z in w2p], True, True)
                        ins.then_inc(s_y.sem, 1)

            def scalar(a):
                for k in range(3):
                    a.wait_ge(*s_raw(16 * 6))
                    a.copy(part[k][0], raw_w[k]).then_inc(s_high.sem, 1)
                with a.Fori(0, B) as i:
                    a.copy(xnb, xn[:, bass.ds(TPB * i, TPB), :]).then_inc(s_blk.sem, 1)
                    a.wait_ge(*s_xT_ps(i + 1))
                    for c in range(DC):
                        a.copy(xp[0][:, c, :], bank(6 + c)).then_inc(s_xhi.sem, 1)
                    for e in range(E_ALL):
                        a.wait_ge(*s_hps(i * E_ALL + e + 1))
                        if e >= 2:
                            a.wait_ge(*s_mid(i * E_ALL + e - 1))
                        a.activation(silu[:, e % 2, :], bank(2 * (e % 2)), ACT.Silu).then_inc(s_act.sem, 1)

            def vector(v):
                for k in range(3):
                    v.wait_ge(*s_high(k + 1))
                    v.tensor_tensor(part[k][1], raw_w[k], part[k][0].bitcast(FP32), ALU.subtract).then_inc(s_low.sem, 1)
                with v.Fori(0, B) as i:
                    for c in range(DC):
                        v.wait_ge(*s_xhi(2 * i + c + 1))
                        v.tensor_tensor(xp[1][:, c, :], bank(6 + c), xp[0][:, c, :].bitcast(FP32),
                                        ALU.subtract).then_inc(s_xlo.sem, 1)

                    def middle(e):
                        n = i * E_ALL + e
                        v.wait_ge(*s_act(n + 1))
                        if e >= 2:
                            v.wait_ge(*s_hlo(n - 1))
                        v.tensor_tensor(h_mid[:, e % 2, :], silu[:, e % 2, :], bank(2 * (e % 2) + 1), ALU.mult)\
                            .then_inc(s_mid.sem, 1)
                        v.wait_ge(*s_mid(n + 1))
                        v.tensor_copy(hp[e % 2][0], h_mid[:, e % 2, :]).then_inc(s_hhi.sem, 1)
                        v.wait_ge(*s_hhi(n + 1))
                        v.tensor_tensor(hp[e % 2][1], h_mid[:, e % 2, :], hp[e % 2][0].bitcast(FP32), ALU.subtract)\
                            .then_inc(s_hlo.sem, 1)

                    def add(e):
                        n = i * E_ALL + e
                        v.wait_ge(*s_y(n + 1))
                        for j in range(TPB):
                            if e:
                                v.wait_ge(*s_add(TPB * (n - 1) + j + 1))
                            v.scalar_tensor_tensor(tile_of(i, j),
                                                   bank(4 + 2 * (e % 2) + j // 2)[:, (j % 2) * D:(j % 2 + 1) * D],
                                                   gates[:, bass.ds(TPB * i + j, 1), e], tile_of(i, j),
                                                   ALU.mult, ALU.add).then_inc(s_add.sem, 1)

                    middle(0)
                    for e in range(E_ALL):
                        if e + 1 < E_ALL:
                            middle(e + 1)
                        add(e)
                v.wait_ge(*s_add(N * TPB))

            return Stage(sync, gpsimd, scalar, vector, tensor), s_add(N * TPB)

        def local_attention(x_before):
            wa = view(0, DC, D)
            wc = view(512, 2 * DC, D)
            ctx_rows = view(1536, B, D, parts=KEYS)
            keep, masked, gauss = (view(2560 + k * 256, B, KEYS) for k in range(3))
            xnb, xnT, qT = view(3328, TPB, D), view(4352, DC, SEQ), view(5376, DC, SEQ)
            align = view(6400, TPB, KEYS)
            alignT = view(6656, SEQ, parts=KEYS)
            contextT = view(7168, DC, SEQ)
            tanh = view(8192, 2, D)
            ctx_now = view(8704, D, parts=KEYS)
            centre, begin, finish, length = (view(8960 + k * B, B) for k in range(4))
            top, total, inverse = (view(8992 + k * TPB, TPB) for k in range(3))

            s_w = signal("local_weights", 16 * 5)
            s_ch = signal("local_chain", 0)
            s_dist, s_gauss = signal("local_distance", 1), signal("local_gauss", 1)
            s_now = signal("local_context_now", B)
            s_var, s_rstd, s_norm = signal("variance", B), signal("rstd", B), signal("local_normed", TILES)
            s_xT_ps, s_xT, s_q_ps, s_q = (signal(f"local_{k}", n * B) for k, n in
                                          (("xT_in_psum", 1), ("xT", 2), ("q_in_psum", 2), ("q", 2)))
            s_sc, s_less, s_exp, s_al = (signal(f"local_{k}", B) for k in ("scores", "shifted", "exp", "aligned"))
            s_aT_ps, s_aT, s_c_ps, s_c = (signal(f"local_{k}", B) for k in ("alignT_in_psum", "alignT", "context_in_psum", "context"))
            s_y, s_tanh, s_x = (signal(f"local_{k}", TILES) for k in ("y", "tanh", "x_updated"))

            def sync(sp):
                sp.wait_ge(*x_before)
                sp.dma_start(wa, io["L2_xcond_W_a"].rearrange("(c p) k -> p c k", p=P)).then_inc(s_w.sem, 16)
                sp.dma_start(wc, io["L2_xcond_W_c"].rearrange("(c p) o -> p c o", p=P)).then_inc(s_w.sem, 16)
                sp.dma_start(ctx_rows, io["ctx_1024"].rearrange("b k d -> k b d")).then_inc(s_w.sem, 16)
                sp.dma_start(centre, io["condB_pt"].to_broadcast([P, B])).then_inc(s_w.sem, 16)
                sp.dma_start(lens[:, :], io["_lenS2"].to_broadcast([P, B])).then_inc(s_w.sem, 16)

            def gpsimd(g):
                g.wait_ge(*s_w(16 * 5))
                with g.Fori(0, B) as i:
                    norm_gpsimd(g, i, s_var, s_rstd)
                    g.wait_ge(*s_c_ps(i))
                    g.tensor_copy(ctx_now, ctx_rows[:, bass.ds(i, 1), :].rearrange("p a d -> p (a d)"))\
                        .then_inc(s_now.sem, 1)

            def tensor(t):
                t.wait_ge(*s_w(16 * 5))
                with t.Fori(0, B) as i:
                    t.wait_ge(*s_tanh(TPB * i))
                    for j in range(TPB):
                        t.wait_ge(*s_norm(TPB * i + j + 1))
                        for c in range(DC):
                            ins = t.transpose(bank(c)[:, j * P:(j + 1) * P], xnb[:, j, c * P:(c + 1) * P], ident[:, :])
                    ins.then_inc(s_xT_ps.sem, 1)
                    t.wait_ge(*s_xT(2 * i + 2))
                    for oc in range(DC):
                        for kc in range(DC):
                            ins = t.matmul(bank(2 + oc), wa[:, kc, oc * P:(oc + 1) * P], xnT[:, kc, :],
                                           start=(kc == 0), stop=(kc == DC - 1))
                        ins.then_inc(s_q_ps.sem, 1)
                    t.wait_ge(*s_q(2 * i + 2))
                    for j in range(TPB):
                        for c in range(DC):
                            ins = t.matmul(bank(4)[:, j * KEYS:(j + 1) * KEYS], qT[:, c, j * P:(j + 1) * P],
                                           ctxT[:, c, bass.ds(i, 1), 0, :].rearrange("p a k -> p (a k)"),
                                           start=(c == 0), stop=(c == DC - 1))
                    ins.then_inc(s_sc.sem, 1)
                    t.wait_ge(*s_al(i + 1))
                    t.transpose(bank(5)[:, 0:P], align[:, 0:2, :].rearrange("p j k -> p (j k)"), ident[:, :])
                    for j in range(1, TPB):
                        ins = t.transpose(bank(5)[0:KEYS, j * P:(j + 1) * P], align[:, j, :], ident[:, :])
                    ins.then_inc(s_aT_ps.sem, 1)
                    t.wait_ge(*s_aT(i + 1))
                    t.wait_ge(*s_now(i + 1))
                    for c in range(DC):
                        ins = t.matmul(bank(6 + c), ctx_now[:, c * P:(c + 1) * P], alignT, start=True, stop=True)
                    ins.then_inc(s_c_ps.sem, 1)
                    t.wait_ge(*s_c(i + 1))
                    for j in range(TPB):
                        o = bank(j)[:, 0:D]
                        for c in range(2 * DC):
                            left = contextT if c < DC else xnT
                            ins = t.matmul(o, left[:, c % DC, j * P:(j + 1) * P], wc[:, c, :],
                                           start=(c == 0), stop=(c == 2 * DC - 1))
                        ins.then_inc(s_y.sem, 1)

            def scalar(a):
                a.wait_ge(*s_dist(1))
                a.activation(gauss, gauss, ACT.Exp, scale=-1.0 / DEV_POW).then_inc(s_gauss.sem, 1)
                with a.Fori(0, B) as i:
                    a.wait_ge(*s_xT_ps(i + 1))
                    for c in range(DC):
                        a.copy(xnT[:, c, :], bank(c)).then_inc(s_xT.sem, 1)
                    for c in range(DC):
                        a.wait_ge(*s_q_ps(2 * i + c + 1))
                        a.copy(qT[:, c, :], bank(2 + c)).then_inc(s_q.sem, 1)
                    a.wait_ge(*s_less(i + 1))
                    a.activation(align, align, ACT.Exp).then_inc(s_exp.sem, 1)
                    a.wait_ge(*s_aT_ps(i + 1))
                    a.copy(alignT, bank(5)[0:KEYS, :]).then_inc(s_aT.sem, 1)
                    a.wait_ge(*s_c_ps(i + 1))
                    a.copy(contextT, bank(6, 2).rearrange("p (c s) -> p c s", c=DC)).then_inc(s_c.sem, 1)
                    for j in range(TPB):
                        a.wait_ge(*s_y(TPB * i + j + 1))
                        if j >= 2:
                            a.wait_ge(*s_x(TPB * i + j - 1))
                        a.activation(tanh[:, j % 2, :], bank(j)[:, 0:D], ACT.Tanh)\
                            .then_inc(s_tanh.sem, 1)

            def vector(v):
                v.wait_ge(*s_w(16 * 5))
                pre = Chain(v, s_ch)
                pre.link(v.tensor_copy(length, lens[:, :]))
                pre.add(v.tensor_scalar(begin, centre, -WINDOW, 0.0, ALU.add, ALU.max))
                pre.link(v.tensor_scalar(finish, centre, WINDOW, None, ALU.add))
                pre.link(v.tensor_tensor(finish, finish, length, ALU.min))
                for b in range(B):
                    pre.add(v.tensor_scalar(keep[:, b, :], key_no[:, :], begin[:, b:b + 1], None, ALU.is_ge))
                    pre.add(v.tensor_scalar(gauss[:, b, :], key_no[:, :], centre[:, b:b + 1], None, ALU.subtract))
                pre.wait()
                for b in range(B):
                    pre.add(v.scalar_tensor_tensor(keep[:, b, :], key_no[:, :], finish[:, b:b + 1], keep[:, b, :],
                                                   ALU.is_le, ALU.mult))
                pre.wait()
                pre.link(v.tensor_scalar(masked, keep, -1.0, 1e9, ALU.add, ALU.mult))
                v.tensor_tensor(gauss, gauss, gauss, ALU.mult).then_inc(s_dist.sem, 1)
                v.wait_ge(*s_gauss(1))
                LINKS = 2 * TPB + 6
                with v.Fori(0, B) as i:
                    ch = Chain(v, s_ch, pre.n + i * LINKS)
                    norm_vector(v, ch, i, xnb, s_var, s_rstd, s_norm)
                    v.wait_ge(*s_sc(i + 1))

                    def of_batch(table):
                        return table[:, bass.ds(i, 1), :].to_broadcast([P, TPB, KEYS])

                    def of_row(row):
                        return row.unsqueeze(2).to_broadcast([P, TPB, KEYS])

                    ch.link(v.tensor_tensor(align, bank(4)[:, 0:TPB * KEYS].rearrange("p (j k) -> p j k", k=KEYS),
                                            of_batch(keep), ALU.mult))
                    ch.link(v.tensor_tensor(align, align, of_batch(masked), ALU.add))
                    ch.link(v.reduce_max(top, align, AX.X))
                    v.tensor_tensor(align, align, of_row(top), ALU.subtract).then_inc(s_less.sem, 1)
                    v.wait_ge(*s_exp(i + 1))
                    ch.link(v.reduce_sum(total, align, AX.X))
                    ch.link(v.reciprocal(inverse, total))
                    ch.link(v.tensor_tensor(align, align, of_row(inverse), ALU.mult))
                    v.tensor_tensor(align, align, of_batch(gauss), ALU.mult).then_inc(s_al.sem, 1)
                    for j in range(TPB):
                        v.wait_ge(*s_tanh(TPB * i + j + 1))
                        v.tensor_tensor(tile_of(i, j), tile_of(i, j), tanh[:, j % 2, :], ALU.add).then_inc(s_x.sem, 1)
                    assert ch.n == LINKS
                v.wait_ge(*s_x(TILES))

            return Stage(sync, gpsimd, scalar, vector, tensor), s_x(TILES)

        b1_buf = view(9216, 2, FC)
        b2_buf = view(9232, 2, D, parts=1)
        y_back = view(0, 16, D)
        lens = sb("lens", [P, B], I32)

        def layer_router(L):
            return {0: lambda: router(0, io["L0_ffn_gate_w"], None, x_done),
                    1: lambda: router(1, io["L1_ffn_router_w"], io["L1_ffn_router_b"], x_done),
                    2: lambda: router(2, io["L2_ffn_gate_w"], io["L2_ffn_gate_b"], x_done),
                    3: lambda: router(3, io["L3_ffn_router_gate"], None, x_done)}[L]

        def layer_experts(L):
            return {0: lambda: moe(0, "gelu", io["L0_ffn_w1"], io["L0_ffn_w2"], routed=x_done),
                    1: lambda: dense_experts([io[f"L1_ffn_routed_{k}"] for k in ("w1", "w3", "w2")],
                                             [io[f"L1_ffn_shared_{k}"] for k in ("w1", "w3", "w2")], x_done),
                    2: lambda: moe(2, "relu", io["L2_ffn_W1"], io["L2_ffn_W2"], b1=io["L2_ffn_b1"],
                                   b2=io["L2_ffn_b2"], routed=x_done),
                    3: lambda: moe(3, "swiglu", io["L3_ffn_gate_w"], io["L3_ffn_down_w"], w3=io["L3_ffn_up_w"],
                                   routed=x_done)}[L]

        plan = [start]
        x_done = None
        for L in range((stages + 1) // 2):
            parts = [(lambda: local_attention(x_done)) if L == 2 else (lambda: attention(L, x_done, s_x_in(16) if L == 0 else None))]
            if 2 * L + 1 < stages:
                parts += [layer_router(L), layer_experts(L)]
            for make in parts:
                stage, x_done = make()
                plan.append(stage)
        plan.insert(2, load_x)

        s_out = signal("output", 16)

        def store(sp):
            sp.wait_ge(*x_done)
            sp.dma_start(out.rearrange("b (t p) d -> p (b t) d", p=P), x[:, :, :]).then_inc(s_out.sem, 16)
            sp.wait_ge(*s_out(16))

        block = ctx.enter_context(nc.Block())

        @block.sync
        def _(sp):
            for stage in plan:
                stage.sync(sp)
            store(sp)

        @block.gpsimd
        def _(g):
            for stage in plan:
                stage.gpsimd(g)

        @block.scalar
        def _(a):
            for stage in plan:
                stage.scalar(a)

        @block.vector
        def _(v):
            for stage in plan:
                stage.vector(v)

        @block.tensor
        def _(t):
            for stage in plan:
                stage.tensor(t)


_TRANSPOSED = [f"L{l}_xcond_W{k}" for l in (0, 1, 3) for k in "qkvo"] + ["L2_xcond_W_c", "L2_ffn_gate_w"]


def kernel(**inputs):
    import concourse.bacc as _bacc
    from concourse.bass_utils import run_bass_kernel_spmd as _run

    nc = _bacc.Bacc("TRN2", target_bir_lowering=False, num_devices=1)
    laid = {k: np.asarray(v) for k, v in inputs.items()}
    for k in _TRANSPOSED:
        laid[k] = laid[k].T
    laid["ctxT"] = laid["ctx_1024"].reshape(B * KEYS, D).T
    laid["condB_tau"] = laid["condB_tau"].reshape(1, B)
    laid["condB_pt"] = laid["condB_pt"].reshape(1, B)
    laid["_lenS2"] = laid["_lenS2"].reshape(1, B)
    laid["L2_ffn_b1"] = laid["L2_ffn_b1"].reshape(E, FC, P).transpose(0, 2, 1)
    arrays, io = {}, {}
    for name, a in laid.items():
        a = np.ascontiguousarray(a)
        arrays[f"in_{name}"] = a
        io[name] = nc.dram_tensor(f"in_{name}", a.shape, mybir.dt.from_np(a.dtype), kind="ExternalInput").ap()
    out = nc.dram_tensor("out_x", (B, SEQ, D), FP32, kind="ExternalOutput").ap()
    build(nc, io, out)
    r = _run(nc, [arrays], core_ids=[0])
    return r.results[0]["out_x"]
```

```python
import math
from contextlib import ExitStack

import numpy as np

import concourse.bass as bass
from concourse import mybir

FP32 = mybir.dt.float32
FP32R = mybir.dt.float32r
BF16 = mybir.dt.bfloat16
I32 = mybir.dt.int32
ALU = mybir.AluOpType
ACT = mybir.ActivationFunctionType
AX = mybir.AxisListType

P = 128
B, SEQ, D = 4, 512, 256
T = B * SEQ
TILES = T // P
TPB = SEQ // P
DC = D // P
HEADS, DK = 16, 16
HPC = HEADS // DC
PAIRS = HEADS // 2
KEYS = 64
E = 8
F = 1024
FC = F // P
FPAIRS = FC // 2
HID = 128
SHARED = 2
E_ALL = E + SHARED
SLOTS = 256
SB = SLOTS // P
KMAX = T // SLOTS
NT = (2 * T + E * (SLOTS - 1)) // SLOTS
BLOCKS = NT * SB
CAP = math.ceil(1.25 * T * 2 / E)
CAP3 = int(1.25 * ((T * 2 + E - 1) // E))
EPS = 1e-5
WINDOW, DEV_POW = 16.0, 128.0
BANK = 512
LOWEST = -3.0e38
ARENA = 15360


class Signal:

    def __init__(self, semaphore, base):
        self.sem, self.base = semaphore, base

    def __call__(self, n):
        return self.sem, self.base + n


class Chain:

    def __init__(self, eng, sig, base=0):
        self.eng, self.sig, self.base, self.n = eng, sig, base, 0

    def add(self, ins):
        self.n += 1
        ins.then_inc(self.sig.sem, 1)

    def wait(self):
        self.eng.wait_ge(*self.sig(self.base + self.n))

    def link(self, ins):
        self.add(ins)
        self.wait()


def wait_all(eng, waits):
    for semaphore_and_count in waits:
        eng.wait_ge(*semaphore_and_count)


class Stage:

    def __init__(self, sync, gpsimd, scalar, vector, tensor):
        self.sync, self.gpsimd, self.scalar, self.vector, self.tensor = sync, gpsimd, scalar, vector, tensor


def build(nc, io, out, stages=8):
    with ExitStack() as ctx:
        def sb(name, shape, dt=FP32):
            return ctx.enter_context(nc.sbuf_tensor(name, shape, dt))

        sems, begins = {}, {}

        def signal(name, total, first=1):
            if name not in sems:
                sems[name] = [ctx.enter_context(nc.semaphore(name)), first]
                begins[name] = first
            entry = sems[name]
            entry[1] += total
            return Signal(entry[0], entry[1] - total)

        x = sb("x", [P, TILES, D])
        ident = sb("ident", [P, P])
        ones_row = sb("ones_row", [1, P])
        before = sb("before", [P, P], BF16)
        ones_bf = sb("ones_bf", [P, P], BF16)
        head_of = sb("head_of", [P, HPC])
        rank_of = sb("rank_of", [P, E])
        key_no = sb("key_no", [P, KEYS])
        tile_no = sb("tile_no", [P, NT])
        step_no = sb("step_no", [P, KMAX])
        neg_half = sb("neg_half", [P, TPB])
        ctxT = sb("ctxT", [P, DC, B, 2, KEYS])
        tau_q = sb("tau_q", [P, B])
        delta_q = sb("delta_q", [33, B, KEYS])
        lo_no = sb("lo_no", [P, P], BF16)
        block_no = sb("block_no", [P, BLOCKS], BF16)
        row_no = sb("row_no", [P, 1])
        pair_tile_no = sb("pair_tile_no", [P, 2 * TILES])
        ids = sb("ids", [P, BLOCKS], I32)
        pair_rows = sb("pair_rows", [P, BLOCKS], I32)
        ids_now = sb("ids_now", [P, 2, SB], I32)
        rows_now = sb("rows_now", [P, 2, SB], I32)
        small = sb("small", [P, 16])
        stats = sb("stats", [P, TPB, 6])
        moments = sb("moments", [P, TPB, 2])
        var_eps = sb("var_eps", [P, TPB])
        rstd = sb("rstd", [P, TPB])
        scrap = sb("scrap", [P, 1])

        with ExitStack() as shared:
            def at_sb(name, shape, dt=FP32):
                return shared.enter_context(nc.sbuf_tensor(name, shape, dt))

            def both(name, *shape):
                names = "abcd"[:len(shape)]
                t = at_sb(name, [P, 2, int(np.prod(shape))], FP32R)
                if len(shape) == 1:
                    return [t[:, z, :] for z in range(2)]
                return [t[:, z, :].rearrange(f"p ({' '.join(names)}) -> p {' '.join(names)}",
                                             **dict(zip(names[1:], shape[1:]))) for z in range(2)]

            kbd = both("kbd", DC, B, HPC * KEYS)
            vbd = both("vbd", PAIRS * P)
            wp = [both(f"w{k}", DC, D) for k in "kvqo"]
            ctxp = both("ctx_parts", DC, B, 2, KEYS)
            pT = [both(f"probsT{k}", PAIRS, 2 * P) for k in range(2)]
            qT = [both(f"qT{k}", DC, 2 * P) for k in range(2)]
            xnT, hT = (both(k, DC, 2 * P) for k in ("xnT", "headsT"))
            vp = both("values", B, D)
            rows = at_sb("rows", [33, 4 * D], FP32R)
            ones33 = at_sb("ones33", [33, 2 * P], FP32R)
            rows_raw = at_sb("rows_raw", [33, 3 * D])
            w_raw_t = at_sb("w_raw", [P, 4, DC, D])
            w_raw = [w_raw_t[:, n] for n in range(4)]
            zero_one = at_sb("zero_one", [P, 2, 256])
            kt_t, kt_low_t = at_sb("kt", [P, DC, B * KEYS]), at_sb("kt_low", [P, DC, B * KEYS])
            kt_high_t = at_sb("kt_high", [P, DC, B * KEYS], FP32R)
            kt, kt_low, kt_high = kt_t[:, :, :], kt_low_t[:, :, :], kt_high_t[:, :, :]
            probs_t, top_t = at_sb("probs", [P, 2, HEADS * KEYS]), at_sb("top", [P, 2, HEADS])
            probs, top = ([z[:, n, :] for n in range(2)] for z in (probs_t, top_t))
            xnb_t = at_sb("xnb", [P, 2, 2, D])
            xnb = [xnb_t[:, n] for n in range(2)]
            total_t, inverse_t = at_sb("sums", [P, 2, HEADS]), at_sb("inverse", [P, 2, HEADS])
            total, inverse = ([z[:, n, :] for n in range(2)] for z in (total_t, inverse_t))

            y_back_t = at_sb("y_back", [P, 16, D])
            y_back = y_back_t[:, :, :]

        with ExitStack() as shared:
            def at_sb(name, shape, dt=FP32):
                return shared.enter_context(nc.sbuf_tensor(name, shape, dt))

            lo_hot = at_sb("lo_hot", [P, 2, TILES, P], BF16)
            block_hot = at_sb("block_hot", [P, 2, TILES, BLOCKS], BF16)
            block_value = at_sb("block_value", [P, 2, TILES, 2, BLOCKS], BF16)

        arena = sb("arena", [P, ARENA])

        def view(at, *shape, parts=P):
            n = int(np.prod(shape))
            v = arena[0:parts, at:at + n]
            if len(shape) == 1:
                return v
            names = "abcd"[:len(shape)]
            return v.rearrange(f"p ({' '.join(names)}) -> p {' '.join(names)}",
                               **dict(zip(names[1:], shape[1:])))

        w_parts = sb("w_parts", [P, 20480], FP32R)
        h_parts = sb("h_parts", [P, 8192], FP32R)
        xT_parts = sb("xT_parts", [P, 2048], FP32R)

        psum = ctx.enter_context(nc.psum_tensor("psum", [P, 8 * BANK], FP32))

        def bank(b, n=1):
            return psum[:, b * BANK:(b + n) * BANK]

        xn_rows = nc.dram_tensor("xn_scratch", (T, D), FP32).ap()
        ys = nc.dram_tensor("ys_scratch", (1 + 2 * T + NT * SLOTS, D), FP32).ap()

        IN_DMAS = 3 + 2 * DC
        s_in, s_x_in = signal("shared_inputs", 16 * IN_DMAS), signal("x_input", 16)
        s_memset, s_const = signal("memset", 8), signal("constants", 12)
        s_scaled = signal("scaled_inputs", 2)

        def sync(sp):
            for c in range(DC):
                for twice in range(2):
                    sp.dma_start(ctxT[:, c, :, twice, :], io["ctxT"][c * P:(c + 1) * P, :].rearrange("p (b k) -> p b k", b=B))\
                        .then_inc(s_in.sem, 16)
            sp.dma_start(tau_q[:, :], io["condB_tau"].to_broadcast([P, B])).then_inc(s_in.sem, 16)
            sp.wait_ge(*s_memset(8))
            for row in (0, 32):
                sp.dma_start(delta_q[row:row + 1, :, :], io["fside_BxS2_0"].rearrange("(o b) k -> o b k", o=1))\
                    .then_inc(s_in.sem, 16)

        def load_tokens(sp):
            sp.dma_start(x[:, :, :], io["x"].rearrange("b (t p) d -> p (b t) d", p=P)).then_inc(s_x_in.sem, 16)

        def gpsimd(g):
            for name, (semaphore, _) in sems.items():
                if begins[name]:
                    g.sem_inc(semaphore, begins[name])
            g.memset(delta_q[:, :, :], 0.0).then_inc(s_memset.sem, 1)
            g.memset(ident[:, :], 0.0).then_inc(s_memset.sem, 1)
            g.memset(before[:, :], 1.0).then_inc(s_memset.sem, 1)
            g.memset(head_of[:, :], 1.0).then_inc(s_memset.sem, 1)
            g.memset(ones_row[:, :], 1.0).then_inc(s_memset.sem, 1)
            g.memset(ones_bf[:, :], 1.0).then_inc(s_memset.sem, 1)
            g.memset(neg_half[:, :], -0.5).then_inc(s_memset.sem, 1)
            g.memset(small[:, :], 0.0).then_inc(s_memset.sem, 1)
            g.wait_ge(*s_memset(8))
            g.affine_select(out=ident[:, :], in_=ident[:, :], compare_op=ALU.not_equal, fill=1.0,
                            base=0, pattern=[[-1, P]], channel_multiplier=1).then_inc(s_const.sem, 1)
            g.affine_select(out=before[:, :], in_=before[:, :], compare_op=ALU.is_gt, fill=0.0,
                            base=0, pattern=[[1, P]], channel_multiplier=-1).then_inc(s_const.sem, 1)
            g.affine_select(out=head_of[:, :], in_=head_of[:, :], compare_op=ALU.is_ge, fill=0.0,
                            base=0, pattern=[[-DK, HPC]], channel_multiplier=1).then_inc(s_const.sem, 1)
            g.wait_ge(*s_const(3))
            g.affine_select(out=head_of[:, :], in_=head_of[:, :], compare_op=ALU.is_ge, fill=0.0,
                            base=DK - 1, pattern=[[DK, HPC]], channel_multiplier=-1).then_inc(s_const.sem, 1)
            g.iota(row_no[:, :], pattern=[[0, 1]], base=1, channel_multiplier=1,
                   allow_small_or_imprecise_dtypes=True).then_inc(s_const.sem, 1)
            for t, pattern, base in ((lo_no, [[1, P]], 0), (block_no, [[P, BLOCKS]], 0),
                                     (pair_tile_no, [[1, 2 * TILES]], 0), (rank_of, [[-1, E]], E), (key_no, [[1, KEYS]], 0),
                                     (tile_no, [[1, NT]], 0), (step_no, [[SLOTS, KMAX]], 0)):
                g.iota(t[:, :], pattern=pattern, base=base, channel_multiplier=0,
                       allow_small_or_imprecise_dtypes=True).then_inc(s_const.sem, 1)

        def vector(v):
            v.wait_ge(*s_in(IN_DMAS * 16))
            v.tensor_scalar(tau_q[:, :], tau_q[:, :], 1.0 / math.sqrt(DK), None, ALU.mult).then_inc(s_scaled.sem, 1)
            v.tensor_scalar(delta_q[:, :, :], delta_q[:, :, :], 1.0 / math.sqrt(DK), None, ALU.mult).then_inc(s_scaled.sem, 1)
            v.wait_ge(*s_scaled(2))
            v.wait_ge(*s_const(12))

        def tensor(t):
            t.wait_ge(*s_in(IN_DMAS * 16))
            t.wait_ge(*s_const(12))
            t.wait_ge(*s_scaled(2))

        def scalar(a):
            a.wait_ge(*s_in(IN_DMAS * 16))
            a.wait_ge(*s_scaled(2))
            a.wait_ge(*s_const(12))

        def nothing(eng):
            pass

        start = Stage(sync, gpsimd, scalar, vector, tensor)
        load_x = Stage(load_tokens, nothing, nothing, nothing, nothing)

        def norm_vector(v, ch, i, dst, s_var, s_rstd, s_norm):
            for j in range(TPB):
                ch.add(v.bn_stats(stats[:, j, :], tile_of(i, j)))
            ch.wait()
            v.memset(scrap[:, :], 0.0)
            for j in range(TPB):
                ch.add(v.bn_aggr(moments[:, j, :], stats[:, j, :]))
            ch.wait()
            v.tensor_scalar(var_eps[:, :], moments[:, :, 1], EPS, None, ALU.add).then_inc(s_var.sem, 1)
            v.wait_ge(*s_rstd(i + 1))
            for j in range(TPB):
                v.tensor_scalar(dst[:, j, :], tile_of(i, j), moments[:, j, 0:1], rstd[:, j:j + 1],
                                ALU.subtract, ALU.mult).then_inc(s_norm.sem, 1)

        def tile_of(i, j):
            return x[:, bass.ds(i * TPB + j, 1), :].rearrange("p a d -> p (a d)")

        def norm_gpsimd(g, i, s_var, s_rstd):
            g.wait_ge(*s_var(i + 1))
            g.tensor_tensor(rstd[:, :], var_eps[:, :], neg_half[:, :], ALU.pow).then_inc(s_rstd.sem, 1)

        UNIT = 2 * P
        UNITS = T // UNIT
        PASSES = ((0, 0), (0, 1), (1, 0))

        def attention(L, x_before, x_here=None, mixture=None):
            load, add, s_comb = mixture or (None, None, None)
            LINKS = 4 + 2
            io_w = {k: io[f"L{L}_xcond_W{k}"] for k in "kvqo"}

            s_w = signal("attn_weights", 11 * 16)
            s_rows0 = signal("attn_rows_cleared", 1)
            s_high = signal("attn_high_parts", 6 + 2)
            s_low = signal("attn_split", 6 + 2)
            s_rows = signal("attn_delta_row", 2)
            s_clear = signal("attn_values_cleared", 5)
            s_k_ps, s_v_ps = signal("attn_keys_in_psum", 1), signal("attn_values_in_psum", 1)
            s_kt, s_kbd = signal("attn_keys_scaled", DC), signal("attn_keys_spread", 2 * DC)
            s_kbd_later = signal("attn_keys_spread_later", 2 * DC * (B - 1))
            s_vbd = signal("attn_values_spread", 16 * B)
            s_ch = signal("attn_dve_chain", LINKS * UNITS)
            s_var, s_rstd, s_norm = signal("attn_variance", UNITS), signal("attn_rstd", UNITS), signal("attn_normed", TILES)
            s_xT_ps, s_xhi, s_xT = (signal(f"attn_xT_{k}", UNITS) for k in ("in_psum", "high", "split"))
            s_q_ps, s_qhi, s_q = (signal(f"attn_q_{k}", UNITS) for k in ("in_psum", "high", "split"))
            s_sc, s_sub, s_exp = signal("attn_scores", TILES), signal("attn_shifted", TILES), signal("attn_exp", TILES)
            s_pT_ps, s_phi, s_pT = (signal(f"attn_pT_{k}", 2 * TILES) for k in ("in_psum", "high", "split"))
            s_sum, s_inv = signal("attn_sums", TILES), signal("attn_inverse_sums", TILES)
            s_prob = signal("attn_probs", TILES)
            s_pv = signal("attn_pv", UNITS)
            s_hhi, s_hT = signal("attn_heads_high", UNITS), signal("attn_heads_split", UNITS)
            s_y, s_x = signal("attn_y", UNITS), signal("attn_x_updated", TILES)

            def pipeline(eng, step):
                for i in (-1, 0):
                    for k in range(2):
                        step(i, k)
                with eng.Fori(1, B - 1) as i:
                    for k in range(2):
                        step(i, k)
                for i in (B - 1, B):
                    for k in range(2):
                        step(i, k)

            def has(u):
                return not isinstance(u, int) or 0 <= u < UNITS

            def in_prologue(i):
                return isinstance(i, int) and i <= 0

            def first(i):
                return isinstance(i, int) and i == -1

            def none_if_first(n):
                return max(n, 0) if isinstance(n, int) else n

            def x_tile(n):
                return x[:, bass.ds(n, 1), :].rearrange("p a d -> p (a d)")

            def sync(sp):
                if x_before is not None:
                    wait_all(sp, x_before)
                for n, k in enumerate("kvqo"):
                    sp.dma_start(w_raw[n], io_w[k].rearrange("(c p) o -> p c o", p=P)).then_inc(s_w.sem, 16)
                sp.dma_start(small[:, 0:DC], io[f"L{L}_xcond_bk"].rearrange("(c p) -> p c", p=P),
                             allow_slow_non_contiguous=True).then_inc(s_w.sem, 16)
                sp.wait_ge(*s_rows0(1))
                for at in (0, 32):
                    for n, k in enumerate("qvo"):
                        sp.dma_start(rows_raw[at:at + 1, n * D:(n + 1) * D],
                                     io[f"L{L}_xcond_b{k}"].rearrange("(o d) -> o d", o=1)).then_inc(s_w.sem, 16)

                if mixture:
                    for u in range(UNITS):
                        load(sp, u)

            def gpsimd(g):
                if x_before is not None:
                    wait_all(g, x_before)
                g.memset(rows_raw[:, :], 0.0).then_inc(s_rows0.sem, 1)
                g.memset(zero_one[:, 0, :], 0.0).then_inc(s_clear.sem, 1)
                g.memset(zero_one[:, 1, :], 1.0).then_inc(s_clear.sem, 1)

                def step(i, k):
                    s = 2 * i + k - 1
                    if has(s):
                        normalise(s, 1)
                    if has(s + 3):
                        u = s + 3
                        g.wait_ge(*s_var(u + 1))
                        g.tensor_tensor(rstd[:, 0:2], var_eps[:, 0:2], neg_half[:, 0:2], ALU.pow).then_inc(s_rstd.sem, 1)
                    if first(i) and k == 1:
                        g.wait_ge(*s_low(7))
                        later_keys(1)
                    if has(s + 1):
                        normalise(s + 1, 0)
                    if isinstance(i, int) and i == 0 and k == 1:
                        for b in range(2, B):
                            later_keys(b)

                def later_keys(b):
                    for z in range(2):
                        for c in range(DC):
                            spread_keys(g, z, c, b).then_inc(s_kbd_later.sem, 1)

                def normalise(u, n):
                    tile = 2 * u + n
                    p = probs[n].rearrange("p (h k) -> p h k", k=KEYS)
                    g.wait_ge(*s_inv(tile + 1))
                    g.tensor_tensor(p, p, inverse[n].unsqueeze(2).to_broadcast([P, HEADS, KEYS]), ALU.mult)\
                        .then_inc(s_prob.sem, 1)

                pipeline(g, step)

            def spread_keys(eng, z, c, b):
                return eng.tensor_tensor(kbd[z][:, c, b, :].rearrange("p (h k) -> p h k", h=HPC),
                                         (kt_high, kt_low)[z].bitcast(FP32)[:, c, b * KEYS:(b + 1) * KEYS]
                                         .unsqueeze(1).to_broadcast([P, HPC, KEYS]),
                                         head_of[:, :].unsqueeze(2).to_broadcast([P, HPC, KEYS]), ALU.mult)

            def tensor(t_eng):
                t = t_eng
                t.wait_ge(*s_clear(3))
                t.wait_ge(*s_low(4))
                for oc in range(DC):
                    for kc in range(DC):
                        for a, b in PASSES:
                            ins = t.matmul(bank(0)[:, oc * 256:(oc + 1) * 256], wp[0][a][:, kc, oc * P:(oc + 1) * P],
                                           ctxp[b][:, kc, :, 0, :], start=(kc == 0 and (a, b) == (0, 0)),
                                           stop=(kc == DC - 1 and (a, b) == (1, 0)))
                ins.then_inc(s_k_ps.sem, 1)
                for b in range(B):
                    o = bank(2 + b // 2)[:, (b % 2) * 256:(b % 2 + 1) * 256]
                    for kc in range(DC):
                        for za, zb in PASSES:
                            t.matmul(o, ctxp[za][:, kc, b, :, :].rearrange("p two k -> p (two k)"), wp[1][zb][:, kc, :],
                                     start=(kc == 0 and (za, zb) == (0, 0)), stop=False)
                    ins = t.matmul(o, ones33[:, 0:P], rows[:, 2 * D:3 * D], start=False, stop=True)
                ins.then_inc(s_v_ps.sem, 1)

                def scores(i, k, n):
                    u, b = 2 * i + k, i
                    if n == 0:
                        t.wait_ge(*s_q(u + 1))
                        if k == 0:
                            if isinstance(i, int) and i == 0:
                                t.wait_ge(*s_kbd(2 * DC))
                            else:
                                t.wait_ge(*s_kbd_later(2 * DC * b))
                    t.wait_ge(*s_sub(2 * u + n))
                    for c in range(DC):
                        for za, zb in PASSES:
                            t.matmul(bank(c), qT[k % 2][za][:, c, n * P:(n + 1) * P],
                                     kbd[zb][:, c, bass.ds(b, 1), :].rearrange("p a n -> p (a n)"),
                                     start=(za, zb) == (0, 0), stop=False)
                        ins = t.matmul(bank(c), ones33[:, 0:P],
                                       rows[:, 0:D].rearrange("p (b k) -> p b k", b=B)[:, bass.ds(b, 1), :]
                                       .to_broadcast([33, HPC, KEYS]), start=False, stop=True)
                    ins.then_inc(s_sc.sem, 1)

                def transpose_probs(s, n):
                    tile = 2 * s + n
                    t.wait_ge(*s_prob(tile + 1))
                    for h in range(2):
                        t.wait_ge(*s_pT(none_if_first(2 * tile + h - 1)))
                        for c in range(4):
                            ins = t.transpose(bank(2 + h)[:, c * P:(c + 1) * P],
                                              probs[n][:, (4 * h + c) * P:(4 * h + c + 1) * P], ident[:, :])
                        ins.then_inc(s_pT_ps.sem, 1)

                def step(i, k):
                    s = 2 * i + k - 1
                    if has(s):
                        transpose_probs(s, 0)
                    if has(s - 1):
                        u = s - 1
                        t.wait_ge(*s_pT(4 * u + 4))
                        t.wait_ge(*s_vbd(16 * i))
                        t.wait_ge(*s_hT(u))
                        for c in range(DC):
                            o = bank(4)[:, c * UNIT:(c + 1) * UNIT]
                            for j in range(4):
                                for za, zb in PASSES:
                                    ins = t.matmul(o, vbd[za][:, (4 * c + j) * P:(4 * c + j + 1) * P],
                                                   pT[k % 2][zb][:, 4 * c + j, :],
                                                   start=(j == 0 and (za, zb) == (0, 0)), stop=(j == 3 and (za, zb) == (1, 0)))
                        ins.then_inc(s_pv.sem, 1)
                    if has(s + 1):
                        scores(i, k, 0)
                    if has(s + 2):
                        u = s + 2
                        if first(i) and k == 1:
                            t.wait_ge(*s_low(6))
                        t.wait_ge(*s_xT(u + 1))
                        t.wait_ge(*s_q(u))
                        for oc in range(DC):
                            o = bank(5)[:, oc * UNIT:(oc + 1) * UNIT]
                            for kc in range(DC):
                                for za, zb in PASSES:
                                    t.matmul(o, wp[2][za][:, kc, oc * P:(oc + 1) * P], xnT[zb][:, kc, :],
                                             start=(kc == 0 and (za, zb) == (0, 0)), stop=False)
                            ins = t.matmul(o, rows[:, D + oc * P:D + (oc + 1) * P], ones33[:, :], start=False, stop=True)
                        ins.then_inc(s_q_ps.sem, 1)
                    if has(s):
                        transpose_probs(s, 1)
                    if has(s + 1):
                        scores(i, k, 1)
                    if has(s + 3):
                        u = s + 3
                        t.wait_ge(*s_norm(2 * u + 2))
                        t.wait_ge(*s_xT(u))
                        for n in range(2):
                            for c in range(DC):
                                ins = t.transpose(bank(6)[:, c * UNIT + n * P:c * UNIT + (n + 1) * P],
                                                  xnb[k % 2][:, n, c * P:(c + 1) * P], ident[:, :])
                        ins.then_inc(s_xT_ps.sem, 1)
                    if has(s - 1):
                        u = s - 1
                        t.wait_ge(*s_hT(u + 1))
                        t.wait_ge(*s_x(2 * u))
                        for n in range(2):
                            o = bank(7)[:, n * D:(n + 1) * D]
                            for c in range(DC):
                                for za, zb in PASSES:
                                    t.matmul(o, hT[za][:, c, n * P:(n + 1) * P], wp[3][zb][:, c, :],
                                             start=(c == 0 and (za, zb) == (0, 0)), stop=False)
                            ins = t.matmul(o, ones33[:, 0:P], rows[:, 3 * D:4 * D], start=False, stop=True)
                        ins.then_inc(s_y.sem, 1)

                pipeline(t, step)

            def flat(z):
                return z.rearrange("p c n -> p (c n)")

            def scalar(a):
                if x_before is not None:
                    wait_all(a, x_before)
                a.copy(ctxp[0], ctxT[:, :, :, :, :]).then_inc(s_high.sem, 1)
                a.wait_ge(*s_clear(2))
                a.copy(ones33[:, :], zero_one[0:33, 1, :]).then_inc(s_clear.sem, 1)
                for z in range(2):
                    a.copy(vbd[z].rearrange("p (g n) -> p g n", g=4),
                           zero_one[:, 0, :].unsqueeze(1).to_broadcast([P, 4, 256])).then_inc(s_clear.sem, 1)
                a.wait_ge(*s_w(11 * 16))
                a.copy(rows[:, 0:D], delta_q[:, :, :].rearrange("p b k -> p (b k)")).then_inc(s_rows.sem, 1)
                a.copy(rows[:, D:4 * D], rows_raw[:, :]).then_inc(s_high.sem, 1)
                for n in range(4):
                    a.copy(wp[n][0], w_raw[n]).then_inc(s_high.sem, 1)
                a.wait_ge(*s_kt(DC))
                a.copy(kt_high, kt).then_inc(s_high.sem, 1)
                a.wait_ge(*s_v_ps(1))
                a.copy(vp[0], bank(2, 2).rearrange("p (b d) -> p b d", b=B)).then_inc(s_high.sem, 1)

                def spread_values(b):
                    for z in range(2):
                        of = vp[z][:, bass.ds(b, 1), :].rearrange("p a (c j two k) -> p (a c) j two k", c=DC, j=4, two=2)
                        to = vbd[z].rearrange("p (c j m) -> p c j m", c=DC, m=P)
                        for j in range(4):
                            for half in range(2):
                                keys, at = slice(64 * half, 64 * half + 64), (2 * j + half) * DK
                                a.copy(to[keys, :, j, at:at + DK], of[keys, :, j, half, :]).then_inc(s_vbd.sem, 1)

                def probs_high(s, k, n):
                    p, tile = (k - 1) % 2, 2 * s + n
                    if n == 0:
                        a.wait_ge(*s_pv(none_if_first(s - 1)))
                    for h in range(2):
                        a.wait_ge(*s_pT_ps(2 * tile + h + 1))
                        a.copy(pT[p][0][:, 4 * h:4 * h + 4, n * P:(n + 1) * P],
                               bank(2 + h).rearrange("p (c q) -> p c q", c=4)).then_inc(s_phi.sem, 1)

                def exp(u, n):
                    a.wait_ge(*s_sub(2 * u + n + 1))
                    a.activation(probs[n], probs[n], ACT.Exp).then_inc(s_exp.sem, 1)

                def step(i, k):
                    s = 2 * i + k - 1
                    if has(s):
                        probs_high(s, k, 0)
                    if has(s - 1):
                        u = s - 1
                        a.wait_ge(*s_pv(u + 1))
                        a.wait_ge(*s_y(u))
                        a.copy(flat(hT[0]), bank(4)).then_inc(s_hhi.sem, 1)
                    if k == 1 and has(s):
                        if has(s - 1):
                            a.wait_ge(*s_pv(s))
                        else:
                            a.wait_ge(*s_clear(5))
                            a.wait_ge(*s_high(8))
                            a.wait_ge(*s_low(8))
                        spread_values(i)
                    if has(s):
                        probs_high(s, k, 1)
                    if has(s + 1):
                        exp(s + 1, 0)
                    if has(s + 2):
                        u = s + 2
                        a.wait_ge(*s_q_ps(u + 1))
                        a.wait_ge(*s_sc(none_if_first(2 * u - 2)))
                        a.copy(flat(qT[(k - 1) % 2][0]), bank(5)).then_inc(s_qhi.sem, 1)
                    if has(s + 3):
                        u = s + 3
                        a.wait_ge(*s_xT_ps(u + 1))
                        a.wait_ge(*s_q_ps(u))
                        a.copy(flat(xnT[0]), bank(6)).then_inc(s_xhi.sem, 1)
                    if has(s + 1):
                        exp(s + 1, 1)

                pipeline(a, step)

            def vector(v):
                def low(dst, src, high):
                    return v.tensor_tensor(dst, src, high.bitcast(FP32), ALU.subtract)

                v.wait_ge(*s_high(1))
                low(ctxp[1], ctxT[:, :, :, :, :], ctxp[0]).then_inc(s_low.sem, 1)
                v.wait_ge(*s_high(2))
                low(rows[32:33, 0:D], delta_q[32:33, :, :].rearrange("p b k -> p (b k)"), rows[32:33, 0:D])\
                    .then_inc(s_rows.sem, 1)
                low(rows[32:33, D:4 * D], rows_raw[32:33, :], rows[32:33, D:4 * D]).then_inc(s_low.sem, 1)
                for n in range(4):
                    v.wait_ge(*s_high(n + 3))
                    low(wp[n][1], w_raw[n], wp[n][0]).then_inc(s_low.sem, 1)
                if x_here is not None:
                    v.wait_ge(*x_here)
                v.wait_ge(*s_k_ps(1))
                for oc in range(DC):
                    v.scalar_tensor_tensor(kt[:, oc, :].rearrange("p (b k) -> p b k", b=B),
                                           bank(0)[:, oc * 256:(oc + 1) * 256].rearrange("p (b k) -> p b k", b=B),
                                           small[:, oc:oc + 1], tau_q[:, :].unsqueeze(2).to_broadcast([P, B, KEYS]),
                                           ALU.add, ALU.mult).then_inc(s_kt.sem, 1)
                v.wait_ge(*s_high(7))
                low(kt_low, kt, kt_high).then_inc(s_low.sem, 1)
                v.wait_ge(*s_high(8))
                low(vp[1], bank(2, 2).rearrange("p (b d) -> p b d", b=B), vp[0]).then_inc(s_low.sem, 1)
                v.wait_ge(*s_low(7))

                def shift(s, k, n):
                    tile = 2 * (s + 1) + n
                    v.wait_ge(*s_sc(tile + 1))
                    sc = bank(0, 2).rearrange("p (h k) -> p h k", k=KEYS)
                    ch.link(v.reduce_max(top[n], sc, AX.X))
                    v.wait_ge(*s_pT_ps(none_if_first(2 * tile - 2)))
                    v.tensor_tensor(probs[n].rearrange("p (h k) -> p h k", k=KEYS), sc,
                                    top[n].unsqueeze(2).to_broadcast([P, HEADS, KEYS]), ALU.subtract)\
                        .then_inc(s_sub.sem, 1)

                def invert(u, n):
                    v.wait_ge(*s_exp(2 * u + n + 1))
                    v.reduce_sum(total[n], probs[n].rearrange("p (h k) -> p h k", k=KEYS), AX.X).then_inc(s_sum.sem, 1)
                    v.wait_ge(*s_sum(2 * u + n + 1))
                    v.reciprocal(inverse[n], total[n]).then_inc(s_inv.sem, 1)

                def probs_low(s, k, n):
                    p = (k - 1) % 2
                    for h in range(2):
                        v.wait_ge(*s_phi(2 * (2 * s + n) + h + 1))
                        low(pT[p][1][:, 4 * h:4 * h + 4, n * P:(n + 1) * P],
                            bank(2 + h).rearrange("p (c q) -> p c q", c=4),
                            pT[p][0][:, 4 * h:4 * h + 4, n * P:(n + 1) * P]).then_inc(s_pT.sem, 1)

                def step(i, k):
                    nonlocal ch
                    s = 2 * i + k - 1
                    ch = Chain(v, s_ch, chain_before(s))
                    if mixture and in_prologue(i):
                        for u in {-3: (0,), -2: (1, 2), -1: (3, 4, 5), 0: (6, 7)}[s]:
                            add(v, u)
                        v.wait_ge(*s_comb(ROWS * (s + 4 if s < 0 else UNITS)))
                    if has(s):
                        invert(s, 1)
                    if has(s):
                        probs_low(s, k, 0)
                    if has(s + 3):
                        u = s + 3
                        for n in range(2):
                            ch.add(v.bn_stats(stats[:, n, :], x_tile(2 * u + n)))
                    if has(s - 1):
                        v.wait_ge(*s_hhi(s))
                        low(flat(hT[1]), bank(4), flat(hT[0])).then_inc(s_hT.sem, 1)
                    if has(s + 3):
                        u = s + 3
                        ch.wait()
                        v.wait_ge(*s_norm(2 * u))
                        v.memset(scrap[:, :], 0.0)
                        for n in range(2):
                            ch.add(v.bn_aggr(moments[:, n, :], stats[:, n, :]))
                        ch.wait()
                        v.tensor_scalar(var_eps[:, 0:2], moments[:, 0:2, 1], EPS, None, ALU.add).then_inc(s_var.sem, 1)
                    if has(s + 1):
                        shift(s, k, 0)
                    if has(s + 3):
                        u = s + 3
                        v.wait_ge(*s_rstd(u + 1))
                        v.wait_ge(*s_xT_ps(none_if_first(u - 1)))
                        for n in range(2):
                            v.tensor_scalar(xnb[k % 2][:, n, :], x_tile(2 * u + n), moments[:, n, 0:1], rstd[:, n:n + 1],
                                            ALU.subtract, ALU.mult).then_inc(s_norm.sem, 1)
                    if first(i) and k == 1:
                        v.wait_ge(*s_low(7))
                        for z in range(2):
                            for c in range(DC):
                                spread_keys(v, z, c, 0).then_inc(s_kbd.sem, 1)
                    if has(s):
                        probs_low(s, k, 1)
                    if has(s + 1):
                        invert(s + 1, 0)
                    if has(s + 1):
                        shift(s, k, 1)
                    if has(s + 2):
                        u = s + 2
                        v.wait_ge(*s_qhi(u + 1))
                        low(flat(qT[(k - 1) % 2][1]), bank(5), flat(qT[(k - 1) % 2][0])).then_inc(s_q.sem, 1)
                    if has(s + 3):
                        u = s + 3
                        v.wait_ge(*s_xhi(u + 1))
                        low(flat(xnT[1]), bank(6), flat(xnT[0])).then_inc(s_xT.sem, 1)
                    if has(s - 1):
                        u = s - 1
                        v.wait_ge(*s_y(u + 1))
                        for n in range(2):
                            v.tensor_tensor(x_tile(2 * u + n), x_tile(2 * u + n), bank(7)[:, n * D:(n + 1) * D],
                                            ALU.add).then_inc(s_x.sem, 1)

                def chain_before(s):
                    return 4 * upto(s + 3) + 2 * upto(s + 1)

                def upto(n):
                    return min(max(n, 0), UNITS) if isinstance(n, int) else n

                ch = None
                pipeline(v, step)
                v.wait_ge(*s_x(TILES))

            return Stage(sync, gpsimd, scalar, vector, tensor), [s_x(TILES)]

        raw = [view(k * 2048, 2048) for k in range(3)]
        x_rows = view(6144, 2, SB, D)
        y_rows = view(7168, 2, SB, D)
        h_raw = view(8192, 2, 2 * SLOTS)
        h_gate = view(9216, 2, 2 * SLOTS)
        work = [view(7168 + k * TILES * E, TILES, E) for k in range(16)]
        route_xT = view(9216, 2, DC, SEQ)
        stats16, moments16 = view(0, TILES, 6), view(TILES * 6, TILES, 2)
        var_eps16, rstd16 = view(TILES * 8, TILES), view(TILES * 9, TILES)
        xn = view(11264, TILES, D)
        assert 11264 + TILES * D <= ARENA

        masks = sb("masks", [P, 2, TILES, E])
        masks_bf = sb("masks_bf", [P, 2, TILES, E], BF16)
        best = sb("best", [P, 2, TILES])
        gates = sb("gates", [P, TILES, E_ALL])
        slot_f = sb("slot_f", [P, 2, TILES])
        slot = sb("slot", [P, 2, TILES], I32)
        expert_f = sb("expert_f", [1, NT])
        expert = sb("expert", [1, NT], I32)
        counts = sb("counts", [P, 8, E])
        limit = sb("limit", [P, E], I32)
        tries = sb("tries", [P, 3, E], I32)
        tile_rows = [sb(f"tile_row{k}", [P, TILES]) for k in range(3)]
        router_w = sb("router_w", [P, DC, E])
        router_b = sb("router_b", [1, E])

        s_xn_out = signal("tokens_stored", 0)

        dense_weights_split = {}
        beside_router = {}

        def router(L, weight, bias, x_before):
            nonlocal s_xn_out
            s_xn_out = signal("tokens_stored", 16 if L != 1 else 0)
            SEARCH = 15 if L == 3 else 0
            s_w = signal("route_weights", 16 * (2 if bias is not None else 1))
            s_ch = signal(f"route_chain{L}", 0)
            s_var, s_rstd, s_norm = signal("variance", B), signal("rstd", B), signal("route_normed", TILES)
            s_xT_ps, s_xT = signal("route_xT_in_psum", B), signal("route_xT", 2 * B)
            s_lg_ps, s_lg = signal("route_logits_in_psum", B), signal("route_logits", 1)
            s_less, s_exp = signal("route_shifted", 1), signal("route_exp", 1)
            rounds = {0: 1, 1: 0, 2: 1, 3: SEARCH + 2}[L]
            s_mask, s_count = signal("route_masks", rounds), signal("route_counts", rounds)
            s_slot = signal("route_slots", 1)
            s_hot, s_ids_ps = signal("route_one_hot", 2 if L != 1 else 0), signal("route_ids_in_psum", 1 if L != 1 else 0)

            def sync(sp):
                wait_all(sp, x_before)
                sp.dma_start(router_w[:, :, :], weight.rearrange("(c p) e -> p c e", p=P)).then_inc(s_w.sem, 16)
                if bias is not None:
                    sp.dma_start(router_b[:, :], bias.rearrange("(o e) -> o e", o=1)).then_inc(s_w.sem, 16)
                if L != 1:
                    sp.wait_ge(*s_norm(TILES))
                    sp.dma_start(xn_rows.rearrange("(t p) d -> p t d", p=P), xn[:, :, :]).then_inc(s_xn_out.sem, 16)

            def of_batch(i):
                return slice(i * TPB, (i + 1) * TPB)

            def gpsimd(g):
                for i in range(B):
                    g.wait_ge(*s_var(i + 1))
                    g.tensor_tensor(rstd16[:, of_batch(i)], var_eps16[:, of_batch(i)], neg_half[:, :], ALU.pow)\
                        .then_inc(s_rstd.sem, 1)

            def tensor(t):
                t.wait_ge(*s_w(16 * (2 if bias is not None else 1)))
                wait_all(t, x_before)

                def logits(i):
                    t.wait_ge(*s_xT(2 * i + 2))
                    for j in range(TPB):
                        o = bank(4)[:, (TPB * i + j) * E:(TPB * i + j + 1) * E]
                        for c in range(DC):
                            ins = t.matmul(o, route_xT[:, i % 2, c, j * P:(j + 1) * P], router_w[:, c, :], start=(c == 0),
                                           stop=(c == DC - 1 and bias is None))
                        if bias is not None:
                            ins = t.matmul(o, ones_row[:, :], router_b[:, :], start=False, stop=True)
                    ins.then_inc(s_lg_ps.sem, 1)

                for i in range(B):
                    if i >= 2:
                        t.wait_ge(*s_xT(2 * i - 2))
                    for j in range(TPB):
                        t.wait_ge(*s_norm(TPB * i + j + 1))
                        for c in range(DC):
                            ins = t.transpose(bank(2 * (i % 2) + c)[:, j * P:(j + 1) * P],
                                              xn[:, TPB * i + j, c * P:(c + 1) * P], ident[:, :])
                    ins.then_inc(s_xT_ps.sem, 1)
                    if i >= 1:
                        logits(i - 1)
                logits(B - 1)
                if L == 1:
                    return
                t.wait_ge(*s_mask(1))
                t.matmul(bank(3)[:, 0:256], before[:, :], masks_bf[:, :, :, :], start=True, stop=True)
                t.matmul(bank(4)[:, 0:256], ones_bf[:, :], masks_bf[:, :, :, :],
                         start=True, stop=True).then_inc(s_count.sem, 1)
                for c in range(2):
                    t.wait_ge(*s_hot(c + 1))
                    for n in range(TILES):
                        ins = t.matmul(bank(5)[:, 0:2 * BLOCKS], lo_hot[:, c, n, :],
                                       block_value[:, c, n, :, :].rearrange("p v b -> p (v b)"),
                                       start=(c == 0 and n == 0), stop=(c == 1 and n == TILES - 1))
                ins.then_inc(s_ids_ps.sem, 1)
                for n in range(SEARCH):
                    t.wait_ge(*s_mask(n + 2))
                    t.matmul(bank(5)[:, 0:3 * E], ones_bf[:, :], masks_bf[:, 0, 0:3, :],
                             start=True, stop=True).then_inc(s_count.sem, 1)
                if SEARCH:
                    t.wait_ge(*s_mask(SEARCH + 2))
                    t.matmul(bank(3)[:, 0:256], before[:, :], masks_bf[:, :, :, :], start=True, stop=True)
                    t.matmul(bank(4)[:, 0:256], ones_bf[:, :], masks_bf[:, :, :, :],
                             start=True, stop=True).then_inc(s_count.sem, 1)

            def scalar(a):
                for i in range(B):
                    a.wait_ge(*s_xT_ps(i + 1))
                    if i >= 2:
                        a.wait_ge(*s_lg_ps(i - 1))
                    for c in range(DC):
                        a.copy(route_xT[:, i % 2, c, :], bank(2 * (i % 2) + c)).then_inc(s_xT.sem, 1)
                if L == 1:
                    beside_router["scalar"](a)
                a.wait_ge(*s_less(1))
                if L == 1:
                    a.activation(tile_rows[0][:, :], tile_rows[0][:, :], ACT.Exp).then_inc(s_exp.sem, 1)
                else:
                    a.activation(work[0], work[0], ACT.Exp).then_inc(s_exp.sem, 1)

            def per_tile(row):
                return row.unsqueeze(2).to_broadcast([P, TILES, E])

            def vector(v):
                ch = Chain(v, s_ch)

                def moments_of(i):
                    for n in range(TPB * i, TPB * i + TPB):
                        ch.add(v.bn_stats(stats16[:, n, :], x[:, n, :]))
                    ch.wait()
                    for n in range(TPB * i, TPB * i + TPB):
                        ch.add(v.bn_aggr(moments16[:, n, :], stats16[:, n, :]))
                    ch.wait()
                    v.tensor_scalar(var_eps16[:, of_batch(i)], moments16[:, of_batch(i), 1], EPS, None, ALU.add).then_inc(s_var.sem, 1)

                moments_of(0)
                for i in range(B):
                    if i + 1 < B:
                        moments_of(i + 1)
                    v.wait_ge(*s_rstd(i + 1))
                    for n in range(TPB * i, TPB * i + TPB):
                        v.tensor_scalar(xn[:, n, :], x[:, n, :], moments16[:, n, 0:1], rstd16[:, n:n + 1],
                                        ALU.subtract, ALU.mult).then_inc(s_norm.sem, 1)
                values, hit, ranked, second = work[0], work[1], work[2], work[3]
                if L == 1:
                    beside_router["vector"](v)
                v.wait_ge(*s_lg_ps(B))
                v.tensor_copy(values, bank(4)[:, 0:TILES * E].rearrange("p (j e) -> p j e", e=E)).then_inc(s_lg.sem, 1)
                v.wait_ge(*s_lg(1))
                top_row, rank_row, sum_row = (r[:, :] for r in tile_rows)
                if L != 1:
                    ch.link(v.reduce_max(top_row, values, AX.X))
                    v.tensor_tensor(values, values, per_tile(top_row), ALU.subtract).then_inc(s_less.sem, 1)
                    v.wait_ge(*s_exp(1))
                    ch.link(v.reduce_sum(sum_row, values, AX.X))
                    ch.link(v.reciprocal(rank_row, sum_row))
                    ch.link(v.tensor_tensor(values, values, per_tile(rank_row), ALU.mult))
                for c in range(2):
                    source = values if c == 0 else second
                    ch.link(v.reduce_max(best[:, c, :], source, AX.X))
                    ch.link(v.tensor_tensor(hit, source, per_tile(best[:, c, :]), ALU.is_equal))
                    ch.link(v.tensor_tensor(ranked, hit, rank_of[:, :].unsqueeze(1).to_broadcast([P, TILES, E]), ALU.mult))
                    ch.link(v.reduce_max(rank_row, ranked, AX.X))
                    ch.link(v.tensor_tensor(masks[:, c, :, :], ranked, per_tile(rank_row), ALU.is_equal))
                    if c == 0:
                        ch.link(v.scalar_tensor_tensor(second, masks[:, 0, :, :], LOWEST, values, ALU.mult, ALU.add))
                if L in (0, 3):
                    ch.link(v.tensor_tensor(sum_row, best[:, 0, :], best[:, 1, :], ALU.add))
                    if L == 3:
                        ch.link(v.tensor_scalar(sum_row, sum_row, 1e-9, None, ALU.add))
                    ch.link(v.reciprocal(rank_row, sum_row))
                    ch.link(v.tensor_tensor(best[:, :, :], best[:, :, :],
                                            rank_row.unsqueeze(1).to_broadcast([P, 2, TILES]), ALU.mult))
                if L == 1:
                    v.tensor_tensor(top_row, best[:, 1, :], best[:, 0, :], ALU.subtract).then_inc(s_less.sem, 1)
                    v.wait_ge(*s_exp(1))
                    ch.link(v.tensor_scalar(sum_row, top_row, 1.0, None, ALU.add))
                    ch.link(v.reciprocal(best[:, 0, :], sum_row))
                    ch.link(v.tensor_tensor(best[:, 1, :], best[:, 0, :], top_row, ALU.mult))
                if L in (1, 3):
                    for c in range(2):
                        ch.link(v.tensor_tensor(work[4 + c], masks[:, c, :, :], per_tile(best[:, c, :]), ALU.mult))
                if L == 3:
                    ch.link(v.tensor_tensor(work[4], work[4], work[5], ALU.add))
                if L == 1:
                    ch.link(v.memset(gates[:, :, :], 1.0))
                    v.tensor_tensor(gates[:, :, 0:E], work[4], work[5], ALU.add).then_inc(s_slot.sem, 1)
                    v.wait_ge(*s_slot(1))
                    return

                def over_tiles():
                    a, b = (view(7168 + k * TILES * E, 2, TILES, E) for k in (8, 10))
                    ch.link(v.tensor_copy(a, bank(4)[:, 0:256].rearrange("p (c t e) -> p c t e", c=2, e=E)))
                    step = 1
                    while step < TILES:
                        ch.add(v.tensor_copy(b[:, :, 0:step, :], a[:, :, 0:step, :]))
                        ch.link(v.tensor_tensor(b[:, :, step:, :], a[:, :, step:, :], a[:, :, :TILES - step, :], ALU.add))
                        a, b = b, a
                        step *= 2
                    ch.link(v.tensor_tensor(b, a, bank(4)[:, 0:256].rearrange("p (c t e) -> p c t e", c=2, e=E), ALU.subtract))
                    ch.link(v.tensor_tensor(b, b, bank(3)[:, 0:256].rearrange("p (c t e) -> p c t e", c=2, e=E), ALU.add))
                    return a, b

                v.tensor_copy(masks_bf[:, :, :, :], masks[:, :, :, :]).then_inc(s_mask.sem, 1)
                v.wait_ge(*s_count(1))
                total, place = over_tiles()
                picked = view(7168 + 12 * TILES * E, 2, TILES, E)
                number, tiles, end, other, first = (counts[:, k, :] for k in range(5))
                ch.link(v.tensor_tensor(number, total[:, 0, TILES - 1, :], total[:, 1, TILES - 1, :], ALU.add))
                more = work[0].rearrange("p t e -> p (t e)")[:, 0:E * KMAX].rearrange("p (e k) -> p e k", k=KMAX)
                ch.link(v.tensor_tensor(more, number.unsqueeze(2).to_broadcast([P, E, KMAX]),
                                        step_no[:, :].unsqueeze(1).to_broadcast([P, E, KMAX]), ALU.is_gt))
                ch.link(v.reduce_sum(tiles, more, AX.X))
                ch.link(v.tensor_copy(end, tiles))
                a, b = end, other
                for step in (1, 2, 4):
                    ch.add(v.tensor_copy(b[:, 0:step], a[:, 0:step]))
                    ch.link(v.tensor_tensor(b[:, step:], a[:, step:], a[:, :E - step], ALU.add))
                    a, b = b, a
                end = a
                ch.link(v.tensor_tensor(first, end, tiles, ALU.subtract))
                ch.link(v.tensor_scalar(first, first, float(SLOTS), None, ALU.mult))
                ch.link(v.tensor_tensor(work[1], place[:, 0, :, :], place[:, 1, :, :], ALU.add))
                ch.link(v.tensor_tensor(work[2], work[1], first.unsqueeze(1).to_broadcast([P, TILES, E]), ALU.add))
                ch.link(v.tensor_tensor(picked, masks[:, :, :, :], work[2].unsqueeze(1).to_broadcast([P, 2, TILES, E]), ALU.mult))
                ch.link(v.reduce_sum(slot_f[:, :, :], picked, AX.X))
                ch.link(v.tensor_copy(slot[:, :, :], slot_f[:, :, :]))
                low_i = work[4 if L != 3 else 5].rearrange("p t e -> p (t e)")[:, 0:2 * TILES]
                low_f = work[2].rearrange("p t e -> p (t e)")[:, 0:2 * TILES]
                block_f = work[2].rearrange("p t e -> p (t e)")[:, 2 * TILES:4 * TILES]
                flat_slot = slot[:, :, :].rearrange("p c t -> p (c t)")
                ch.link(v.tensor_scalar(low_i.bitcast(I32), flat_slot, P - 1, None, ALU.bitwise_and))
                ch.link(v.tensor_copy(low_f, low_i.bitcast(I32)))
                ch.link(v.tensor_tensor(block_f, slot_f[:, :, :].rearrange("p c t -> p (c t)"), low_f, ALU.subtract))
                for c in range(2):
                    of = slice(c * TILES, (c + 1) * TILES)
                    ch.link(v.tensor_tensor(block_hot[:, c, :, :], block_f[:, of].unsqueeze(2).to_broadcast([P, TILES, BLOCKS]),
                                            block_no[:, :].unsqueeze(1).to_broadcast([P, TILES, BLOCKS]), ALU.is_equal))
                    ch.add(v.tensor_scalar(block_value[:, c, :, 0, :], block_hot[:, c, :, :], row_no[:, 0:1], None, ALU.mult))
                    ch.add(v.tensor_tensor(block_value[:, c, :, 1, :], block_hot[:, c, :, :],
                                           pair_tile_no[:, of].unsqueeze(2).to_broadcast([P, TILES, BLOCKS]), ALU.mult))
                    ch.wait()
                    v.tensor_tensor(lo_hot[:, c, :, :], low_f[:, of].unsqueeze(2).to_broadcast([P, TILES, P]),
                                    lo_no[:, :].unsqueeze(1).to_broadcast([P, TILES, P]), ALU.is_equal).then_inc(s_hot.sem, 1)
                ended = view(7168, NT, E, parts=1)
                ch.link(v.tensor_tensor(ended, end[0:1, :].unsqueeze(1).to_broadcast([1, NT, E]),
                                        tile_no[0:1, :].unsqueeze(2).to_broadcast([1, NT, E]), ALU.is_le))
                ch.link(v.reduce_sum(expert_f[:, :], ended, AX.X))
                ch.link(v.tensor_scalar(expert[:, :], expert_f[:, :], float(E - 1), None, ALU.min))
                v.wait_ge(*s_ids_ps(1))
                tile_part = work[3].rearrange("p t e -> p (t e)")[:, 0:BLOCKS]
                ch.link(v.tensor_copy(tile_part, bank(5)[:, BLOCKS:2 * BLOCKS]))
                pair_f, unused, spare = (work[k].rearrange("p t e -> p (t e)")[:, 0:BLOCKS] for k in (0, 1, 2))
                ch.link(v.scalar_tensor_tensor(pair_f, tile_part, float(P), bank(5)[:, 0:BLOCKS], ALU.mult, ALU.add))
                ch.link(v.tensor_scalar(unused, pair_f, 0.5, None, ALU.is_lt))
                ch.add(v.tensor_scalar(spare, block_no[:, :], row_no[:, 0:1], float(2 * T), ALU.add, ALU.add))
                ch.wait()
                ch.link(v.tensor_tensor(spare, spare, unused, ALU.mult))
                ch.link(v.tensor_tensor(pair_rows[:, :], spare, pair_f, ALU.add))
                ch.link(v.tensor_scalar(unused, pair_f, T + 0.5, float(-T), ALU.is_gt, ALU.mult))
                ch.link(v.scalar_tensor_tensor(pair_f, pair_f, -1.0, unused, ALU.add, ALU.add))
                v.tensor_scalar(ids[:, :], pair_f, 0.0, None, ALU.max).then_inc(s_slot.sem, 1)
                v.wait_ge(*s_slot(1))
                if L == 2:
                    kept = view(7168 + 12 * TILES * E, 2, TILES, E)
                    ch.link(v.tensor_tensor(kept, masks[:, :, :, :], place, ALU.mult))
                    ch.link(v.reduce_sum(slot_f[:, :, :], kept, AX.X))
                    ch.link(v.scalar_tensor_tensor(best[:, :, :], slot_f[:, :, :], CAP - 0.5, best[:, :, :], ALU.is_lt, ALU.mult))
                if L == 3:
                    gate, over, at_limit = work[4], work[6], work[7]
                    ch.link(v.memset(limit[:, :], 0))
                    passed = view(7168 + 8 * TILES * E, 3, TILES, E)
                    for n in range(SEARCH):
                        shift = 2 * (SEARCH - 1 - n)
                        for k in range(3):
                            ch.add(v.tensor_scalar(tries[:, k, :], limit[:, :], (k + 1) << shift, None, ALU.bitwise_or))
                        ch.wait()
                        ch.link(v.tensor_tensor(passed, gate.unsqueeze(1).to_broadcast([P, 3, TILES, E]),
                                                tries[:, :, :].bitcast(FP32).unsqueeze(2).to_broadcast([P, 3, TILES, E]),
                                                ALU.is_ge))
                        with nc.allow_low_precision("whole numbers up to 16"):
                            v.reduce_sum(masks_bf[:, 0, 0:3, :], passed.rearrange("p k t e -> p k e t"), AX.X)\
                                .then_inc(s_mask.sem, 1)
                        v.wait_ge(*s_count(n + 2))
                        ch.link(v.tensor_scalar(counts[:, 0:3, :], bank(5)[:, 0:3 * E].rearrange("p (k e) -> p k e", e=E),
                                                CAP3 - 0.5, float(1 << shift), ALU.is_gt, ALU.mult))
                        with nc.allow_low_precision("one of four multiples of a power of two"):
                            ch.link(v.reduce_sum(tries[:, 0, :], counts[:, 0:3, :].rearrange("p k e -> p e k"), AX.X))
                        ch.link(v.tensor_tensor(limit[:, :], limit[:, :], tries[:, 0, :], ALU.bitwise_or))
                    limit_f = limit[:, :].bitcast(FP32).unsqueeze(1).to_broadcast([P, TILES, E])
                    ch.add(v.tensor_tensor(over, gate, limit_f, ALU.is_gt))
                    ch.link(v.tensor_tensor(at_limit, gate, limit_f, ALU.is_equal))
                    ch.add(v.tensor_copy(masks_bf[:, 0, :, :], over))
                    v.tensor_copy(masks_bf[:, 1, :, :], at_limit).then_inc(s_mask.sem, 1)
                    v.wait_ge(*s_count(SEARCH + 2))
                    total, place = over_tiles()
                    room = counts[:, 0, :]
                    ch.link(v.tensor_scalar(room, total[:, 0, TILES - 1, :], -1.0, float(CAP3), ALU.mult, ALU.add))
                    ch.link(v.tensor_tensor(work[3], place[:, 1, :, :], room.unsqueeze(1).to_broadcast([P, TILES, E]), ALU.is_lt))
                    ch.link(v.tensor_tensor(work[5], work[3], at_limit, ALU.mult))
                    ch.link(v.tensor_tensor(work[3], work[5], over, ALU.add))
                    kept = view(7168 + 12 * TILES * E, 2, TILES, E)
                    ch.link(v.tensor_tensor(kept, masks[:, :, :, :], work[3].unsqueeze(1).to_broadcast([P, 2, TILES, E]), ALU.mult))
                    ch.link(v.reduce_sum(slot_f[:, :, :], kept, AX.X))
                    ch.link(v.tensor_tensor(best[:, :, :], best[:, :, :], slot_f[:, :, :], ALU.mult))


            return Stage(sync, gpsimd, scalar, vector, tensor), [s_slot(1)]

        def moe(L, kind, w1, w2, w3=None, b1=None, b2=None, routed=None):
            lead = 0 if w3 is not None else 1
            w_ins = [w1] + ([w3] if w3 is not None else [])
            n_in = len(w_ins)
            def parts(k):
                v = w_parts[:, k * 2048:(k + 1) * 2048]
                return v
            in_parts = [[[parts(4 * m + 2 * u + q).rearrange("p (c f) -> p c f", c=DC) for q in range(2)]
                         for u in range(2)] for m in range(n_in)]
            out_parts = [[parts(4 * n_in + 2 * u + q).rearrange("p (c o) -> p c o", c=FC) for q in range(2)]
                         for u in range(lead + 1)]
            h_part = [[h_parts[:, (2 * u + q) * 2048:(2 * u + q + 1) * 2048].rearrange("p (c s) -> p c s", c=FC)
                       for q in range(2)] for u in range(2)]
            x_part = [[xT_parts[:, (2 * u + q) * 512:(2 * u + q + 1) * 512].rearrange("p (c s) -> p c s", c=DC)
                       for q in range(2)] for u in range(2)]
            quarters2 = ((0,), (1,), (2,), (3,)) if lead else ((0, 1, 2, 3), (), (), ())
            quarters = ((0,), (1,), (2, 3), ())
            half = [(NT + 1 - u) // 2 for u in range(2)]

            tokens_stored = s_xn_out
            s_raw = [[signal(f"moe_raw{m}_half{h}", 16 * NT) for h in range(2)] for m in range(n_in)]
            s_raw2 = [signal(f"moe_raw_w2_half{h}", 16 * NT) for h in range(2)]
            s_xin = [signal(f"moe_x_in{u}", 16 * SB * half[u], first=0) for u in range(2)]
            s_now, s_here = signal("moe_ids_now", NT), signal("moe_ids_here", NT)
            s_b1 = [signal(f"moe_b1_in{u}", 16 * half[u]) for u in range(2)] if b1 is not None else None
            s_b2 = [signal(f"moe_b2_in{u}", 16 * half[u]) for u in range(2)] if b2 is not None else None
            s_hi = [signal(f"moe_w_high{m}", 4 * NT) for m in range(n_in)]
            s_hi2 = signal("moe_w2_high", 4 * NT)
            s_split = [signal(f"moe_w_split{m}", 2 * NT, first=2) for m in range(n_in)]
            s_split2 = signal("moe_w2_split", 2 * NT, first=2)
            s_xT_ps = [signal(f"moe_xT_in_psum{u}", half[u]) for u in range(2)]
            s_xhi, s_xsplit = signal("moe_x_high", NT), signal("moe_x_split", NT)
            s_hps = signal("moe_h_in_psum", FPAIRS * NT)
            s_act = signal("moe_activated", FPAIRS * NT)
            s_gated = signal("moe_gated", FPAIRS * NT if kind == "swiglu" else 0)
            s_hhi, s_hsplit = signal("moe_h_high", FPAIRS * NT), signal("moe_h_split", FPAIRS * NT)
            s_mm2 = [signal(f"moe_mm2{u}", half[u]) for u in range(2)]
            s_y = [signal(f"moe_y_in_sbuf{u}", half[u]) for u in range(2)]
            s_stored = [signal(f"moe_y_stored{u}", 16 * SB * half[u], first=0) for u in range(2)]
            s_rows, s_rows_here = signal("moe_rows_now", NT), signal("moe_rows_here", NT)
            s_yfree = [signal(f"moe_y_buffer_free{u}", half[u]) for u in range(2)]

            def none_if_first(n):
                return max(n, 0) if isinstance(n, int) else n

            def exists(t):
                return not isinstance(t, int) or 0 <= t < NT

            def tiles(eng, step):
                pairs = (NT - 2) // 2
                for t in range(2):
                    step(t, t, 0)
                with eng.Fori(1, pairs) as it:
                    step(2 * it, 0, it)
                    step(2 * it + 1, 1, it)
                for t in range(2 * pairs, NT):
                    step(t, t % 2, t // 2)

            def sync(sp):
                wait_all(sp, routed)

                def expert_of(t):
                    return sp.value_load(expert[0:1, bass.ds(t, 1)] if not isinstance(t, int) else expert[0:1, t:t + 1],
                                         min_val=0, max_val=E - 1)

                def load_in(t, e, h):
                    for m in range(n_in):
                        sp.wait_ge(*s_split[m](none_if_first(2 * t - 1 + h)))
                        sp.dma_start(raw[m][:, h * F:(h + 1) * F],
                                     w_ins[m][bass.ds(e, 1), h * P:(h + 1) * P, :].rearrange("a p f -> p (a f)"))\
                            .then_inc(s_raw[m][h].sem, 16)

                def load_out(t, e, h):
                    sp.wait_ge(*s_split2(none_if_first(2 * t - 1 + h)))
                    sp.dma_start(raw[2][:, h * F:(h + 1) * F].rearrange("p (c o) -> p c o", c=FC // 2),
                                 w2[bass.ds(e, 1), h * F // 2:(h + 1) * F // 2, :].rearrange("a (c p) o -> p (a c) o", p=P))\
                        .then_inc(s_raw2[h].sem, 16)

                def load_b1(t, u, it, e):
                    if b1 is not None:
                        if not isinstance(t, int) or t > 1:
                            sp.wait_ge(*s_act(FPAIRS * (t - 1)))
                        sp.dma_start(b1_buf[:, u, :], b1[bass.ds(e, 1), :, :].rearrange("a p c -> p (a c)"))\
                            .then_inc(s_b1[u].sem, 16)

                def load_b2(t, u, it):
                    if b2 is not None:
                        e = expert_of(t)
                        sp.wait_ge(*s_mm2[u](it))
                        sp.dma_start(b2_buf[:, u, :], b2[bass.ds(e, 1), :]).then_inc(s_b2[u].sem, 16)

                for t in range(3):
                    if t > 0 and t - 1 < 1 + lead:
                        e = expert_of(t - 1)
                        for h in range(2):
                            load_out(t - 1, e, h)
                    e = expert_of(t)
                    for h in range(2):
                        load_in(t, e, h)
                    load_b1(t, t % 2, t // 2, e)
                load_b2(0, 0, 0)

                def step(t, u, it):
                    if exists(t + 1 + lead):
                        e_out = expert_of(t + 1 + lead)
                    if exists(t + 3):
                        e_in = expert_of(t + 3)
                    for h in range(2):
                        if exists(t + 1 + lead):
                            load_out(t + 1 + lead, e_out, h)
                        if exists(t + 3):
                            load_in(t + 3, e_in, h)
                        if h == 0 and exists(t + 1):
                            load_b2(t + 1, 1 - u, it + u)
                    if exists(t + 3):
                        load_b1(t + 3, 1 - u, it + 1 + u, e_in)

                tiles(sp, step)

            def gpsimd(g):
                wait_all(g, routed)
                g.wait_ge(*tokens_stored(16))

                def gather(t, u, it):
                    g.wait_ge(*s_xT_ps[u](it))
                    g.wait_ge(*s_xin[u](16 * SB * it))
                    g.tensor_copy(ids_now[:, u, :], ids[:, bass.ds(t * SB, SB)]).then_inc(s_now.sem, 1)
                    g.wait_ge(*s_now(t + 1))
                    g.sem_inc(s_here.sem, 1)
                    for n in range(SB):
                        g.indirect_dma_start(out=x_rows[:, u, n, :], out_offset=None, in_=xn_rows,
                                             in_offset=bass.IndirectOffsetOnAxis(ap=ids_now[:, u, n:n + 1], axis=0))\
                            .then_inc(s_xin[u].sem, 16)

                for t in range(3):
                    gather(t, t % 2, t // 2)

                def step(t, u, it):
                    if exists(t + 3):
                        gather(t + 3, 1 - u, it + 1 + u)
                    g.wait_ge(*s_y[u](it + 1))
                    g.tensor_copy(rows_now[:, u, :], pair_rows[:, bass.ds(t * SB, SB)]).then_inc(s_rows.sem, 1)
                    g.wait_ge(*s_rows(t + 1))
                    g.sem_inc(s_rows_here.sem, 1)
                    for n in range(SB):
                        g.indirect_dma_start(out=ys, out_offset=bass.IndirectOffsetOnAxis(ap=rows_now[:, u, n:n + 1], axis=0),
                                             in_=y_rows[:, u, n, :], in_offset=None).then_inc(s_stored[u].sem, 16)
                    g.wait_ge(*s_stored[u](16 * SB * (it + 1)))
                    g.sem_inc(s_yfree[u].sem, 1)

                tiles(g, step)
            def tensor(t_eng):
                def product(o, pairs, first, last):
                    (ah, al), (bh, bl) = pairs
                    t_eng.matmul(o, ah, bh, start=first, stop=False)
                    t_eng.matmul(o, ah, bl, start=False, stop=False)
                    return t_eng.matmul(o, al, bh, start=False, stop=last)

                def transposes(t, u, it):
                    t_eng.wait_ge(*s_xin[u](16 * SB * (it + 1)))
                    if b1 is not None:
                        t_eng.wait_ge(*s_b1[u](16 * (it + 1)))
                    t_eng.wait_ge(*s_xsplit(t))
                    for s in range(SB):
                        for c in range(DC):
                            o = bank(6)[:, c * SLOTS + s * P:c * SLOTS + (s + 1) * P]
                            ins = t_eng.transpose(o, x_rows[:, u, s, c * P:(c + 1) * P], ident[:, :])
                    ins.then_inc(s_xT_ps[u].sem, 1)

                def hidden(t, u, it):
                    for m in range(n_in):
                        t_eng.wait_ge(*s_split[m](2 * t + 2))
                    t_eng.wait_ge(*s_xsplit(t + 1))
                    for p in range(FPAIRS):
                        for m in range(n_in):
                            k = p if n_in == 1 else 2 * m + p % 2
                            if n_in == 1 and (not isinstance(t, int) or t > 0):
                                t_eng.wait_ge(*s_act(FPAIRS * (t - 1) + p + 1))
                            if n_in == 2 and (not isinstance(t, int) or t > 0 or p >= 2):
                                t_eng.wait_ge(*(s_act, s_gated)[m](FPAIRS * t + p - 1))
                            for q in range(2):
                                f = 2 * p + q
                                for c in range(DC):
                                    ins = product(bank(k)[:, q * SLOTS:(q + 1) * SLOTS],
                                                  ([in_parts[m][u][z][:, c, f * P:(f + 1) * P] for z in range(2)],
                                                   [x_part[u][z][:, c, :] for z in range(2)]), c == 0, c == DC - 1)
                        ins.then_inc(s_hps.sem, 1)

                def output(t, u, it):
                    t_eng.wait_ge(*s_split2(2 * t + 2))
                    t_eng.wait_ge(*s_y[u](it))
                    if b2 is not None:
                        t_eng.wait_ge(*s_b2[u](16 * (it + 1)))
                    for s in range(SB):
                        o = bank(4 + u)[:, s * D:(s + 1) * D]
                        for f in range(FC):
                            if s == 0 and f % 2 == 0:
                                t_eng.wait_ge(*s_hsplit(FPAIRS * t + f // 2 + 1))
                            ins = product(o, ([h_part[u][z][:, f, s * P:(s + 1) * P] for z in range(2)],
                                              [out_parts[u * lead][z][:, f, :] for z in range(2)]),
                                          f == 0, f == FC - 1 and b2 is None)
                        if b2 is not None:
                            ins = t_eng.matmul(o, ones_row[:, :], b2_buf[:, u, :], start=False, stop=True)
                    ins.then_inc(s_mm2[u].sem, 1)

                transposes(0, 0, 0)
                hidden(0, 0, 0)
                transposes(1, 1, 0)

                def step(t, u, it):
                    if exists(t + 1):
                        hidden(t + 1, 1 - u, it + u)
                    if exists(t + 2):
                        transposes(t + 2, u, it + 1)
                    output(t, u, it)

                tiles(t_eng, step)

            def scalar(a):
                def high(m, t, u, it, q):
                    if q % 2 == 0:
                        a.wait_ge(*s_raw[m][q // 2](16 * (t + 1)))
                    if q == 0:
                        if not isinstance(t, int) or t >= 2:
                            a.wait_ge(*s_hps(FPAIRS * (t - 1)))
                    a.copy(in_parts[m][u][0].rearrange("p c f -> p (c f)")[:, q * 512:(q + 1) * 512],
                           raw[m][:, q * 512:(q + 1) * 512]).then_inc(s_hi[m].sem, 1)

                def high2(t, u, it, q):
                    if q % 2 == 0:
                        a.wait_ge(*s_raw2[q // 2](16 * (t + 1)))
                    if q == 0:
                        if lead:
                            a.wait_ge(*s_mm2[u](it))
                        elif not isinstance(t, int) or t > 0:
                            a.wait_ge(*s_mm2[1 - u](it + u))
                    a.copy(out_parts[u * lead][0].rearrange("p c o -> p (c o)")[:, q * 512:(q + 1) * 512],
                           raw[2][:, q * 512:(q + 1) * 512]).then_inc(s_hi2.sem, 1)

                def high_x(t, u, it):
                    a.wait_ge(*s_xT_ps[u](it + 1))
                    a.copy(x_part[u][0], bank(6).rearrange("p (c s) -> p c s", c=DC)).then_inc(s_xhi.sem, 1)

                def activate(t, u, it, p):
                    a.wait_ge(*s_hps(FPAIRS * t + p + 1))
                    first = isinstance(t, int) and t == 0 and p < 2
                    if kind == "swiglu":
                        if not first:
                            a.wait_ge(*s_gated(FPAIRS * t + p - 1))
                        a.activation(h_gate[:, p % 2, :], bank(p % 2), ACT.Silu).then_inc(s_act.sem, 1)
                        return
                    if not first:
                        a.wait_ge(*s_hsplit(FPAIRS * t + p - 1))
                    if kind == "gelu":
                        a.activation(h_raw[:, p % 2, :], bank(p), ACT.Gelu_apprx_tanh).then_inc(s_act.sem, 1)
                    else:
                        for q in range(2):
                            f = 2 * p + q
                            ins = a.activation(h_raw[:, p % 2, q * SLOTS:(q + 1) * SLOTS], bank(p)[:, q * SLOTS:(q + 1) * SLOTS],
                                               ACT.Relu, bias=b1_buf[:, u, f:f + 1])
                        ins.then_inc(s_act.sem, 1)

                def evict(t, u, it):
                    a.wait_ge(*s_mm2[u](it + 1))
                    a.wait_ge(*s_yfree[u](it))
                    a.copy(y_rows[:, u, :, :], bank(4 + u).rearrange("p (s d) -> p s d", s=SB)).then_inc(s_y[u].sem, 1)

                for t in range(2):
                    if t == 1 and lead:
                        for q in range(4):
                            high2(0, 0, 0, q)
                    for q in range(4):
                        for m in range(n_in):
                            high(m, t, t, 0, q)
                    if t == 1:
                        for p in range(FPAIRS):
                            activate(0, 0, 0, p)
                    high_x(t, t, 0)

                def step(t, u, it):
                    for q in range(4):
                        for q2 in quarters2[q]:
                            if exists(t + lead):
                                high2(t + lead, (1 - u) if lead else u, (it + u) if lead else it, q2)
                        if exists(t + 1):
                            activate(t + 1, 1 - u, it + u, q)
                        for q1 in quarters[q]:
                            if exists(t + 2):
                                for m in range(n_in):
                                    high(m, t + 2, u, it + 1, q1)
                        if q == 0 and not (isinstance(t, int) and t == 0):
                            evict(t - 1, 1 - u, it - 1 + u)
                    if exists(t + 2):
                        high_x(t + 2, u, it + 1)

                tiles(a, step)
                evict(NT - 1, (NT - 1) % 2, (NT - 1) // 2)

            def vector(v):
                def low(m, t, u, it, q):
                    v.wait_ge(*s_hi[m](4 * t + q + 1))
                    part = slice(q * 512, (q + 1) * 512)
                    hi, lo = (z.rearrange("p c f -> p (c f)")[:, part] for z in in_parts[m][u])
                    ins = v.tensor_tensor(lo, raw[m][:, part], hi.bitcast(FP32), ALU.subtract)
                    if q % 2 == 1:
                        ins.then_inc(s_split[m].sem, 1)

                def low2(t, u, it, q):
                    v.wait_ge(*s_hi2(4 * t + q + 1))
                    part = slice(q * 512, (q + 1) * 512)
                    hi, lo = (z.rearrange("p c o -> p (c o)")[:, part] for z in out_parts[u * lead])
                    ins = v.tensor_tensor(lo, raw[2][:, part], hi.bitcast(FP32), ALU.subtract)
                    if q % 2 == 1:
                        ins.then_inc(s_split2.sem, 1)

                def low_x(t, u, it):
                    v.wait_ge(*s_xhi(t + 1))
                    v.tensor_tensor(x_part[u][1], bank(6).rearrange("p (c s) -> p c s", c=DC),
                                    x_part[u][0].bitcast(FP32), ALU.subtract).then_inc(s_xsplit.sem, 1)

                def high_h(t, u, it, p):
                    if p == 0:
                        v.wait_ge(*s_mm2[u](it))
                    v.wait_ge(*s_act(FPAIRS * t + p + 1))
                    hi, lo = (h_part[u][z][:, 2 * p:2 * p + 2, :].rearrange("p c s -> p (c s)") for z in range(2))
                    if kind == "swiglu":
                        if not isinstance(t, int) or t > 0 or p >= 2:
                            v.wait_ge(*s_hsplit(FPAIRS * t + p - 1))
                        v.tensor_tensor(h_raw[:, p % 2, :], h_gate[:, p % 2, :], bank(2 + p % 2), ALU.mult)\
                            .then_inc(s_gated.sem, 1)
                        v.wait_ge(*s_gated(FPAIRS * t + p + 1))
                    v.tensor_copy(hi, h_raw[:, p % 2, :]).then_inc(s_hhi.sem, 1)

                def low_h(t, u, it, p):
                    hi, lo = (h_part[u][z][:, 2 * p:2 * p + 2, :].rearrange("p c s -> p (c s)") for z in range(2))
                    v.wait_ge(*s_hhi(FPAIRS * t + p + 1))
                    v.tensor_tensor(lo, h_raw[:, p % 2, :], hi.bitcast(FP32), ALU.subtract).then_inc(s_hsplit.sem, 1)

                for t in range(2):
                    if t == 1 and lead:
                        for q in range(4):
                            low2(0, 0, 0, q)
                    for q in range(4):
                        for m in range(n_in):
                            low(m, t, t, 0, q)
                    if t == 1:
                        for p in range(FPAIRS):
                            high_h(0, 0, 0, p)
                            low_h(0, 0, 0, p)
                    low_x(t, t, 0)

                def step(t, u, it):
                    for q in range(4):
                        if not lead:
                            for q2 in quarters2[q]:
                                low2(t, u, it, q2)
                        if exists(t + 1):
                            high_h(t + 1, 1 - u, it + u, q)
                        if lead and exists(t + 1):
                            for q2 in quarters2[q]:
                                low2(t + 1, 1 - u, it + u, q2)
                        if exists(t + 1):
                            low_h(t + 1, 1 - u, it + u, q)
                        for q1 in quarters[q]:
                            if exists(t + 2):
                                for m in range(n_in):
                                    low(m, t + 2, u, it + 1, q1)
                    if exists(t + 2):
                        low_x(t + 2, u, it + 1)

                tiles(v, step)

            return (Stage(sync, gpsimd, scalar, vector, tensor),
                    [s_stored[u](16 * SB * half[u]) for u in range(2)])

        ROWS = 4
        RING = 16 // ROWS

        def combine():
            s_back = [signal(f"moe_outputs_back{k}", 16 * 2 * (UNITS // RING)) for k in range(RING)]
            s_comb = signal("moe_combined", ROWS * UNITS)

            def load(sp, u):
                if u >= RING:
                    sp.wait_ge(*s_comb(ROWS * (u - RING + 1)))
                for c in range(2):
                    at = 1 + c * T + u * UNIT
                    sp.dma_start(y_back[:, ROWS * (u % RING) + 2 * c:ROWS * (u % RING) + 2 * c + 2, :],
                                 ys[at:at + UNIT, :].rearrange("(t p) d -> p t d", p=P)).then_inc(s_back[u % RING].sem, 16)

            def add(v, u):
                v.wait_ge(*s_back[u % RING](16 * 2 * (u // RING + 1)))
                for c in range(2):
                    if c == 1:
                        v.wait_ge(*s_comb(ROWS * u + 2))
                    for t in range(2):
                        v.scalar_tensor_tensor(x[:, 2 * u + t, :], y_back[:, ROWS * (u % RING) + 2 * c + t, :],
                                               best[:, c, 2 * u + t:2 * u + t + 1], x[:, 2 * u + t, :],
                                               ALU.mult, ALU.add).then_inc(s_comb.sem, 1)

            return load, add, s_comb

        def combine_and_store(before):
            load, add, s_comb = combine()
            s_out = signal("output", 16 * B)

            def sync(sp):
                def store(i):
                    sp.wait_ge(*s_comb(ROWS * UNITS // B * (i + 1)))
                    sp.dma_start(out.rearrange("b (t p) d -> p (b t) d", p=P)[:, TPB * i:TPB * (i + 1), :],
                                 x[:, TPB * i:TPB * (i + 1), :]).then_inc(s_out.sem, 16)

                wait_all(sp, before)
                for u in range(UNITS):
                    load(sp, u)
                    if u == RING + 1:
                        store(0)
                for i in range(1, B):
                    store(i)
                sp.wait_ge(*s_out(16 * B))

            def vector(v):
                for u in range(UNITS):
                    add(v, u)

            return Stage(sync, nothing, nothing, vector, nothing), [s_comb(ROWS * UNITS)]

        def dense_experts(routed_w, shared_w, routed, x_before):
            n_w = E_ALL * DC * HID
            raw_w = [view(256 + k * n_w, n_w) for k in (0, 1, 0)]
            silu = view(7936, 2, SEQ)
            xnb = view(9216, TPB, D)
            h_mid = view(10240, 2, SEQ)
            part = [[w_parts[:, (2 * k + z) * n_w:(2 * k + z + 1) * n_w] for z in range(2)] for k in range(3)]
            w1p, w3p = ([z.rearrange("p (e c h) -> p e c h", e=E_ALL, c=DC) for z in part[k]] for k in range(2))
            w2p = [z.rearrange("p (e o) -> p e o", e=E_ALL) for z in part[2]]
            xp = [xT_parts[:, z * 1024:(z + 1) * 1024].rearrange("p (c s) -> p c s", c=DC) for z in range(2)]
            hp = [[h_parts[:, (2 * u + z) * SEQ:(2 * u + z + 1) * SEQ] for z in range(2)] for u in range(2)]
            N = B * E_ALL
            s_raw, s_raw_w2, s_high, s_low = signal("dense_weights", 16 * 4), signal("dense_weights_w2", 16 * 2), signal("dense_w_high", 3), signal("dense_w_split", 3)
            s_blk, s_xT_ps, s_xhi, s_xlo = (signal("dense_block", B), signal("dense_xT_in_psum", B),
                                            signal("dense_x_high", 2 * B), signal("dense_x_split", 2 * B))
            s_hps, s_act, s_mid, s_hhi, s_hlo = (signal(f"dense_{k}", N) for k in
                                                 ("h_in_psum", "silu", "gated", "h_high", "h_split"))
            s_y, s_add = signal("dense_y", N), signal("dense_added", N * TPB)

            def sync(sp):
                wait_all(sp, x_before)
                for k, (name, of) in enumerate(zip(("w1", "w3", "w2"), (P, P, HID))):
                    form = "e (c p) h -> p (e c) h" if k < 2 else "e p o -> p e o"
                    kw = {"p": P} if k < 2 else {}
                    last = HID if k < 2 else D
                    if k == 2:
                        sp.wait_ge(*s_low(1))
                    dst = raw_w[k].rearrange("p (n h) -> p n h", h=last)
                    cut = E * DC if k < 2 else E
                    sp.dma_start(dst[:, 0:cut, :], routed_w[k].rearrange(form, **kw)).then_inc((s_raw if k < 2 else s_raw_w2).sem, 16)
                    sp.dma_start(dst[:, cut:, :], shared_w[k].rearrange(form, **kw)).then_inc((s_raw if k < 2 else s_raw_w2).sem, 16)

            def gpsimd(g):
                pass

            def tensor(t):
                def product(o, a, b, first, last):
                    t.matmul(o, a[0], b[0], start=first, stop=False)
                    t.matmul(o, a[0], b[1], start=False, stop=False)
                    return t.matmul(o, a[1], b[0], start=False, stop=last)

                with t.Fori(0, B) as i:
                    t.wait_ge(*s_blk(i + 1))
                    t.wait_ge(*s_add(i * (E_ALL * TPB)))
                    for j in range(TPB):
                        for c in range(DC):
                            ins = t.transpose(bank(6 + c)[:, j * P:(j + 1) * P], xnb[:, j, c * P:(c + 1) * P], ident[:, :])
                    ins.then_inc(s_xT_ps.sem, 1)
                    t.wait_ge(*s_xlo(2 * i + 2))
                    t.wait_ge(*s_low(2))

                    def hidden(e):
                        if e >= 2:
                            t.wait_ge(*s_mid(i * E_ALL + e - 1))
                        for m, w in enumerate((w1p, w3p)):
                            for c in range(DC):
                                ins = product(bank(2 * (e % 2) + m), [z[:, e, c, :] for z in w],
                                              [z[:, c, :] for z in xp], c == 0, c == DC - 1)
                        ins.then_inc(s_hps.sem, 1)

                    hidden(0)
                    for e in range(E_ALL):
                        if e + 1 < E_ALL:
                            hidden(e + 1)
                        if e == 0:
                            t.wait_ge(*s_low(3))
                        t.wait_ge(*s_hlo(i * E_ALL + e + 1))
                        if e >= 2:
                            t.wait_ge(*s_add(TPB * (i * E_ALL + e - 1)))
                        for j in range(TPB):
                            o = bank(4 + 2 * (e % 2) + j // 2)[:, (j % 2) * D:(j % 2 + 1) * D]
                            ins = product(o, [z[:, j * P:(j + 1) * P] for z in hp[e % 2]], [z[:, e, :] for z in w2p], True, True)
                        ins.then_inc(s_y.sem, 1)

            def split_low(v, k):
                v.wait_ge(*s_high(k + 1))
                v.tensor_tensor(part[k][1], raw_w[k], part[k][0].bitcast(FP32), ALU.subtract).then_inc(s_low.sem, 1)

            def high_beside_router(a):
                for k in range(2):
                    a.wait_ge(*s_raw(16 * 4))
                    a.copy(part[k][0], raw_w[k]).then_inc(s_high.sem, 1)

            def low_beside_router(v):
                for k in range(2):
                    split_low(v, k)

            dense_weights_split["all"] = s_low(3)
            beside_router["scalar"], beside_router["vector"] = high_beside_router, low_beside_router

            def scalar(a):
                a.wait_ge(*s_raw_w2(16 * 2))
                a.copy(part[2][0], raw_w[2]).then_inc(s_high.sem, 1)
                with a.Fori(0, B) as i:
                    a.copy(xnb, xn[:, bass.ds(TPB * i, TPB), :]).then_inc(s_blk.sem, 1)
                    a.wait_ge(*s_xT_ps(i + 1))
                    for c in range(DC):
                        a.copy(xp[0][:, c, :], bank(6 + c)).then_inc(s_xhi.sem, 1)
                    for e in range(E_ALL):
                        a.wait_ge(*s_hps(i * E_ALL + e + 1))
                        if e >= 2:
                            a.wait_ge(*s_mid(i * E_ALL + e - 1))
                        a.activation(silu[:, e % 2, :], bank(2 * (e % 2)), ACT.Silu).then_inc(s_act.sem, 1)

            def vector(v):
                split_low(v, 2)
                with v.Fori(0, B) as i:
                    for c in range(DC):
                        v.wait_ge(*s_xhi(2 * i + c + 1))
                        v.tensor_tensor(xp[1][:, c, :], bank(6 + c), xp[0][:, c, :].bitcast(FP32),
                                        ALU.subtract).then_inc(s_xlo.sem, 1)

                    def middle(e):
                        n = i * E_ALL + e
                        v.wait_ge(*s_act(n + 1))
                        if e >= 2:
                            v.wait_ge(*s_hlo(n - 1))
                        v.tensor_tensor(h_mid[:, e % 2, :], silu[:, e % 2, :], bank(2 * (e % 2) + 1), ALU.mult)\
                            .then_inc(s_mid.sem, 1)
                        v.wait_ge(*s_mid(n + 1))
                        v.tensor_copy(hp[e % 2][0], h_mid[:, e % 2, :]).then_inc(s_hhi.sem, 1)
                        v.wait_ge(*s_hhi(n + 1))
                        v.tensor_tensor(hp[e % 2][1], h_mid[:, e % 2, :], hp[e % 2][0].bitcast(FP32), ALU.subtract)\
                            .then_inc(s_hlo.sem, 1)

                    def add(e):
                        n = i * E_ALL + e
                        v.wait_ge(*s_y(n + 1))
                        for j in range(TPB):
                            if e:
                                v.wait_ge(*s_add(TPB * (n - 1) + j + 1))
                            v.scalar_tensor_tensor(tile_of(i, j),
                                                   bank(4 + 2 * (e % 2) + j // 2)[:, (j % 2) * D:(j % 2 + 1) * D],
                                                   gates[:, bass.ds(TPB * i + j, 1), e], tile_of(i, j),
                                                   ALU.mult, ALU.add).then_inc(s_add.sem, 1)

                    middle(0)
                    for e in range(E_ALL):
                        if e + 1 < E_ALL:
                            middle(e + 1)
                        add(e)
                v.wait_ge(*s_add(N * TPB))

            return Stage(sync, gpsimd, scalar, vector, tensor), [s_add(N * TPB)]

        def local_attention(x_before):
            wa = view(0, DC, D)
            wc = view(512, 2 * DC, D)
            ctx_rows = view(1536, B, D, parts=KEYS)
            keep, masked, gauss = (view(2560 + k * 256, B, KEYS) for k in range(3))
            xnb, qT = view(3328, TPB, D), view(5376, DC, SEQ)
            wap = [w_parts[:, z * 512:(z + 1) * 512].rearrange("p (c o) -> p c o", c=DC) for z in range(2)]
            wcp = [w_parts[:, 1024 * (z + 1):1024 * (z + 2)].rearrange("p (c o) -> p c o", c=2 * DC) for z in range(2)]
            xnT = [[of[:, z * 1024:(z + 1) * 1024].rearrange("p (c s) -> p c s", c=DC) for z in range(2)]
                   for of in (xT_parts[:, :], h_parts[:, 2048:4096])]
            contextT = [h_parts[:, z * 1024:(z + 1) * 1024].rearrange("p (c s) -> p c s", c=DC) for z in range(2)]
            align = view(6400, TPB, KEYS)
            alignT = view(6656, SEQ, parts=KEYS)
            tanh = view(8192, 2, D)
            centre, begin, finish, length = (view(8960 + k * B, B) for k in range(4))
            top, total, inverse = (view(8992 + k * TPB, TPB) for k in range(3))

            s_w = signal("local_weights", 16 * 5)
            s_whi, s_wlo = signal("local_w_high", 2), signal("local_w_split", 2)
            s_xlo, s_clo = signal("local_x_split", 2 * B), signal("local_context_split", B)
            s_ch = signal("local_chain", 0)
            s_dist, s_gauss = signal("local_distance", 1), signal("local_gauss", 1)
            s_var, s_rstd, s_norm = signal("variance", B), signal("rstd", B), signal("local_normed", TILES)
            s_xT_ps, s_xT, s_q_ps, s_q = (signal(f"local_{k}", n * B) for k, n in
                                          (("xT_in_psum", 1), ("xT", 2), ("q_in_psum", 2), ("q", 2)))
            s_sc, s_less, s_exp, s_al = (signal(f"local_{k}", B) for k in ("scores", "shifted", "exp", "aligned"))
            s_aT_ps, s_aT, s_c_ps, s_c = (signal(f"local_{k}", B) for k in ("alignT_in_psum", "alignT", "context_in_psum", "context"))
            s_y, s_tanh, s_x = (signal(f"local_{k}", TILES) for k in ("y", "tanh", "x_updated"))

            Y_BANKS = (4, 5, 2, 3)

            def sync(sp):
                sp.wait_ge(*dense_weights_split["all"])
                sp.dma_start(wa, io["L2_xcond_W_a"].rearrange("(c p) k -> p c k", p=P)).then_inc(s_w.sem, 16)
                sp.dma_start(wc, io["L2_xcond_W_c"].rearrange("(c p) o -> p c o", p=P)).then_inc(s_w.sem, 16)
                sp.dma_start(ctx_rows, io["ctx_1024"].rearrange("b k d -> k b d")).then_inc(s_w.sem, 16)
                sp.dma_start(centre, io["condB_pt"].to_broadcast([P, B])).then_inc(s_w.sem, 16)
                sp.dma_start(lens[:, :], io["_lenS2"].to_broadcast([P, B])).then_inc(s_w.sem, 16)

            def gpsimd(g):
                for i in range(B):
                    norm_gpsimd(g, i, s_var, s_rstd)

            def tensor(t):
                t.wait_ge(*s_w(16 * 5))
                t.wait_ge(*s_wlo(2))

                def transposes(i):
                    t.wait_ge(*s_xlo(2 * i))
                    for j in range(TPB):
                        t.wait_ge(*s_norm(TPB * i + j + 1))
                        for c in range(DC):
                            ins = t.transpose(bank(c)[:, j * P:(j + 1) * P], xnb[:, j, c * P:(c + 1) * P], ident[:, :])
                    ins.then_inc(s_xT_ps.sem, 1)

                def queries(i):
                    t.wait_ge(*s_xlo(2 * i + 2))
                    for oc in range(DC):
                        for kc in range(DC):
                            for za, zb in PASSES:
                                ins = t.matmul(bank(2 + oc), wap[za][:, kc, oc * P:(oc + 1) * P], xnT[i % 2][zb][:, kc, :],
                                               start=(kc == 0 and (za, zb) == (0, 0)),
                                               stop=(kc == DC - 1 and (za, zb) == (1, 0)))
                        ins.then_inc(s_q_ps.sem, 1)

                transposes(0)
                queries(0)
                for i in range(B):
                    if i + 1 < B:
                        transposes(i + 1)
                    t.wait_ge(*s_q(2 * i + 2))
                    t.wait_ge(*s_tanh(TPB * i))
                    for j in range(TPB):
                        for c in range(DC):
                            ins = t.matmul(bank(4)[:, j * KEYS:(j + 1) * KEYS], qT[:, c, j * P:(j + 1) * P],
                                           ctxT[:, c, i, 0, :], start=(c == 0), stop=(c == DC - 1))
                    ins.then_inc(s_sc.sem, 1)
                    if i + 1 < B:
                        queries(i + 1)
                    t.wait_ge(*s_al(i + 1))
                    t.transpose(bank(5)[:, 0:P], align[:, 0:2, :].rearrange("p j k -> p (j k)"), ident[:, :])
                    for j in range(1, TPB):
                        ins = t.transpose(bank(5)[0:KEYS, j * P:(j + 1) * P], align[:, j, :], ident[:, :])
                    ins.then_inc(s_aT_ps.sem, 1)
                    t.wait_ge(*s_aT(i + 1))
                    t.wait_ge(*s_clo(i))
                    for c in range(DC):
                        ins = t.matmul(bank(6 + c), ctx_rows[:, i, c * P:(c + 1) * P], alignT, start=True, stop=True)
                    ins.then_inc(s_c_ps.sem, 1)
                    t.wait_ge(*s_clo(i + 1))
                    t.wait_ge(*s_q(2 * min(i + 2, B)))
                    for j in range(TPB):
                        o = bank(Y_BANKS[j])[:, 0:D]
                        for c in range(2 * DC):
                            left = contextT if c < DC else xnT[i % 2]
                            for za, zb in PASSES:
                                ins = t.matmul(o, left[za][:, c % DC, j * P:(j + 1) * P], wcp[zb][:, c, :],
                                               start=(c == 0 and (za, zb) == (0, 0)),
                                               stop=(c == 2 * DC - 1 and (za, zb) == (1, 0)))
                        ins.then_inc(s_y.sem, 1)

            def scalar(a):
                a.wait_ge(*s_w(16 * 5))
                wait_all(a, x_before)
                a.copy(wap[0], wa).then_inc(s_whi.sem, 1)
                a.copy(wcp[0], wc).then_inc(s_whi.sem, 1)
                a.wait_ge(*s_dist(1))
                a.activation(gauss, gauss, ACT.Exp, scale=-1.0 / DEV_POW).then_inc(s_gauss.sem, 1)

                def tokens(i):
                    a.wait_ge(*s_xT_ps(i + 1))
                    if i >= 2:
                        a.wait_ge(*s_y(TPB * (i - 1)))
                    for c in range(DC):
                        a.copy(xnT[i % 2][0][:, c, :], bank(c)).then_inc(s_xT.sem, 1)

                def queries(i):
                    a.wait_ge(*s_sc(i))
                    for c in range(DC):
                        a.wait_ge(*s_q_ps(2 * i + c + 1))
                        a.copy(qT[:, c, :], bank(2 + c)).then_inc(s_q.sem, 1)

                tokens(0)
                queries(0)
                for i in range(B):
                    if i + 1 < B:
                        tokens(i + 1)
                    a.wait_ge(*s_less(i + 1))
                    a.activation(align, align, ACT.Exp).then_inc(s_exp.sem, 1)
                    if i + 1 < B:
                        queries(i + 1)
                    a.wait_ge(*s_aT_ps(i + 1))
                    a.copy(alignT, bank(5)[0:KEYS, :]).then_inc(s_aT.sem, 1)
                    a.wait_ge(*s_c_ps(i + 1))
                    a.wait_ge(*s_y(TPB * i))
                    a.copy(contextT[0], bank(6, 2).rearrange("p (c s) -> p c s", c=DC)).then_inc(s_c.sem, 1)
                    for j in range(TPB):
                        m = TPB * i + j
                        a.wait_ge(*s_y(m + 1))
                        if m >= 2:
                            a.wait_ge(*s_x(m - 1))
                        a.activation(tanh[:, j % 2, :], bank(Y_BANKS[j])[:, 0:D], ACT.Tanh).then_inc(s_tanh.sem, 1)

            def vector(v):
                pre = ch = Chain(v, s_ch)

                def normalise(i):
                    v.wait_ge(*s_xT_ps(i))
                    norm_vector(v, ch, i, xnb, s_var, s_rstd, s_norm)

                normalise(0)
                v.wait_ge(*s_w(16 * 5))
                pre.link(v.tensor_copy(length, lens[:, :]))
                pre.add(v.tensor_scalar(begin, centre, -WINDOW, 0.0, ALU.add, ALU.max))
                pre.link(v.tensor_scalar(finish, centre, WINDOW, None, ALU.add))
                pre.link(v.tensor_tensor(finish, finish, length, ALU.min))
                for b in range(B):
                    pre.add(v.tensor_scalar(keep[:, b, :], key_no[:, :], begin[:, b:b + 1], None, ALU.is_ge))
                    pre.add(v.tensor_scalar(gauss[:, b, :], key_no[:, :], centre[:, b:b + 1], None, ALU.subtract))
                pre.wait()
                for b in range(B):
                    pre.add(v.scalar_tensor_tensor(keep[:, b, :], key_no[:, :], finish[:, b:b + 1], keep[:, b, :],
                                                   ALU.is_le, ALU.mult))
                pre.wait()
                pre.link(v.tensor_scalar(masked, keep, -1.0, 1e9, ALU.add, ALU.mult))
                v.tensor_tensor(gauss, gauss, gauss, ALU.mult).then_inc(s_dist.sem, 1)
                v.wait_ge(*s_gauss(1))
                for n, (w, parts_of) in enumerate(((wa, wap), (wc, wcp))):
                    v.wait_ge(*s_whi(n + 1))
                    v.tensor_tensor(parts_of[1], w, parts_of[0].bitcast(FP32), ALU.subtract).then_inc(s_wlo.sem, 1)

                def tokens_low(i):
                    for c in range(DC):
                        v.wait_ge(*s_xT(2 * i + c + 1))
                        v.tensor_tensor(xnT[i % 2][1][:, c, :], bank(c), xnT[i % 2][0][:, c, :].bitcast(FP32), ALU.subtract)\
                            .then_inc(s_xlo.sem, 1)

                def of_row(row):
                    return row.unsqueeze(2).to_broadcast([P, TPB, KEYS])

                tokens_low(0)
                normalise(1)
                for i in range(B):
                    if i + 1 < B:
                        tokens_low(i + 1)

                    def of_batch(table):
                        return table[:, i:i + 1, :].to_broadcast([P, TPB, KEYS])

                    v.wait_ge(*s_sc(i + 1))
                    v.wait_ge(*s_aT_ps(i))
                    ch.link(v.tensor_tensor(align, bank(4)[:, 0:TPB * KEYS].rearrange("p (j k) -> p j k", k=KEYS),
                                            of_batch(keep), ALU.mult))
                    ch.link(v.tensor_tensor(align, align, of_batch(masked), ALU.add))
                    ch.link(v.reduce_max(top, align, AX.X))
                    v.tensor_tensor(align, align, of_row(top), ALU.subtract).then_inc(s_less.sem, 1)
                    v.wait_ge(*s_exp(i + 1))
                    ch.link(v.reduce_sum(total, align, AX.X))
                    ch.link(v.reciprocal(inverse, total))
                    ch.link(v.tensor_tensor(align, align, of_row(inverse), ALU.mult))
                    v.tensor_tensor(align, align, of_batch(gauss), ALU.mult).then_inc(s_al.sem, 1)
                    if i + 2 < B:
                        normalise(i + 2)
                    v.wait_ge(*s_c(i + 1))
                    v.tensor_tensor(contextT[1], bank(6, 2).rearrange("p (c s) -> p c s", c=DC),
                                    contextT[0].bitcast(FP32), ALU.subtract).then_inc(s_clo.sem, 1)
                    for j in range(TPB):
                        v.wait_ge(*s_tanh(TPB * i + j + 1))
                        v.tensor_tensor(x[:, TPB * i + j, :], x[:, TPB * i + j, :], tanh[:, j % 2, :], ALU.add)\
                            .then_inc(s_x.sem, 1)
                v.wait_ge(*s_x(TILES))

            return Stage(sync, gpsimd, scalar, vector, tensor), [s_x(TILES)]

        b1_buf = view(9216, 2, FC)
        b2_buf = view(9232, 2, D, parts=1)
        lens = sb("lens", [P, B], I32)

        def layer_router(L):
            return {0: lambda: router(0, io["L0_ffn_gate_w"], None, x_done),
                    1: lambda: router(1, io["L1_ffn_router_w"], io["L1_ffn_router_b"], x_done),
                    2: lambda: router(2, io["L2_ffn_gate_w"], io["L2_ffn_gate_b"], x_done),
                    3: lambda: router(3, io["L3_ffn_router_gate"], None, x_done)}[L]

        def layer_experts(L):
            return {0: lambda: moe(0, "gelu", io["L0_ffn_w1"], io["L0_ffn_w2"], routed=x_done),
                    1: lambda: dense_experts([io[f"L1_ffn_routed_{k}"] for k in ("w1", "w3", "w2")],
                                             [io[f"L1_ffn_shared_{k}"] for k in ("w1", "w3", "w2")], x_done, x_attended),
                    2: lambda: moe(2, "relu", io["L2_ffn_W1"], io["L2_ffn_W2"], b1=io["L2_ffn_b1"],
                                   b2=io["L2_ffn_b2"], routed=x_done),
                    3: lambda: moe(3, "swiglu", io["L3_ffn_gate_w"], io["L3_ffn_down_w"], w3=io["L3_ffn_up_w"],
                                   routed=x_done)}[L]


        plan = [start]
        x_done = x_attended = x_before_stage = None
        for L in range((stages + 1) // 2):
            if L == 2:
                parts = [lambda: local_attention(x_done)]
            else:
                parts = [lambda: attention(L, x_done, s_x_in(16) if L == 0 else None, combine() if L else None)]
            if 2 * L + 1 < stages:
                parts += [layer_router(L), layer_experts(L)]
            for make in parts:
                x_attended, x_before_stage = x_before_stage, x_done
                stage, x_done = make()
                plan.append(stage)
        if stages in (2, 6, 8):
            plan.append(combine_and_store(x_done)[0])
        plan.insert(2, load_x)

        block = ctx.enter_context(nc.Block())

        @block.sync
        def _(sp):
            for stage in plan:
                stage.sync(sp)

        @block.gpsimd
        def _(g):
            for stage in plan:
                stage.gpsimd(g)

        @block.scalar
        def _(a):
            for stage in plan:
                stage.scalar(a)

        @block.vector
        def _(v):
            for stage in plan:
                stage.vector(v)

        @block.tensor
        def _(t):
            for stage in plan:
                stage.tensor(t)


_TRANSPOSED = [f"L{l}_xcond_W{k}" for l in (0, 1, 3) for k in "qkvo"] + ["L2_xcond_W_c", "L2_ffn_gate_w"]


def kernel(**inputs):
    import concourse.bacc as _bacc
    from concourse.bass_utils import run_bass_kernel_spmd as _run

    nc = _bacc.Bacc("TRN2", target_bir_lowering=False, num_devices=1)
    laid = {k: np.asarray(v) for k, v in inputs.items()}
    for k in _TRANSPOSED:
        laid[k] = laid[k].T
    laid["ctxT"] = laid["ctx_1024"].reshape(B * KEYS, D).T
    laid["condB_tau"] = laid["condB_tau"].reshape(1, B)
    laid["condB_pt"] = laid["condB_pt"].reshape(1, B)
    laid["_lenS2"] = laid["_lenS2"].reshape(1, B)
    laid["L2_ffn_b1"] = laid["L2_ffn_b1"].reshape(E, FC, P).transpose(0, 2, 1)
    arrays, io = {}, {}
    for name, a in laid.items():
        a = np.ascontiguousarray(a)
        arrays[f"in_{name}"] = a
        io[name] = nc.dram_tensor(f"in_{name}", a.shape, mybir.dt.from_np(a.dtype), kind="ExternalInput").ap()
    out = nc.dram_tensor("out_x", (B, SEQ, D), FP32, kind="ExternalOutput").ap()
    build(nc, io, out)
    r = _run(nc, [arrays], core_ids=[0])
    return r.results[0]["out_x"]
```
